# Optimizing a Trainium2 kernel written in Bass

```python
import numpy as np
import jax
import jax.numpy as jnp

def _softmax(x, axis=-1):
    return jax.nn.softmax(x, axis=axis)

def _gelu(x):
    return jax.nn.gelu(x, approximate=True)

def _silu(x):
    return jax.nn.silu(x)

def _sigmoid(x):
    return jax.nn.sigmoid(x)

def _layernorm(x, axis=-1, eps=1e-05):
    m = jnp.mean(x, axis=axis, keepdims=True)
    v = jnp.var(x, axis=axis, keepdims=True)
    return (x - m) / jnp.sqrt(v + eps)

def _scatter_add(tgt, idx, src, axis=0):
    return tgt.at[idx].add(src)

def _segment_sum(src, seg, n):
    return jax.ops.segment_sum(src, seg, n)
kernel_name = 'mk_conv_attn_hybrid_d4_conv_nchw512_r4_b63141'

def setup_inputs(seed: int=0):
    np.random.seed(seed)
    _w = jnp.asarray

    def _rec_inputs():
        import jax
        import jax.numpy as jnp
        _gk = jax.random.key(seed)
        x = 7.22e-05 + 1 * jax.random.normal(jax.random.fold_in(_gk, 1), (16, 128, 32, 32), jnp.float32)
        return x
    x = _rec_inputs()

    def _L0_conv_setup():
        import jax, jax.numpy as jnp
        import numpy as np
        GROUPS = 8
        EPS = 1e-05
        key = jax.random.key(seed)
        ks = jax.random.split(key, 7)
        B, C, H, W = (16, 128, 32, 32)
        x = jax.random.normal(ks[0], (B, C, H, W), dtype=jnp.float32)
        norm_w = jnp.ones((C,), jnp.float32)
        norm_b = jnp.zeros((C,), jnp.float32)
        qkv_w = jax.random.normal(ks[1], (3 * C, C), dtype=jnp.float32) * (1.0 / np.sqrt(C))
        qkv_b = jnp.zeros((3 * C,), jnp.float32)
        proj_w = jax.random.normal(ks[2], (C, C), dtype=jnp.float32) * (1.0 / np.sqrt(C))
        proj_b = jnp.zeros((C,), jnp.float32)
        num_heads = 8
        return {'x': x, 'norm_w': norm_w, 'norm_b': norm_b, 'qkv_w': qkv_w, 'qkv_b': qkv_b, 'proj_w': proj_w, 'proj_b': proj_b, 'num_heads': num_heads}
    _L0_conv_all = _L0_conv_setup()
    _L0_conv_in = {k: v for k, v in _L0_conv_all.items() if k in ('norm_w', 'norm_b', 'qkv_w', 'qkv_b', 'proj_w', 'proj_b')}
    del _L0_conv_all

    def _L1_conv_setup():
        import jax, jax.numpy as jnp
        import numpy as np
        DN = ('NCHW', 'OIHW', 'NCHW')

        def dwconv(x, w, b, pad, dil=(1, 1)):
            y = jax.lax.conv_general_dilated(x, w, window_strides=(1, 1), padding=[pad[0], pad[1]], rhs_dilation=dil, dimension_numbers=DN, feature_group_count=w.shape[0])
            return y + b[None, :, None, None]
        key = jax.random.key(seed)
        ks = jax.random.split(key, 18)
        dim, B, H, W = (128, 8, 16, 16)
        s = 0.1
        inp = {'x': jax.random.normal(ks[0], (B, dim, H, W), jnp.float32)}
        shapes = {'w0': (dim, 1, 5, 5), 'w0_1': (dim, 1, 1, 7), 'w0_2': (dim, 1, 7, 1), 'w1_1': (dim, 1, 1, 11), 'w1_2': (dim, 1, 11, 1), 'w2_1': (dim, 1, 1, 21), 'w2_2': (dim, 1, 21, 1), 'w3': (dim, dim, 1, 1)}
        i = 1
        for name, shp in shapes.items():
            fan_in = shp[1] * shp[2] * shp[3]
            inp[name] = jax.random.normal(ks[i], shp, jnp.float32) * (s / np.sqrt(fan_in))
            inp['b' + name[1:]] = jax.random.normal(ks[i + 1], (dim,), jnp.float32) * 0.01
            i += 2
        return inp
    _L1_conv_all = _L1_conv_setup()
    _L1_conv_in = {k: v for k, v in _L1_conv_all.items() if k in ('w0', 'b0', 'w0_1', 'b0_1', 'w0_2', 'b0_2', 'w1_1', 'b1_1', 'w1_2', 'b1_2', 'w2_1', 'b2_1', 'w2_2', 'b2_2', 'w3', 'b3')}
    del _L1_conv_all

    def _L2_attn_setup():
        import jax, jax.numpy as jnp
        import numpy as np
        N_HEADS = 8
        N_LANDMARKS = 16
        NEWTON_ITERS = 6

        def _iterative_inv(mat):
            L = mat.shape[-1]
            fro = jnp.sqrt(jnp.sum(mat * mat, axis=(-2, -1), keepdims=True))
            fro = jnp.maximum(fro, 1e-06)
            z = jnp.swapaxes(mat, -2, -1) / (fro * fro)
            for _ in range(NEWTON_ITERS):
                z = 2.0 * z - z @ mat @ z
            return z
        key = jax.random.key(seed)
        ks = jax.random.split(key, 5)
        B, N, C = (4, 2048, 128)
        s = 1.0 / np.sqrt(C)
        return {'x': jax.random.normal(ks[0], (B, N, C), jnp.float32), 'Wqkv': jax.random.normal(ks[1], (3 * C, C), jnp.float32) * s, 'bqkv': jax.random.normal(ks[2], (3 * C,), jnp.float32) * 0.01, 'Wproj': jax.random.normal(ks[3], (C, C), jnp.float32) * s, 'bproj': jax.random.normal(ks[4], (C,), jnp.float32) * 0.01}
    _L2_attn_all = _L2_attn_setup()
    _L2_attn_in = {k: v for k, v in _L2_attn_all.items() if k in ('Wqkv', 'bqkv', 'Wproj', 'bproj')}
    del _L2_attn_all

    def _L2_ffn_setup():
        import jax, jax.numpy as jnp
        import numpy as np
        B, L, D, H, E, K = (8, 2048, 128, 512, 8, 2)
        SCALE = 0.02
        key = jax.random.key(seed)
        ks = jax.random.split(key, 6)
        return {'x': jax.random.normal(ks[0], (B, L, D), dtype=jnp.float32), 'Wg': jax.random.normal(ks[1], (D, E), dtype=jnp.float32) * SCALE, 'W1': jax.random.normal(ks[2], (E, D, H), dtype=jnp.float32) * SCALE, 'b1': jax.random.normal(ks[3], (E, H), dtype=jnp.float32) * SCALE, 'W2': jax.random.normal(ks[4], (E, H, D), dtype=jnp.float32) * SCALE, 'b2': jax.random.normal(ks[5], (E, D), dtype=jnp.float32) * SCALE}
    _L2_ffn_all = _L2_ffn_setup()
    _L2_ffn_in = {k: v for k, v in _L2_ffn_all.items() if k in ('Wg', 'W1', 'b1', 'W2', 'b2')}
    del _L2_ffn_all

    def _L3_attn_setup():
        import jax, jax.numpy as jnp
        import numpy as np
        key = jax.random.key(seed)
        k1, k2 = jax.random.split(key)
        B, S, D = (8, 512, 128)
        x = jax.random.normal(k1, (B, S, D), dtype=jnp.float32)
        W = jax.random.normal(k2, (D, D), dtype=jnp.float32) * 0.05
        b = jnp.zeros((D,), dtype=jnp.float32)
        return {'x': x, 'W': W, 'b': b}
    _L3_attn_all = _L3_attn_setup()
    _L3_attn_in = {k: v for k, v in _L3_attn_all.items() if k in ('W', 'b')}
    del _L3_attn_all

    def _L3_ffn_setup():
        import jax, jax.numpy as jnp
        import numpy as np
        TOP_K = 6
        CAP_FACTOR = 2.0
        key = jax.random.key(seed)
        ks = jax.random.split(key, 9)
        B, S, D, F, E, SH = (4, 512, 128, 64, 16, 2)
        return {'x': jax.random.normal(ks[0], (B, S, D), jnp.float32), 'router_w': jax.random.normal(ks[1], (E, D), jnp.float32) * 0.02, 'bias': jnp.zeros((E,), jnp.float32), 'shared_w_gate': jax.random.normal(ks[2], (SH, F, D), jnp.float32) * 0.02, 'shared_w_up': jax.random.normal(ks[3], (SH, F, D), jnp.float32) * 0.02, 'shared_w_down': jax.random.normal(ks[4], (SH, D, F), jnp.float32) * 0.02, 'w_gate': jax.random.normal(ks[5], (E, F, D), jnp.float32) * 0.02, 'w_up': jax.random.normal(ks[6], (E, F, D), jnp.float32) * 0.02, 'w_down': jax.random.normal(ks[7], (E, D, F), jnp.float32) * 0.02}
    _L3_ffn_all = _L3_ffn_setup()
    _L3_ffn_in = {k: v for k, v in _L3_ffn_all.items() if k in ('router_w', 'bias', 'shared_w_gate', 'shared_w_up', 'shared_w_down', 'w_gate', 'w_up', 'w_down')}
    del _L3_ffn_all
    return {'x': x, 'L0_conv_norm_w': _L0_conv_in['norm_w'], 'L0_conv_norm_b': _L0_conv_in['norm_b'], 'L0_conv_qkv_w': _L0_conv_in['qkv_w'], 'L0_conv_qkv_b': _L0_conv_in['qkv_b'], 'L0_conv_proj_w': _L0_conv_in['proj_w'], 'L0_conv_proj_b': _L0_conv_in['proj_b'], 'L1_conv_w0': _L1_conv_in['w0'], 'L1_conv_b0': _L1_conv_in['b0'], 'L1_conv_w0_1': _L1_conv_in['w0_1'], 'L1_conv_b0_1': _L1_conv_in['b0_1'], 'L1_conv_w0_2': _L1_conv_in['w0_2'], 'L1_conv_b0_2': _L1_conv_in['b0_2'], 'L1_conv_w1_1': _L1_conv_in['w1_1'], 'L1_conv_b1_1': _L1_conv_in['b1_1'], 'L1_conv_w1_2': _L1_conv_in['w1_2'], 'L1_conv_b1_2': _L1_conv_in['b1_2'], 'L1_conv_w2_1': _L1_conv_in['w2_1'], 'L1_conv_b2_1': _L1_conv_in['b2_1'], 'L1_conv_w2_2': _L1_conv_in['w2_2'], 'L1_conv_b2_2': _L1_conv_in['b2_2'], 'L1_conv_w3': _L1_conv_in['w3'], 'L1_conv_b3': _L1_conv_in['b3'], 'L2_attn_Wqkv': _L2_attn_in['Wqkv'], 'L2_attn_bqkv': _L2_attn_in['bqkv'], 'L2_attn_Wproj': _L2_attn_in['Wproj'], 'L2_attn_bproj': _L2_attn_in['bproj'], 'L2_ffn_Wg': _L2_ffn_in['Wg'], 'L2_ffn_W1': _L2_ffn_in['W1'], 'L2_ffn_b1': _L2_ffn_in['b1'], 'L2_ffn_W2': _L2_ffn_in['W2'], 'L2_ffn_b2': _L2_ffn_in['b2'], 'L3_attn_W': _L3_attn_in['W'], 'L3_attn_b': _L3_attn_in['b'], 'L3_ffn_router_w': _L3_ffn_in['router_w'], 'L3_ffn_bias': _L3_ffn_in['bias'], 'L3_ffn_shared_w_gate': _L3_ffn_in['shared_w_gate'], 'L3_ffn_shared_w_up': _L3_ffn_in['shared_w_up'], 'L3_ffn_shared_w_down': _L3_ffn_in['shared_w_down'], 'L3_ffn_w_gate': _L3_ffn_in['w_gate'], 'L3_ffn_w_up': _L3_ffn_in['w_up'], 'L3_ffn_w_down': _L3_ffn_in['w_down']}

def reference(x, L0_conv_norm_w, L0_conv_norm_b, L0_conv_qkv_w, L0_conv_qkv_b, L0_conv_proj_w, L0_conv_proj_b, L1_conv_w0, L1_conv_b0, L1_conv_w0_1, L1_conv_b0_1, L1_conv_w0_2, L1_conv_b0_2, L1_conv_w1_1, L1_conv_b1_1, L1_conv_w1_2, L1_conv_b1_2, L1_conv_w2_1, L1_conv_b2_1, L1_conv_w2_2, L1_conv_b2_2, L1_conv_w3, L1_conv_b3, L2_attn_Wqkv, L2_attn_bqkv, L2_attn_Wproj, L2_attn_bproj, L2_ffn_Wg, L2_ffn_W1, L2_ffn_b1, L2_ffn_W2, L2_ffn_b2, L3_attn_W, L3_attn_b, L3_ffn_router_w, L3_ffn_bias, L3_ffn_shared_w_gate, L3_ffn_shared_w_up, L3_ffn_shared_w_down, L3_ffn_w_gate, L3_ffn_w_up, L3_ffn_w_down):
    import jax
    import jax.numpy as jnp

    def _L0_conv_ref(x, norm_w, norm_b, qkv_w, qkv_b, proj_w, proj_b, num_heads):
        import jax, jax.numpy as jnp
        import numpy as np
        GROUPS = 8
        EPS = 1e-05
        b, c, h, w = x.shape
        n = h * w
        x_in = x
        xg = x.reshape(b, GROUPS, c // GROUPS, n)
        mean = jnp.mean(xg, axis=(2, 3), keepdims=True)
        var = jnp.var(xg, axis=(2, 3), keepdims=True)
        xn = (xg - mean) * jax.lax.rsqrt(var + EPS)
        xn = xn.reshape(b, c, n) * norm_w[None, :, None] + norm_b[None, :, None]
        qkv = jnp.einsum('oc,bcn->bon', qkv_w, xn) + qkv_b[None, :, None]
        q, k, v = jnp.split(qkv, 3, axis=1)
        d = c // num_heads
        q = q.reshape(b, num_heads, d, n)
        k = k.reshape(b, num_heads, d, n)
        v = v.reshape(b, num_heads, d, n)
        scale = 1.0 / np.sqrt(d).astype(np.float32)
        attn = jnp.einsum('bhdn,bhdm->bhnm', q * scale, k * scale)
        attn = jax.nn.softmax(attn, axis=-1)
        out = jnp.einsum('bhnm,bhdm->bhdn', attn, v).reshape(b, c, n)
        out = jnp.einsum('oc,bcn->bon', proj_w, out) + proj_b[None, :, None]
        return out.reshape(b, c, h, w) + x_in

    def _L1_conv_ref(x, w0, b0, w0_1, b0_1, w0_2, b0_2, w1_1, b1_1, w1_2, b1_2, w2_1, b2_1, w2_2, b2_2, w3, b3):
        import jax, jax.numpy as jnp
        import numpy as np
        DN = ('NCHW', 'OIHW', 'NCHW')

        def dwconv(x, w, b, pad, dil=(1, 1)):
            y = jax.lax.conv_general_dilated(x, w, window_strides=(1, 1), padding=[pad[0], pad[1]], rhs_dilation=dil, dimension_numbers=DN, feature_group_count=w.shape[0])
            return y + b[None, :, None, None]
        u = x
        attn = dwconv(x, w0, b0, ((2, 2), (2, 2)))
        a0 = dwconv(attn, w0_1, b0_1, ((0, 0), (9, 9)), (3, 3))
        a0 = dwconv(a0, w0_2, b0_2, ((9, 9), (0, 0)), (3, 3))
        a1 = dwconv(attn, w1_1, b1_1, ((0, 0), (15, 15)), (3, 3))
        a1 = dwconv(a1, w1_2, b1_2, ((15, 15), (0, 0)), (3, 3))
        a2 = dwconv(attn, w2_1, b2_1, ((0, 0), (30, 30)), (3, 3))
        a2 = dwconv(a2, w2_2, b2_2, ((30, 30), (0, 0)), (3, 3))
        attn = attn + a0 + a1 + a2
        attn = jax.lax.conv_general_dilated(attn, w3, (1, 1), [(0, 0), (0, 0)], dimension_numbers=DN)
        attn = attn + b3[None, :, None, None]
        return attn * u

    def _L2_attn_ref(x, Wqkv, bqkv, Wproj, bproj):
        import jax, jax.numpy as jnp
        import numpy as np
        N_HEADS = 8
        N_LANDMARKS = 16
        NEWTON_ITERS = 6

        def _iterative_inv(mat):
            L = mat.shape[-1]
            fro = jnp.sqrt(jnp.sum(mat * mat, axis=(-2, -1), keepdims=True))
            fro = jnp.maximum(fro, 1e-06)
            z = jnp.swapaxes(mat, -2, -1) / (fro * fro)
            for _ in range(NEWTON_ITERS):
                z = 2.0 * z - z @ mat @ z
            return z
        B, N, C = x.shape
        H = N_HEADS
        hd = C // H
        scale = hd ** (-0.5)
        n_lm = N_LANDMARKS
        qkv = x @ Wqkv.T + bqkv
        qkv = qkv.reshape(B, N, 3, H, hd).transpose(2, 0, 3, 1, 4)
        q, k, v = (qkv[0], qkv[1], qkv[2])
        if N <= n_lm:
            attn = jax.nn.softmax(q @ jnp.swapaxes(k, -2, -1) * scale, axis=-1)
            out = attn @ v
        else:
            stride = max(N // n_lm, 1)
            lm_idx = jnp.arange(0, N, stride)[:n_lm]
            q_lm = q[:, :, lm_idx]
            k_lm = k[:, :, lm_idx]
            kernel_1 = jax.nn.softmax(q @ jnp.swapaxes(k_lm, -2, -1) * scale, axis=-1)
            kernel_2 = jax.nn.softmax(q_lm @ jnp.swapaxes(k_lm, -2, -1) * scale, axis=-1)
            kernel_3 = jax.nn.softmax(q_lm @ jnp.swapaxes(k, -2, -1) * scale, axis=-1)
            kernel_2_inv = _iterative_inv(kernel_2)
            out = kernel_1 @ (kernel_2_inv @ (kernel_3 @ v))
        out = jnp.swapaxes(out, 1, 2).reshape(B, N, C)
        return out @ Wproj.T + bproj

    def _L2_ffn_ref(x, Wg, W1, b1, W2, b2):
        import jax, jax.numpy as jnp
        import numpy as np
        B, L, D, H, E, K = (8, 2048, 128, 512, 8, 2)
        SCALE = 0.02
        b, l, d = x.shape
        xt = x.reshape(-1, d)
        T = xt.shape[0]
        gate = jax.nn.softmax(xt @ Wg, axis=-1)
        topv, topi = jax.lax.top_k(gate, K)
        topv = topv / (jnp.sum(topv, axis=-1, keepdims=True) + 1e-06)
        scores = jnp.zeros((T, E), dtype=xt.dtype).at[jnp.arange(T)[:, None], topi].set(topv)
        out = jnp.zeros_like(xt)
        for e in range(E):
            h = jax.nn.gelu(xt @ W1[e] + b1[e], approximate=False)
            ye = h @ W2[e] + b2[e]
            out = out + ye * scores[:, e:e + 1]
        return out.reshape(b, l, d)

    def _L3_attn_ref(x, W, b):
        import jax, jax.numpy as jnp
        import numpy as np
        Q = jnp.einsum('bsd,de->bse', x, W) + b
        scores = jnp.einsum('bsd,btd->bst', Q, Q)
        A = jax.nn.softmax(scores, axis=-1)
        return jnp.einsum('bst,btd->bsd', A, x)

    def _L3_ffn_ref(x, router_w, bias, shared_w_gate, shared_w_up, shared_w_down, w_gate, w_up, w_down):
        import jax, jax.numpy as jnp
        import numpy as np
        TOP_K = 6
        CAP_FACTOR = 2.0
        B, S, D = x.shape
        E = router_w.shape[0]
        K = TOP_K
        N = B * S
        C = max(1, int(N * K * CAP_FACTOR / E))
        router_logits = jnp.einsum('bsd,ed->bse', x, router_w) + bias
        hg = jnp.einsum('bsd,efd->bsef', x, shared_w_gate)
        hu = jnp.einsum('bsd,efd->bsef', x, shared_w_up)
        shared_out = jnp.einsum('bsef,edf->bsd', jax.nn.silu(hg) * hu, shared_w_down)
        shared_out = shared_out / shared_w_gate.shape[0]
        router_probs = jax.nn.softmax(router_logits, axis=-1)
        topk_p, topk_i = jax.lax.top_k(router_probs, K)
        topk_p = topk_p / (jnp.sum(topk_p, axis=-1, keepdims=True) + 1e-09)
        x_flat = x.reshape(N, D)
        flat_e = topk_i.reshape(-1)
        flat_g = topk_p.reshape(-1)
        token_ids = jnp.repeat(jnp.arange(N), K)
        order = jnp.argsort(flat_e)
        se = flat_e[order]
        st = token_ids[order]
        sg = flat_g[order]
        M = se.shape[0]
        pos = jnp.arange(M)
        is_first = jnp.concatenate([jnp.ones((1,), bool), se[1:] != se[:-1]])
        group_starts = jax.lax.cummax(pos * is_first.astype(pos.dtype))
        slot = pos - group_starts
        valid = slot < C
        safe_slot = jnp.where(valid, slot, C)
        expert_in = jnp.zeros((E, C + 1, D), x.dtype).at[se, safe_slot].set(x_flat[st])
        expert_gate = jnp.zeros((E, C + 1), x.dtype).at[se, safe_slot].set(sg)
        expert_tok = jnp.full((E, C + 1), N, jnp.int32).at[se, safe_slot].set(st.astype(jnp.int32))
        expert_mask = jnp.zeros((E, C + 1), bool).at[se, safe_slot].set(valid)
        expert_in = expert_in[:, :C]
        expert_gate = expert_gate[:, :C]
        expert_tok = expert_tok[:, :C]
        expert_mask = expert_mask[:, :C]
        hg = jnp.einsum('ecd,efd->ecf', expert_in, w_gate)
        hu = jnp.einsum('ecd,efd->ecf', expert_in, w_up)
        expert_out = jnp.einsum('ecf,edf->ecd', jax.nn.silu(hg) * hu, w_down)
        fm = expert_mask.reshape(-1)
        dst = jnp.where(fm, expert_tok.reshape(-1), N)
        fg = jnp.where(fm, expert_gate.reshape(-1), jnp.zeros((), x.dtype))
        sparse = jax.ops.segment_sum(fg[:, None] * expert_out.reshape(-1, D), dst, num_segments=N + 1)[:N]
        return shared_out + sparse.reshape(B, S, D)

    def _gn(v, G=32, eps=1e-05):
        B_, C_, H_, W_ = v.shape
        g = v.reshape(B_, G, C_ // G, H_, W_)
        m = jnp.mean(g, axis=(2, 3, 4), keepdims=True)
        s = jnp.var(g, axis=(2, 3, 4), keepdims=True)
        return ((g - m) / jnp.sqrt(s + eps)).reshape(v.shape)

    def _ln_c(v, eps=1e-06):
        m = jnp.mean(v, axis=1, keepdims=True)
        s = jnp.var(v, axis=1, keepdims=True)
        return (v - m) / jnp.sqrt(s + eps)

    def _ln_t(v, eps=1e-05):
        m = jnp.mean(v, axis=-1, keepdims=True)
        s = jnp.var(v, axis=-1, keepdims=True)
        return (v - m) / jnp.sqrt(s + eps)

    def _to_tokens(v):
        B_, C_, H_, W_ = v.shape
        return v.reshape(B_, C_, H_ * W_).transpose(0, 2, 1)

    def _from_tokens(t, like):
        B_, C_, H_, W_ = like.shape
        return t.transpose(0, 2, 1).reshape(B_, C_, H_, W_)
    x = _L0_conv_ref(x, L0_conv_norm_w, L0_conv_norm_b, L0_conv_qkv_w, L0_conv_qkv_b, L0_conv_proj_w, L0_conv_proj_b, 8)
    x = x + _L1_conv_ref(_gn(x), L1_conv_w0, L1_conv_b0, L1_conv_w0_1, L1_conv_b0_1, L1_conv_w0_2, L1_conv_b0_2, L1_conv_w1_1, L1_conv_b1_1, L1_conv_w1_2, L1_conv_b1_2, L1_conv_w2_1, L1_conv_b2_1, L1_conv_w2_2, L1_conv_b2_2, L1_conv_w3, L1_conv_b3)
    t = _to_tokens(x)
    t = t + _L2_attn_ref(_ln_t(t), L2_attn_Wqkv, L2_attn_bqkv, L2_attn_Wproj, L2_attn_bproj)
    t = t + _L2_ffn_ref(_ln_t(t), L2_ffn_Wg, L2_ffn_W1, L2_ffn_b1, L2_ffn_W2, L2_ffn_b2)
    t = t + _L3_attn_ref(_ln_t(t), L3_attn_W, L3_attn_b)
    t = t + _L3_ffn_ref(_ln_t(t), L3_ffn_router_w, L3_ffn_bias, L3_ffn_shared_w_gate, L3_ffn_shared_w_up, L3_ffn_shared_w_down, L3_ffn_w_gate, L3_ffn_w_up, L3_ffn_w_down)
    x = _from_tokens(t, x)
    return x

_drawn_inputs = setup_inputs


def setup_inputs(seed=0):
    import zlib

    import numpy as np

    out = dict(_drawn_inputs(seed))
    spreads = {'L0_conv_norm_w': (1.0, 0.6),
     'L0_conv_norm_b': (0.0, 0.1),
     'L0_conv_qkv_b': (0.0, 0.1),
     'L0_conv_proj_b': (0.0, 0.1),
     'L3_attn_b': (0.0, 0.8),
     'L3_ffn_bias': (0.0, 0.8)}
    factors = {'L1_conv_w0': 5.514,
     'L1_conv_b0': 8.0,
     'L1_conv_w0_1': 8.0,
     'L1_conv_b0_1': 8.0,
     'L1_conv_w0_2': 8.0,
     'L1_conv_b0_2': 8.0,
     'L1_conv_w1_1': 8.0,
     'L1_conv_b1_1': 8.0,
     'L1_conv_w1_2': 8.0,
     'L1_conv_b1_2': 8.0,
     'L1_conv_w2_1': 8.0,
     'L1_conv_b2_1': 8.0,
     'L1_conv_w2_2': 8.0,
     'L1_conv_b2_2': 8.0,
     'L1_conv_w3': 5.415,
     'L1_conv_b3': 5.223,
     'L2_attn_bqkv': 4.939,
     'L2_attn_bproj': 5.361,
     'L2_ffn_b1': 8.0,
     'L2_ffn_b2': 4.032,
     'L3_attn_W': 8.0,
     'L3_ffn_router_w': 8.0,
     'L3_ffn_shared_w_gate': 8.0,
     'L3_ffn_shared_w_up': 8.0,
     'L3_ffn_shared_w_down': 8.0,
     'L3_ffn_w_gate': 8.0,
     'L3_ffn_w_up': 8.0,
     'L3_ffn_w_down': 8.0}
    for name, (base, spread) in spreads.items():
        noise = np.random.default_rng([zlib.crc32(name.encode()), seed]).standard_normal(out[name].shape)
        drawn = base * np.exp(spread * noise) if base else spread * noise
        out[name] = jnp.asarray(drawn.astype(out[name].dtype))
    for name, factor in factors.items():
        out[name] = (out[name] * factor).astype(out[name].dtype)
    return out
```

```python
import concourse.bass as bass
from concourse import mybir
from concourse.alu_op_type import AluOpType as ALU
from contextlib import ExitStack
import numpy as np

F32 = mybir.dt.float32
BF16 = mybir.dt.bfloat16
I32 = mybir.dt.int32
ACT = mybir.ActivationFunctionType
AX = mybir.AxisListType

C = 128
HW = 32
N = HW * HW
NT = N // 128
HALVES = N // 512
HEADS = 8
D = C // HEADS
CQ = 4


def shape_constants():
    p = np.arange(128)
    f = np.float32
    m = {}
    m["ident"] = np.eye(128, dtype=f)
    m["block16"] = (p[:, None] // 16 == p[None, :] // 16).astype(f)
    m["block4"] = (p[:, None] // 4 == p[None, :] // 4).astype(f)
    m["sumsel"] = ((p[:, None] % 32 == 16) & (p[:, None] // 32 == p[None, :] // 32)).astype(f)
    m["before"] = (p[:, None] < p[None, :]).astype(f)
    m["ones"] = np.ones((128, 128), f)
    m["pairsel"] = np.stack([(np.arange(16)[:, None] == 2 * q + (p[None, :] // 64)) for q in range(8)], 1).astype(f).reshape(16, 1024)
    for e in (8, 16):
        r = np.arange(e)
        m[f"tie{e}"] = np.broadcast_to((r[None, :] < r[:, None]).astype(f).reshape(1, e * e), (128, e * e)).copy()
    return m


def rsqrt(dve, y, v, t):
    dve.tensor_scalar(y.bitcast(I32), v.bitcast(I32), -0.5, 1597463007.0, ALU.mult, ALU.add)
    for _ in range(4):
        dve.drain()
        dve.tensor_tensor(t, y, y, ALU.mult)
        dve.drain()
        dve.tensor_tensor(t, t, v, ALU.mult)
        dve.drain()
        dve.tensor_scalar(t, t, -0.5, 1.5, ALU.mult, ALU.add)
        dve.drain()
        last = dve.tensor_tensor(y, y, t, ALU.mult)
    dve.drain()
    return last


def channel_moments(dve, moments, stats, mv, x):
    for k in range(HALVES):
        dve.bn_stats(stats[:, k, :], x[:, 512 * k:512 * k + 512])
    dve.drain()
    dve.bn_aggr(mv[:, :], stats[:, :, :])
    dve.drain()
    dve.tensor_copy(moments[:, 0:1], mv[:, 0:1])
    return dve.scalar_tensor_tensor(moments[:, 1:2], mv[:, 0:1], mv[:, 0:1], mv[:, 1:2], ALU.mult, ALU.add)


def group_affine(dve, scale, shift, group, sums, width, small, eps):
    dve.tensor_scalar(group[:, :], sums, 1.0 / width, None, ALU.mult)
    dve.drain()
    dve.tensor_tensor(small[:, 0:1], group[:, 0:1], group[:, 0:1], ALU.mult)
    dve.drain()
    dve.tensor_tensor(small[:, 1:2], group[:, 1:2], small[:, 0:1], ALU.subtract)
    dve.drain()
    dve.tensor_scalar(small[:, 1:2], small[:, 1:2], 0.0, eps, ALU.max, ALU.add)
    dve.drain()
    rsqrt(dve, scale, small[:, 1:2], small[:, 2:3])
    dve.scalar_tensor_tensor(shift, group[:, 0:1], -1.0, scale, ALU.mult, ALU.mult)
    dve.drain()


def attention_phase(nc, ctx, B, io, const, u_cols, gn2, x1_dram, split_dram):
    with ExitStack() as st:
        def sb(name, shape, dt=F32):
            return st.enter_context(nc.sbuf_tensor("a_" + name, shape, dt))

        def sem(name):
            return ctx.enter_context(nc.semaphore("a_" + name))

        SLOTS = ((0, 0), (0, 1), (1, 0), (1, 1), (0, 2), (2, 0))
        KS = len(SLOTS) * D
        PIECES = 3
        x = sb("x", [128, N])
        xn = sb("xn", [128, N])
        full, rest = sb("full", [128, N]), sb("rest", [128, N])
        pieces = sb("pieces", [128, 2, PIECES, N], BF16)
        q_stack = sb("q_stack", [KS + PIECES, HEADS, N], BF16)
        k_stack = sb("k_stack", [KS + PIECES, HEADS, N], BF16)
        v_ones = sb("v_ones", [128, NT, HEADS, 32])
        probs = sb("probs", [128, 3, N])
        o_sums = sb("o_sums", [128, 2, N])
        o_inv = sb("o_inv", [128, 512])
        x1 = sb("x1", [128, N])
        u_tr = sb("u_tr", [128, 32, HW])
        wqkv = sb("wqkv", [128, 3 * C])
        wproj = sb("wproj", [128, 2, C])
        vbias = sb("vbias", [128, C])
        qbias, kbias, pbias = sb("qbias", [128, 1]), sb("kbias", [128, 1]), sb("pbias", [128, 1])
        nw, nb = sb("nw", [128, 1]), sb("nb", [128, 1])
        stats, mv = sb("stats", [128, HALVES, 6]), sb("mv", [128, 2])
        moments, group, small = sb("moments", [128, 2]), sb("group", [128, 2]), sb("small", [128, 4])
        gscale, gshift = sb("gscale", [128, 1]), sb("gshift", [128, 1])
        maxes = sb("maxes", [128, 2, NT, 2])
        negmax = sb("negmax", [128, 2, NT])
        shift32 = sb("shift32", [NT, 2, 128])
        shift3 = sb("shift3", [NT, 2, PIECES, 128], BF16)
        ps_a = st.enter_context(nc.psum_tensor("ps_a", [128, 2, 512], F32))
        ps_b = st.enter_context(nc.psum_tensor("ps_b", [128, 2, N], F32))
        ps_o = st.enter_context(nc.psum_tensor("ps_o", [128, N], F32))

        params_in, x_in, zeroed = sem("params_in"), sem("x_in"), sem("zeroed")
        moments_up, sums_up, xn_up = sem("moments_up"), sem("sums_up"), sem("xn_up")
        qk_ps, v_ps, split_up, v_up = sem("qk_ps"), sem("v_ps"), sem("split_up"), sem("v_up")
        split_stored, qk_stacked = [sem(f"split_stored{n}") for n in range(2)], sem("qk_stacked")
        shift_in = [sem(f"shift_in{n}") for n in range(2)]
        a_up, a_read, max_up, shift_up = sem("a_up"), sem("a_read"), sem("max_up"), sem("shift_up")
        b_up, b_exp, o_up, o_out = sem("b_up"), sem("b_exp"), sem("o_up"), sem("o_out")
        bc_up, on_up, proj_up, x1_up = sem("bc_up"), sem("on_up"), sem("proj_up"), sem("x1_up")
        moments2_up, sums2_up, ut_up = sem("moments2_up"), sem("sums2_up"), sem("ut_up")
        x1_stored, u_stored, x_free = sem("x1_stored"), sem("u_stored"), sem("x_free")

        ring = []
        for h in range(HEADS):
            ring += [("scores", h, g) for g in range(2)]
            if h:
                ring.append(("shift", h - 1, 0))
            ring += [("scores", h, g) for g in range(2, 2 * NT)]
        ring.append(("shift", HEADS - 1, 0))
        place = {item: n for n, item in enumerate(ring)}
        A_PER, B_PER = len(ring), HEADS * NT
        PARAMS = 16 * (7 + HEADS)
        SHIFTS = 16 * PIECES * HEADS // 2
        block = st.enter_context(nc.Block())

        @block.sync
        def _(sp):
            sp.wait_ge(zeroed, 1)
            for dst, src in ((wqkv[:, :], io["L0_qkvT"]), (qbias[:, :], io["L0_conv_qkv_b"][0:C, :]),
                             (kbias[:, :], io["L0_conv_qkv_b"][C:2 * C, :]), (pbias[:, :], io["L0_conv_proj_b"]),
                             (nw[:, :], io["L0_conv_norm_w"]), (nb[:, :], io["L0_conv_norm_b"]),
                             (vbias[:, :], io["L0_conv_qkv_b"][2 * C:3 * C, :].rearrange("c b -> b c").broadcast_to((128, C)))):
                sp.dma_start(dst, src).then_inc(params_in, 16)
            for h in range(HEADS):
                sp.dma_start(wproj[32 * (h % 4):32 * (h % 4) + D, h // 4, :],
                             io["L0_projT"][D * h:D * h + D, :]).then_inc(params_in, 16)
            with sp.Fori(0, B) as i:
                sp.wait_ge(x_free, i + 1)
                sp.dma_start(x[:, :], io["x"][bass.ds(i, 1), :, :].rearrange("a c n -> (a c) n")).then_inc(x_in, 16)
                for qk in range(2):
                    sp.wait_ge(split_up, i * 2 + qk + 1)
                    sp.dma_start(split_dram[qk, :, :, :].rearrange("s c n -> c s n"), pieces[:, qk, :, :]).then_inc(split_stored[qk], 16)
                for qk, stack in enumerate((q_stack, k_stack)):
                    sp.wait_ge(split_stored[qk], i * 16 + 16)
                    for s, slot in enumerate(SLOTS):
                        sp.dma_start(stack[D * s:D * s + D, :, :],
                                     split_dram[qk, slot[qk], :, :].rearrange("(h d) n -> d h n", d=D)).then_inc(qk_stacked, 16)
                for h in range(HEADS):
                    sp.wait_ge(shift_up, i * HEADS + h + 1)
                    for s in range(PIECES):
                        sp.dma_start(q_stack[KS + s:KS + s + 1, h, :].rearrange("s (t n) -> s t n", t=NT),
                                     shift3[:, h % 2, s, :]).then_inc(shift_in[h % 2], 16)
                sp.wait_ge(ut_up, i + 1)
                sp.dma_start(x1_dram[bass.ds(i, 1), :, :].rearrange("a c n -> (a c) n"), x1[:, :]).then_inc(x1_stored, 16)
                sp.dma_start(u_cols[:, bass.ds(i, 1), :, :].rearrange("p a c h -> p (a c h)"),
                             u_tr[:, :, :].rearrange("p c h -> p (c h)")).then_inc(u_stored, 16)
            sp.wait_ge(x1_stored, 16 * B + 16)
            sp.wait_ge(u_stored, 16 * B + 16)

        @block.gpsimd
        def _(pool):
            pool.memset(wproj[:, :, :], 0.0)
            pool.drain()
            pool.memset(k_stack[KS:KS + PIECES, :, :], 1.0)
            pool.drain()
            pool.memset(v_ones[:, :, :, :], 1.0)
            pool.drain().then_inc(zeroed, 1)

        @block.vector
        def _(dve):
            dve.wait_ge(params_in, PARAMS)
            dve.sem_inc(x_free, 1)
            dve.sem_inc(x1_stored, 16)
            dve.sem_inc(u_stored, 16)
            with dve.Fori(0, B) as i:
                dve.wait_ge(x_in, i * 16 + 16)
                channel_moments(dve, moments, stats, mv, x).then_inc(moments_up, 1)
                dve.wait_ge(sums_up, i + 1)
                group_affine(dve, gscale[:, :], gshift[:, :], group, ps_a[:, 0, 0:2], C // 8, small, 1e-5)
                dve.tensor_tensor(gscale[:, :], gscale[:, :], nw[:, :], ALU.mult)
                dve.tensor_tensor(gshift[:, :], gshift[:, :], nw[:, :], ALU.mult)
                dve.drain()
                dve.tensor_tensor(gshift[:, :], gshift[:, :], nb[:, :], ALU.add)
                dve.drain()
                dve.tensor_scalar(xn[:, :], x[:, :], gscale[:, :], gshift[:, :], ALU.mult, ALU.add).then_inc(xn_up, 1)
                for qk, bias in enumerate((qbias, kbias)):
                    dve.drain()
                    dve.wait_ge(qk_ps, i * 2 + qk + 1)
                    dve.tensor_scalar(full[:, :], ps_b[:, qk, :], bias[:, :], 1.0 if qk else 1.0 / D, ALU.add, ALU.mult)
                    dve.drain()
                    for s in range(PIECES):
                        src = full if s == 0 else rest
                        dve.tensor_copy(pieces[:, qk, s, :], src[:, :])
                        dve.drain()
                        if s < PIECES - 1:
                            dve.tensor_tensor(rest[:, :], src[:, :], pieces[:, qk, s, :], ALU.subtract)
                            dve.drain()
                    dve.drain().then_inc(split_up, 1)
                dve.wait_ge(v_ps, i + 1)
                for t in range(NT):
                    last = dve.tensor_tensor(v_ones[:, t, :, 0:D],
                                             ps_o[:, 128 * t:128 * t + 128].rearrange("p (h d) -> p h d", h=HEADS),
                                             vbias[:, :].rearrange("p (h d) -> p h d", h=HEADS), ALU.add)
                last.then_inc(v_up, 1)

                def take_output(h):
                    dve.wait_ge(o_up, i * HEADS + h + 1)
                    r = 32 * (h % 4)
                    dve.tensor_copy(o_sums[r:r + 32, h // 4, :], ps_o[r:r + 32, :]).then_inc(o_out, 1)

                for n, (what, h, g) in enumerate(ring):
                    dve.wait_ge(a_up, i * A_PER + n + 1)
                    if what == "scores":
                        dve.reduce_max(maxes[:, h % 2, g // 2, g % 2:g % 2 + 1], ps_a[:, n % 2, :], axis=AX.X).then_inc(a_read, 1)
                        if g == 2 * NT - 1:
                            dve.drain()
                            dve.tensor_reduce(negmax[:, h % 2, :], maxes[:, h % 2, :, :], axis=AX.X, op=ALU.max,
                                              negate=True).then_inc(max_up, 1)
                        if g == NT and h >= 3:
                            take_output(h - 3)
                    else:
                        if h >= 2:
                            dve.wait_ge(shift_in[h % 2], i * SHIFTS + 16 * PIECES * (h // 2))
                        dve.tensor_copy(shift32[:, h % 2, :], ps_a[0:NT, n % 2, 0:128]).then_inc(a_read, 1)
                        dve.drain()
                        for s in range(PIECES):
                            dve.tensor_copy(shift3[:, h % 2, s, :], shift32[:, h % 2, :])
                            dve.drain()
                            if s < PIECES - 1:
                                dve.tensor_tensor(shift32[:, h % 2, :], shift32[:, h % 2, :], shift3[:, h % 2, s, :], ALU.subtract)
                                dve.drain()
                        dve.drain().then_inc(shift_up, 1)
                for h in range(HEADS - 3, HEADS):
                    take_output(h)
                for n in range(4):
                    g, k = n // 2, n % 2
                    dve.wait_ge(bc_up, i * 4 + n + 1)
                    dve.reciprocal(o_inv[:, :], ps_b[:, g, 512 * k:512 * k + 512])
                    dve.drain()
                    part = o_sums[:, g, 512 * k:512 * k + 512]
                    dve.tensor_tensor(part, part, o_inv[:, :], ALU.mult)
                    dve.drain()
                dve.drain().then_inc(on_up, 1)
                dve.wait_ge(proj_up, i + 1)
                dve.wait_ge(x1_stored, i * 16 + 16)
                dve.wait_ge(u_stored, i * 16 + 16)
                dve.scalar_tensor_tensor(x1[:, :], ps_o[:, :], pbias[:, :], x[:, :], ALU.add, ALU.add).then_inc(x_free, 1)
                dve.drain()
                channel_moments(dve, moments, stats, mv, x1).then_inc(moments2_up, 1)
                dve.wait_ge(sums2_up, i + 1)
                group_affine(dve, gscale[:, :], gshift[:, :], group, ps_a[:, 0, 0:2], C // 32, small, 1e-5)
                dve.tensor_copy(gn2[:, 0, bass.ds(i, 1)], gscale[:, :])
                dve.tensor_copy(gn2[:, 1, bass.ds(i, 1)], gshift[:, :])
                dve.tensor_scalar(xn[:, :], x1[:, :], gscale[:, :], gshift[:, :], ALU.mult, ALU.add)
                dve.drain()
                dve.transpose(u_tr[:, :, :].rearrange("p c h -> p h c"), xn[:, :]).then_inc(ut_up, 1)
                dve.drain()

        @block.scalar
        def _(act):
            with act.Fori(0, B) as i:
                for m in range(B_PER):
                    act.wait_ge(b_up, i * B_PER + m + 1)
                    act.activation(probs[:, m % 3, :], ps_b[:, m % 2, :], ACT.Exp).then_inc(b_exp, 1)

        @block.tensor
        def _(pe):
            pe.wait_ge(params_in, PARAMS)
            with pe.Fori(0, B) as i:
                pe.wait_ge(moments_up, i + 1)
                pe.matmul(ps_a[:, 0, 0:2], const["block16"], moments[:, :], start=True, stop=True).then_inc(sums_up, 1)
                pe.wait_ge(xn_up, i + 1)
                for qk in range(2):
                    for k in range(HALVES):
                        last = pe.matmul(ps_b[:, qk, 512 * k:512 * k + 512], wqkv[:, C * qk:C * qk + C],
                                         xn[:, 512 * k:512 * k + 512], start=True, stop=True)
                    last.then_inc(qk_ps, 1)
                for t in range(NT):
                    last = pe.matmul(ps_o[:, 128 * t:128 * t + 128], xn[:, 128 * t:128 * t + 128], wqkv[:, 2 * C:3 * C],
                                     start=True, stop=True)
                last.then_inc(v_ps, 1)
                pe.wait_ge(qk_stacked, i * 32 * len(SLOTS) + 32 * len(SLOTS))

                def ring_item(n):
                    what, h, g = ring[n]
                    if n >= 2:
                        pe.wait_ge(a_read, i * A_PER + n - 1)
                    if what == "scores":
                        t, k = g // 2, g % 2
                        pe.matmul(ps_a[:, n % 2, :], q_stack[0:KS, h, 128 * t:128 * t + 128],
                                  k_stack[0:KS, h, 512 * k:512 * k + 512], start=True, stop=True).then_inc(a_up, 1)
                    else:
                        pe.wait_ge(max_up, i * HEADS + h + 1)
                        pe.transpose(ps_a[0:NT, n % 2, 0:128], negmax[:, h % 2, :], const["ident"]).then_inc(a_up, 1)

                def shifted_scores(m):
                    h, t = divmod(m, NT)
                    if t == 0:
                        pe.wait_ge(shift_in[h % 2], i * SHIFTS + 16 * PIECES * (h // 2 + 1))
                    if m >= 2:
                        pe.wait_ge(b_exp, i * B_PER + m - 1)
                    for k in range(HALVES):
                        last = pe.matmul(ps_b[:, m % 2, 512 * k:512 * k + 512], k_stack[:, h, 128 * t:128 * t + 128],
                                         q_stack[:, h, 512 * k:512 * k + 512], start=True, stop=True)
                    last.then_inc(b_up, 1)

                def weigh_values(m):
                    h, t = divmod(m, NT)
                    r = 32 * (h % 4)
                    if m == 0:
                        pe.wait_ge(v_up, i + 1)
                    if t == 0 and h >= 4:
                        pe.wait_ge(o_out, i * HEADS + h - 3)
                    pe.wait_ge(b_exp, i * B_PER + m + 1)
                    for k in range(HALVES):
                        last = pe.matmul(ps_o[r:r + 32, 512 * k:512 * k + 512], v_ones[:, t, h, :],
                                         probs[:, m % 3, 512 * k:512 * k + 512], start=(t == 0), stop=(t == NT - 1))
                    if t == NT - 1:
                        last.then_inc(o_up, 1)

                n = 0
                for step in range(HEADS + 2):
                    for t in range(NT):
                        upto = place[("scores", step, 2 * t + 1)] + 1 if step < HEADS else len(ring)
                        while n < upto:
                            ring_item(n)
                            n += 1
                        if step >= 2:
                            m = (step - 2) * NT + t
                            shifted_scores(m)
                            if m >= 1:
                                weigh_values(m - 1)
                weigh_values(B_PER - 1)
                pe.wait_ge(o_out, i * HEADS + HEADS)
                for g in range(2):
                    for k in range(HALVES):
                        pe.matmul(ps_b[:, g, 512 * k:512 * k + 512], const["sumsel"], o_sums[:, g, 512 * k:512 * k + 512],
                                  start=True, stop=True).then_inc(bc_up, 1)
                pe.wait_ge(on_up, i + 1)
                for k in range(HALVES):
                    for g in range(2):
                        last = pe.matmul(ps_o[:, 512 * k:512 * k + 512], wproj[:, g, :], o_sums[:, g, 512 * k:512 * k + 512],
                                         start=(g == 0), stop=(g == 1))
                last.then_inc(proj_up, 1)
                pe.wait_ge(moments2_up, i + 1)
                pe.matmul(ps_a[:, 0, 0:2], const["block4"], moments[:, :], start=True, stop=True).then_inc(sums2_up, 1)


KERNELS = (("w0_1", "w0_2", 7), ("w1_1", "w1_2", 11), ("w2_1", "w2_2", 21))
ROWS5 = 5
BANDS = ROWS5 + 2 * len(KERNELS)
BAND = 2 * HW - 1


def setup_phase(nc, ctx, io, const, const_in, band_dram):
    with ExitStack() as st:
        def sb(name, shape, dt=F32):
            return st.enter_context(nc.sbuf_tensor("s_" + name, shape, dt))

        def sem(name):
            return ctx.enter_context(nc.semaphore("s_" + name))

        taps5 = sb("taps_square", [128, ROWS5, 5])
        taps = [sb(f"taps{n}", [128, k]) for n, k in enumerate(k for _, _, k in KERNELS for _ in range(2))]
        row = sb("row", [128, BANDS, BAND])
        rows = sb("rows", [128, 2, HW, BAND])
        consts_in, taps_in, rows_up = sem("consts_in"), sem("taps_in"), sem("rows_up")
        rows_stored = [sem(f"rows_stored{n}") for n in range(2)]
        block = st.enter_context(nc.Block())

        @block.sync
        def _(sp):
            sp.dma_start(taps5[:, :, :], io["L1_conv_w0"].rearrange("c (a b) -> c a b", a=ROWS5)).then_inc(taps_in, 16)
            names = [w for v, h, _ in KERNELS for w in (v, h)]
            for tap, name in zip(taps, names):
                sp.dma_start(tap[:, :], io["L1_conv_" + name]).then_inc(taps_in, 16)
            for dst, src in const_in:
                sp.dma_start(dst, src).then_inc(consts_in, 16)
            for k in range(BANDS):
                sp.wait_ge(rows_up, k + 1)
                sp.dma_start(band_dram[k, :, :], rows[:, k % 2, :, :].rearrange("c a b -> c (a b)")).then_inc(rows_stored[k % 2], 16)
            for n in range(2):
                sp.wait_ge(rows_stored[n], 16 * ((BANDS + 1 - n) // 2))
            sp.wait_ge(consts_in, 16 * len(const_in))

        @block.vector
        def _(dve):
            dve.memset(row[:, :, :], 0.0)
            dve.wait_ge(taps_in, 16 * (1 + len(taps)))
            dve.drain()
            dve.tensor_copy(row[:, 0:ROWS5, HW - 3:HW + 2], taps5[:, :, :])
            for n, tap in enumerate(taps):
                half = 3 * (KERNELS[n // 2][2] // 2)
                dve.tensor_copy(row[:, ROWS5 + n, HW - 1 - half:HW + half:3], tap[:, :])
            dve.drain()
            for k in range(BANDS):
                if k >= 2:
                    dve.wait_ge(rows_stored[k % 2], 16 * (k // 2))
                dve.tensor_copy(rows[:, k % 2, :, :], row[:, k, :].unsqueeze(1).broadcast_to((128, HW, BAND))).then_inc(rows_up, 1)


def conv_phase(nc, ctx, B, io, u_cols, maps, band_dram):
    with ExitStack() as st:
        def sb(name, shape, dt=F32):
            return st.enter_context(nc.sbuf_tensor("c_" + name, shape, dt))

        def sem(name):
            return ctx.enter_context(nc.semaphore("c_" + name))

        K = len(KERNELS)
        L = B * HW
        bands = [sb(f"bands{n}", [128, BANDS, 128]) for n in range(2)]
        square = [sb(f"square{n}", [128, L]) for n in range(2)]
        square_t = [sb(f"square_t{n}", [128, L]) for n in range(2)]
        along = [sb(f"along{n}", [128, K, L]) for n in range(2)]
        along_t = [sb(f"along_t{n}", [128, K, L]) for n in range(2)]
        bias = sb("bias", [128, 1 + 2 * K, 32])
        last_bias = sb("last_bias", [128, 32])
        ps_s = [st.enter_context(nc.psum_tensor(f"c_ps_s{n}", [128, 512], F32)) for n in range(2)]
        ps_h = [st.enter_context(nc.psum_tensor(f"c_ps_h{n}", [128, K, 512], F32)) for n in range(2)]
        zeroed, bias_in, bands_in = sem("zeroed"), sem("bias_in"), [sem(f"bands_in{n}") for n in range(2)]
        square_ps, square_up, square_turned = sem("square_ps"), sem("square_up"), sem("square_turned")
        along_ps, along_up, turned = sem("along_ps"), sem("along_up"), sem("turned")
        maps_ps, maps_up = sem("maps_ps"), sem("maps_up")
        block = st.enter_context(nc.Block())
        names = ["L1_conv_b0"] + ["L1_conv_b" + v[1:] for v, _, _ in KERNELS] + ["L1_conv_b" + h[1:] for _, h, _ in KERNELS]

        @block.gpsimd
        def _(pool):
            for n in range(2):
                pool.memset(bands[n][:, :, :], 0.0)
                pool.drain()
            pool.drain().then_inc(zeroed, 1)

        @block.sync
        def _(sp):
            for n, name in enumerate(names):
                for q in range(CQ):
                    sp.dma_start(bias[HW * q:HW * q + HW, n, :],
                                 io[name][32 * q:32 * q + 32, :].rearrange("c b -> b c").broadcast_to((HW, 32))).then_inc(bias_in, 16)
            sp.wait_ge(zeroed, 1)
            with sp.Fori(0, 16) as j:
                c = j * 2
                for n in range(2):
                    sp.wait_ge(maps_ps, c + n + 1)
                    for q in range(CQ):
                        rows = band_dram[:, bass.ds(c + (32 * q + n), 1), HW - 1:HW - 1 + HW * (BAND - 1)]
                        sp.dma_start(bands[n][HW * q:HW * q + HW, :, HW * q:HW * q + HW],
                                     rows.rearrange("t a (w e) -> w t (a e)", e=BAND - 1)[:, :, 0:HW]).then_inc(bands_in[n], 16)

        @block.tensor
        def _(pe):
            pe.sem_inc(maps_ps, 2)
            with pe.Fori(0, 16) as j:
                c = j * 2
                for n in range(2):
                    pe.wait_ge(bands_in[n], c * 32 + 64)
                    pe.wait_ge(maps_up, c + n + 1)
                    out4 = ps_s[n][:, 0:L].rearrange("p (b h) -> p b h", b=B)
                    src = u_cols[:, :, bass.ds(c + n, 1), :].rearrange("p b a h -> p b (a h)")
                    for j, ky in enumerate((2, 0, 1, 3, 4)):
                        d = ky - 2
                        lo, hi = max(0, -d), min(HW, HW - d)
                        last = pe.matmul(out4[:, :, lo:hi], bands[n][:, ky, :], src[:, :, lo + d:hi + d],
                                         start=(j == 0), stop=(j == 4))
                    last.then_inc(square_ps, 1)
                for n in range(2):
                    pe.wait_ge(square_up, c + n + 1)
                    pe.wait_ge(along_up, c + n + 1)
                    for k in range(K):
                        last = pe.matmul(ps_h[n][:, k, 0:L], bands[n][:, ROWS5 + 2 * k, :], square[n][:, :], start=True, stop=True)
                    last.then_inc(along_ps, 1)
                for n in range(2):
                    pe.wait_ge(turned, c + n + 3)
                    for k in range(K):
                        last = pe.matmul(ps_s[n][:, 0:L], bands[n][:, ROWS5 + 2 * k + 1, :], along_t[n][:, k, :],
                                         start=(k == 0), stop=(k == K - 1))
                    last.then_inc(maps_ps, 1)

        @block.scalar
        def _(act):
            act.wait_ge(bias_in, 16 * CQ * len(names))
            act.sem_inc(along_up, 2)
            act.sem_inc(square_turned, 2)
            act.sem_inc(turned, 2)
            with act.Fori(0, 16) as j:
                c = j * 2
                for n in range(2):
                    act.wait_ge(square_ps, c + n + 1)
                    act.wait_ge(square_turned, c + n + 1)
                    act.activation(square[n][:, :], ps_s[n][:, 0:L], ACT.Identity, bias=bias[:, 0, bass.ds(c + n, 1)]).then_inc(square_up, 1)
                for n in range(2):
                    act.wait_ge(along_ps, c + n + 1)
                    act.wait_ge(turned, c + n + 1)
                    for k in range(K):
                        last = act.activation(along[n][:, k, :], ps_h[n][:, k, 0:L], ACT.Identity,
                                              bias=bias[:, 1 + k, bass.ds(c + n, 1)])
                    last.then_inc(along_up, 1)

        @block.vector
        def _(dve):
            dve.wait_ge(bias_in, 16 * CQ * len(names))
            dve.tensor_tensor(last_bias[:, :], bias[:, 1 + K, :], bias[:, 2 + K, :], ALU.add)
            dve.drain()
            dve.tensor_tensor(last_bias[:, :], last_bias[:, :], bias[:, 3 + K, :], ALU.add)
            dve.drain()
            dve.sem_inc(maps_up, 2)
            with dve.Fori(0, 16) as j:
                c = j * 2
                for n in range(2):
                    dve.wait_ge(square_up, c + n + 1)
                    dve.transpose(square_t[n][:, :], square[n][:, :]).then_inc(square_turned, 1)
                for n in range(2):
                    dve.wait_ge(along_up, c + n + 3)
                    dve.transpose(along_t[n][:, :, :].rearrange("p k l -> p (k l)"), along[n][:, :, :].rearrange("p k l -> p (k l)")).then_inc(turned, 1)
                for n in range(2):
                    dve.wait_ge(maps_ps, c + n + 3)
                    dve.scalar_tensor_tensor(square_t[n][:, :], ps_s[n][:, 0:L], last_bias[:, bass.ds(c + n, 1)], square_t[n][:, :],
                                             ALU.add, ALU.add)
                    dve.drain()
                    dve.tensor_copy(maps[:, :, bass.ds(c + n, 1), :].rearrange("p b a w -> p b (a w)"),
                                    square_t[n][:, :].rearrange("p (b w) -> p b w", b=B)).then_inc(maps_up, 1)
                    dve.drain()


def token_norm(dve, i, out, tokens, stats, mv, var, inv, tmp):
    for t in range(NT):
        dve.bn_stats(stats[:, t, :], tokens[:, bass.ds(i, 1), t, :].rearrange("p a c -> p (a c)"))
    dve.drain()
    for t in range(NT):
        dve.bn_aggr(mv[:, t, :], stats[:, t, :])
    dve.drain()
    dve.tensor_scalar(var[:, :], mv[:, :, 1], 1e-5, None, ALU.add)
    dve.drain()
    rsqrt(dve, inv[:, :], var[:, :], tmp[:, :])
    for t in range(NT):
        last = dve.tensor_scalar(out[:, t, :], tokens[:, bass.ds(i, 1), t, :].rearrange("p a c -> p (a c)"),
                                 mv[:, t, 0:1], inv[:, t:t + 1], ALU.subtract, ALU.mult)
    return last


def turn_tiles(pe, out, tiles, ident):
    for t in range(NT):
        last = pe.transpose(out[:, 128 * t:128 * t + 128], tiles[:, t, :], ident)
    return last


def landmark_phase(nc, ctx, B, io, const, maps, gn2, x1_dram, tokens):
    with ExitStack() as st:
        def sb(name, shape, dt=F32):
            return st.enter_context(nc.sbuf_tensor("n_" + name, shape, dt))

        def sem(name):
            return ctx.enter_context(nc.semaphore("n_" + name))

        LM = 16
        STEP = N // LM
        NEWTON = 6
        SCALE = float(D) ** -0.5
        y_in, yt = sb("y_in", [128, 32, HW]), sb("yt", [128, N])
        x1, u = sb("x1", [128, N]), sb("u", [128, N])
        w3, wqkv, wproj = sb("w3", [128, C]), sb("wqkv", [128, 3 * C]), sb("wproj", [128, C])
        b3, qb, kb = sb("b3", [128, 1]), sb("qb", [128, 1]), sb("kb", [128, 1])
        vb, pb = sb("vb", [128, C]), sb("pb", [128, C])
        xln = sb("xln", [128, NT, C])
        xt, qt, kt = sb("xt", [128, N]), sb("qt", [128, N]), sb("kt", [128, N])
        v = sb("v", [128, NT, C])
        q_lm, k_lm = sb("q_lm", [128, C]), sb("k_lm", [128, C])
        k1, e3 = sb("k1", [128, NT, C]), sb("e3", [128, NT, 128])
        k1t, e3t = sb("k1t", [128, N]), sb("e3t", [128, N])
        max1, sum1 = sb("max1", [128, NT * HEADS]), sb("sum1", [128, NT * HEADS])
        max3, sum3 = sb("max3", [128, 1]), sb("sum3", [128, 1])
        max2, sum2, e2, e2q = sb("max2", [128, 1]), sb("sum2", [128, 1]), sb("e2", [128, LM]), sb("e2q", [128, LM])
        fro = sb("fro", [128, 1])
        m2, m2t = sb("m2", [128, 128]), sb("m2t", [128, 128])
        z, zt, mz = sb("z", [128, 128]), sb("zt", [128, 128]), sb("mz", [128, 128])
        kv, mixed, mixed_p = sb("kv", [128, 128]), sb("mixed", [128, 128]), sb("mixed_p", [128, 128])
        stats, mv = sb("stats", [128, NT, 6]), sb("mv", [128, NT, 2])
        var, inv, tmp = sb("var", [128, NT]), sb("inv", [128, NT]), sb("tmp", [128, NT])
        ps = [st.enter_context(nc.psum_tensor(f"n_ps{n}", [128, N], F32)) for n in range(4)]
        events = ("x1_in y_turned gate_ps x2_up tok_ps tok_up ln_up lnt_ps xt_up q_ps k_ps v_ps q_up k_up v_up lm_up "
                  "s2_ps s1_ps s3_ps d2_up e2_up m2_up m2t_ps fro_in fro_ps z0_up d1_up e1_up k1_up k1t_ps k1t_up max3_up e3_up e3t_ps e3t_up "
                  "kv_ps kv_up mixed_ps mixed_up mixp_ps mixp_up attn_ps done")
        S = {name: sem(name) for name in events.split()}
        mz_ps, mz_up, znew_ps, z_up = sem("mz_ps"), sem("mz_up"), sem("znew_ps"), sem("z_up")
        params_in, y_loaded = sem("params_in"), sem("y_loaded")
        params = [(w3[:, :], io["L1_w3T"]), (wqkv[:, :], io["L2_qkvT"]), (wproj[:, :], io["L2_projT"]), (b3[:, :], io["L1_conv_b3"]),
                  (qb[:, :], io["L2_attn_bqkv"][0:C, :]), (kb[:, :], io["L2_attn_bqkv"][C:2 * C, :]),
                  (vb[:, :], io["L2_attn_bqkv"][2 * C:3 * C, :].rearrange("c b -> b c").broadcast_to((128, C))),
                  (pb[:, :], io["L2_attn_bproj"].rearrange("c b -> b c").broadcast_to((128, C)))]
        block = st.enter_context(nc.Block())

        @block.sync
        def _(sp):
            for dst, src in params:
                sp.dma_start(dst, src).then_inc(params_in, 16)
            with sp.Fori(0, B) as i:
                sp.wait_ge(S["x2_up"], i + 1)
                sp.dma_start(y_in[:, :, :].rearrange("p c w -> p (c w)"), maps[:, bass.ds(i, 1), :, :].rearrange("p a c w -> p (a c w)")).then_inc(y_loaded, 16)
                sp.dma_start(x1[:, :], x1_dram[bass.ds(i, 1), :, :].rearrange("a c n -> (a c) n")).then_inc(S["x1_in"], 16)

        @block.vector
        def _(dve):
            dve.wait_ge(params_in, 16 * len(params))
            dve.sem_inc(S["x2_up"], 1)
            with dve.Fori(0, B) as i:
                dve.wait_ge(y_loaded, i * 16 + 16)
                dve.transpose(yt[:, :].rearrange("p (h w) -> p w h", h=HW), y_in[:, :, :].rearrange("p c w -> p w c")).then_inc(S["y_turned"], 1)
                dve.wait_ge(S["x1_in"], i * 16 + 16)
                dve.tensor_scalar(u[:, :], x1[:, :], gn2[:, 0, bass.ds(i, 1)], gn2[:, 1, bass.ds(i, 1)], ALU.mult, ALU.add)
                dve.drain()
                dve.wait_ge(S["gate_ps"], i + 1)
                dve.scalar_tensor_tensor(u[:, :], ps[0][:, :], b3[:, :], u[:, :], ALU.add, ALU.mult)
                dve.drain()
                dve.tensor_tensor(u[:, :], u[:, :], x1[:, :], ALU.add).then_inc(S["x2_up"], 1)
                dve.wait_ge(S["tok_up"], i + 1)
                token_norm(dve, i, xln, tokens, stats, mv, var, inv, tmp).then_inc(S["ln_up"], 1)
                dve.wait_ge(S["v_ps"], i + 1)
                dve.tensor_tensor(v[:, :, :], ps[3][:, :].rearrange("p (t c) -> p t c", t=NT),
                                  vb[:, :].unsqueeze(1).broadcast_to((128, NT, C)), ALU.add).then_inc(S["v_up"], 1)
                for src, dst, up in ((qt, q_lm, "q_up"), (kt, k_lm, "k_up")):
                    dve.wait_ge(S[up], i + 1)
                    last = dve.tensor_tensor(dst[:, :].rearrange("p (h l) -> p h l", h=HEADS), const["block16"].rearrange("p (h l) -> p h l", h=HEADS),
                                             src[:, 0:N:STEP].unsqueeze(1).broadcast_to((128, HEADS, LM)), ALU.mult)
                last.then_inc(S["lm_up"], 1)
                dve.wait_ge(S["s2_ps"], i + 1)
                dve.tensor_reduce(max2[:, :], ps[2][:, 0:LM], axis=AX.X, op=ALU.max)
                dve.drain()
                dve.tensor_scalar(e2[:, :], ps[2][:, 0:LM], max2[:, :], None, ALU.subtract).then_inc(S["d2_up"], 1)
                dve.wait_ge(S["e2_up"], i + 1)
                dve.reciprocal(sum2[:, :], sum2[:, :])
                dve.drain()
                dve.tensor_scalar(e2[:, :], e2[:, :], sum2[:, :], None, ALU.mult)
                dve.drain()
                dve.tensor_tensor(m2[:, :].rearrange("p (h l) -> p h l", h=HEADS), const["block16"].rearrange("p (h l) -> p h l", h=HEADS),
                                  e2[:, :].unsqueeze(1).broadcast_to((128, HEADS, LM)), ALU.mult).then_inc(S["m2_up"], 1)
                dve.tensor_tensor(e2q[:, :], e2[:, :], e2[:, :], ALU.mult)
                dve.drain()
                dve.tensor_reduce(max2[:, :], e2q[:, :], axis=AX.X, op=ALU.add).then_inc(S["fro_in"], 1)
                dve.wait_ge(S["fro_ps"], i + 1)
                dve.wait_ge(S["m2t_ps"], i + 1)
                dve.tensor_scalar(fro[:, :], ps[2][:, 0:1], 1e-12, None, ALU.max)
                dve.tensor_copy(m2t[:, :], ps[3][:, 0:128])
                dve.drain()
                dve.reciprocal(fro[:, :], fro[:, :])
                dve.drain()
                dve.tensor_scalar(z[:, :], m2t[:, :], fro[:, :], None, ALU.mult)
                dve.tensor_scalar(zt[:, :], m2[:, :], fro[:, :], None, ALU.mult).then_inc(S["z0_up"], 1)
                for it in range(NEWTON):
                    dve.drain()
                    dve.wait_ge(mz_ps, i * NEWTON + it + 1)
                    dve.tensor_copy(mz[:, :], ps[2][:, 0:128]).then_inc(mz_up, 1)
                    dve.wait_ge(znew_ps, i * NEWTON + it + 1)
                    dve.scalar_tensor_tensor(z[:, :], z[:, :], 2.0, ps[2][:, 512:640], ALU.mult, ALU.subtract)
                    dve.scalar_tensor_tensor(zt[:, :], zt[:, :], 2.0, ps[3][:, 512:640], ALU.mult, ALU.subtract).then_inc(z_up, 1)
                    dve.drain()
                s1 = ps[0][:, :].rearrange("p (g l) -> p g l", l=LM)
                k1v = k1[:, :, :].rearrange("p t (h l) -> p (t h) l", l=LM)
                dve.wait_ge(S["s1_ps"], i + 1)
                dve.tensor_reduce(max1[:, :], s1, axis=AX.X, op=ALU.max)
                dve.drain()
                dve.tensor_tensor(k1v, s1, max1[:, :].unsqueeze(2).broadcast_to((128, NT * HEADS, LM)), ALU.subtract).then_inc(S["d1_up"], 1)
                dve.wait_ge(S["s3_ps"], i + 1)
                dve.tensor_reduce(max3[:, :], ps[1][:, :], axis=AX.X, op=ALU.max)
                dve.drain()
                dve.tensor_scalar(max3[:, :], max3[:, :], -SCALE, None, ALU.mult).then_inc(S["max3_up"], 1)
                dve.wait_ge(S["e1_up"], i + 1)
                dve.tensor_reduce(sum1[:, :], k1v, axis=AX.X, op=ALU.add)
                dve.drain()
                dve.reciprocal(sum1[:, :], sum1[:, :])
                dve.drain()
                dve.tensor_tensor(k1v, k1v, sum1[:, :].unsqueeze(2).broadcast_to((128, NT * HEADS, LM)), ALU.mult).then_inc(S["k1_up"], 1)
                dve.wait_ge(S["e3_up"], i + 1)
                dve.reciprocal(sum3[:, :], sum3[:, :])
                dve.drain()
                dve.wait_ge(S["kv_ps"], i + 1)
                dve.scalar_tensor_tensor(kv[:, :], ps[2][:, 0:128], sum3[:, :], const["block16"], ALU.mult, ALU.mult).then_inc(S["kv_up"], 1)
                dve.wait_ge(S["mixed_ps"], i + 1)
                dve.tensor_copy(mixed[:, :], ps[2][:, 0:128]).then_inc(S["mixed_up"], 1)
                dve.wait_ge(S["mixp_ps"], i + 1)
                dve.tensor_copy(mixed_p[:, :], ps[2][:, 512:640]).then_inc(S["mixp_up"], 1)
                here = tokens[:, bass.ds(i, 1), :, :].rearrange("p a t c -> p (a t) c")
                dve.tensor_tensor(here, here, pb[:, :].unsqueeze(1).broadcast_to((128, NT, C)), ALU.add)
                dve.drain()
                dve.wait_ge(S["attn_ps"], i + 1)
                dve.tensor_tensor(here, here, ps[3][:, :].rearrange("p (t c) -> p t c", t=NT), ALU.add).then_inc(S["done"], 1)
                dve.drain()

        @block.scalar
        def _(act):
            act.wait_ge(params_in, 16 * len(params))
            with act.Fori(0, B) as i:
                act.wait_ge(S["tok_ps"], i + 1)
                act.activation(tokens[:, bass.ds(i, 1), :, :].rearrange("p a t c -> p (a t c)"), ps[1][:, :], ACT.Copy).then_inc(S["tok_up"], 1)
                act.wait_ge(S["lnt_ps"], i + 1)
                act.activation(xt[:, :], ps[0][:, :], ACT.Copy).then_inc(S["xt_up"], 1)
                act.wait_ge(S["q_ps"], i + 1)
                act.activation(qt[:, :], ps[1][:, :], ACT.Identity, bias=qb[:, :]).then_inc(S["q_up"], 1)
                act.wait_ge(S["k_ps"], i + 1)
                act.activation(kt[:, :], ps[2][:, :], ACT.Identity, bias=kb[:, :]).then_inc(S["k_up"], 1)
                act.wait_ge(S["d2_up"], i + 1)
                act.activation(e2[:, :], e2[:, :], ACT.Exp, scale=SCALE, accum_out=sum2[:, :]).then_inc(S["e2_up"], 1)
                act.wait_ge(S["d1_up"], i + 1)
                act.activation(k1[:, :, :], k1[:, :, :], ACT.Exp, scale=SCALE).then_inc(S["e1_up"], 1)
                act.wait_ge(S["max3_up"], i + 1)
                act.activation(e3[:, :, :].rearrange("p t n -> p (t n)"), ps[1][:, :], ACT.Exp, scale=SCALE, bias=max3[:, :], accum_out=sum3[:, :]).then_inc(S["e3_up"], 1)
                act.wait_ge(S["k1t_ps"], i + 1)
                act.activation(k1t[:, :], ps[0][:, :], ACT.Copy).then_inc(S["k1t_up"], 1)
                act.wait_ge(S["e3t_ps"], i + 1)
                act.activation(e3t[:, :], ps[1][:, :], ACT.Copy).then_inc(S["e3t_up"], 1)

        @block.tensor
        def _(pe):
            pe.wait_ge(params_in, 16 * len(params))
            ident = const["ident"]

            def wide(out, w, src):
                for k in range(HALVES):
                    last = pe.matmul(out[:, 512 * k:512 * k + 512], w, src[:, 512 * k:512 * k + 512], start=True, stop=True)
                return last

            with pe.Fori(0, B) as i:
                pe.wait_ge(S["y_turned"], i + 1)
                wide(ps[0], w3[:, :], yt).then_inc(S["gate_ps"], 1)
                pe.wait_ge(S["x2_up"], i + 2)
                for t in range(NT):
                    last = pe.transpose(ps[1][:, 128 * t:128 * t + 128], u[:, 128 * t:128 * t + 128], ident)
                last.then_inc(S["tok_ps"], 1)
                pe.wait_ge(S["ln_up"], i + 1)
                turn_tiles(pe, ps[0], xln, ident).then_inc(S["lnt_ps"], 1)
                pe.wait_ge(S["xt_up"], i + 1)
                wide(ps[1], wqkv[:, 0:C], xt).then_inc(S["q_ps"], 1)
                wide(ps[2], wqkv[:, C:2 * C], xt).then_inc(S["k_ps"], 1)
                for t in range(NT):
                    last = pe.matmul(ps[3][:, 128 * t:128 * t + 128], xt[:, 128 * t:128 * t + 128], wqkv[:, 2 * C:3 * C], start=True, stop=True)
                last.then_inc(S["v_ps"], 1)
                pe.wait_ge(S["lm_up"], i + 1)
                pe.matmul(ps[2][:, 0:LM], q_lm[:, :], kt[:, 0:N:STEP], start=True, stop=True).then_inc(S["s2_ps"], 1)
                for t in range(NT):
                    last = pe.matmul(ps[0][:, 128 * t:128 * t + 128], qt[:, 128 * t:128 * t + 128], k_lm[:, :], start=True, stop=True)
                last.then_inc(S["s1_ps"], 1)
                wide(ps[1], q_lm[:, :], kt).then_inc(S["s3_ps"], 1)
                pe.wait_ge(S["m2_up"], i + 1)
                pe.wait_ge(S["v_up"], i + 1)
                pe.transpose(ps[3][:, 0:128], m2[:, :], ident).then_inc(S["m2t_ps"], 1)
                pe.wait_ge(S["fro_in"], i + 1)
                pe.matmul(ps[2][:, 0:1], const["block16"], max2[:, :], start=True, stop=True).then_inc(S["fro_ps"], 1)
                pe.wait_ge(S["z0_up"], i + 1)
                for it in range(NEWTON):
                    if it:
                        pe.wait_ge(z_up, i * NEWTON + it)
                    pe.matmul(ps[2][:, 0:128], m2t[:, :], z[:, :], start=True, stop=True).then_inc(mz_ps, 1)
                    pe.wait_ge(mz_up, i * NEWTON + it + 1)
                    pe.matmul(ps[2][:, 512:640], zt[:, :], mz[:, :], start=True, stop=True)
                    pe.matmul(ps[3][:, 512:640], mz[:, :], zt[:, :], start=True, stop=True).then_inc(znew_ps, 1)
                pe.wait_ge(S["k1_up"], i + 1)
                turn_tiles(pe, ps[0], k1, ident).then_inc(S["k1t_ps"], 1)
                pe.wait_ge(S["e3_up"], i + 1)
                turn_tiles(pe, ps[1], e3, ident).then_inc(S["e3t_ps"], 1)
                pe.wait_ge(S["e3t_up"], i + 1)
                for t in range(NT):
                    last = pe.matmul(ps[2][:, 0:128], e3t[:, 128 * t:128 * t + 128], v[:, t, :], start=(t == 0), stop=(t == NT - 1))
                last.then_inc(S["kv_ps"], 1)
                pe.wait_ge(S["kv_up"], i + 1)
                pe.matmul(ps[2][:, 0:128], kv[:, :], zt[:, :], start=True, stop=True).then_inc(S["mixed_ps"], 1)
                pe.wait_ge(S["mixed_up"], i + 1)
                pe.matmul(ps[2][:, 512:640], mixed[:, :], wproj[:, :], start=True, stop=True).then_inc(S["mixp_ps"], 1)
                pe.wait_ge(S["mixp_up"], i + 1)
                pe.wait_ge(S["k1t_up"], i + 1)
                for t in range(NT):
                    last = pe.matmul(ps[3][:, 128 * t:128 * t + 128], k1t[:, 128 * t:128 * t + 128], mixed_p[:, :], start=True, stop=True)
                last.then_inc(S["attn_ps"], 1)


def gate_tiles(st_sb, E):
    t = {n: st_sb("gate_" + n, [128, NT, E]) for n in ("logits", "probs", "rank", "chosen", "score")}
    t.update({n: st_sb("gate_" + n, [128, NT]) for n in ("top", "total", "picked")})
    t.update({n: st_sb("gate_" + n, [128, NT * E, E]) for n in ("above", "same")})
    return t


def gate_shift(dve, t, E):
    dve.tensor_reduce(t["top"][:, :], t["logits"][:, :, :], axis=AX.X, op=ALU.max)
    dve.drain()
    return dve.tensor_tensor(t["probs"][:, :, :], t["logits"][:, :, :], t["top"][:, :].unsqueeze(2).broadcast_to((128, NT, E)), ALU.subtract)


def gate_choose(dve, t, E, K, eps, tie):
    p, rank, chosen = t["probs"], t["rank"], t["chosen"]
    other = p[:, :, :].unsqueeze(2).broadcast_to((128, NT, E, E))
    own = p[:, :, :].unsqueeze(3).broadcast_to((128, NT, E, E))
    above = t["above"][:, :, :].rearrange("p (t e) f -> p t e f", t=NT)
    same = t["same"][:, :, :].rearrange("p (t e) f -> p t e f", t=NT)
    dve.tensor_tensor(above, other, own, ALU.is_gt)
    dve.tensor_tensor(same, other, own, ALU.is_equal)
    dve.tensor_reduce(t["total"][:, :], p[:, :, :], axis=AX.X, op=ALU.add)
    dve.drain()
    flat = t["same"][:, :, :].rearrange("p (t e) f -> p t (e f)", t=NT)
    dve.tensor_tensor(flat, flat, tie.unsqueeze(1).broadcast_to((128, NT, E * E)), ALU.mult)
    dve.drain()
    dve.tensor_tensor(t["above"][:, :, :], t["above"][:, :, :], t["same"][:, :, :], ALU.add)
    dve.drain()
    dve.tensor_reduce(rank[:, :, :], above, axis=AX.X, op=ALU.add)
    dve.drain()
    dve.tensor_scalar(chosen[:, :, :], rank[:, :, :], float(K), None, ALU.is_lt)
    dve.drain()
    dve.tensor_tensor(t["score"][:, :, :], p[:, :, :], chosen[:, :, :], ALU.mult)
    dve.drain()
    dve.tensor_reduce(t["picked"][:, :], t["score"][:, :, :], axis=AX.X, op=ALU.add)
    dve.drain()
    dve.scalar_tensor_tensor(t["picked"][:, :], t["total"][:, :], eps, t["picked"][:, :], ALU.mult, ALU.add)
    dve.drain()
    dve.reciprocal(t["picked"][:, :], t["picked"][:, :])
    dve.drain()
    return dve.tensor_tensor(t["score"][:, :, :], t["score"][:, :, :], t["picked"][:, :].unsqueeze(2).broadcast_to((128, NT, E)), ALU.mult)


def gelu_experts_phase(nc, ctx, B, io, const, tokens):
    with ExitStack() as st:
        def sb(name, shape, dt=F32):
            return st.enter_context(nc.sbuf_tensor("g_" + name, shape, dt))

        def sem(name):
            return ctx.enter_context(nc.semaphore("g_" + name))

        E, K, F = 8, 2, 512
        FT = F // 128
        xln, xt = sb("xln", [128, NT, C]), sb("xt", [128, N])
        stats, mv = sb("stats", [128, NT, 6]), sb("mv", [128, NT, 2])
        var, inv, tmp = sb("var", [128, NT]), sb("inv", [128, NT]), sb("tmp", [128, NT])
        gate = gate_tiles(sb, E)
        score_t = sb("score_t", [E, N])
        hidden = sb("hidden", [128, 2, FT, N])
        wg, w1, w2 = sb("wg", [128, E]), sb("w1", [128, E, F]), sb("w2", [128, E, FT, C])
        b1, b2, tie = sb("b1", [128, E, FT]), sb("b2", [E, C]), sb("tie", [128, E * E])
        ps_h = [st.enter_context(nc.psum_tensor(f"g_ps_h{n}", [128, N], F32)) for n in range(2)]
        ps_y = [st.enter_context(nc.psum_tensor(f"g_ps_y{n}", [128, N], F32)) for n in range(2)]
        events = "ln_up lnt_ps xt_up gate_ps shift_up exp_up score_up st_ps st_up b2_ps done"
        S = {name: sem(name) for name in events.split()}
        params_in, hidden_ps, hidden_up, y_ps, y_added = sem("params_in"), sem("hidden_ps"), sem("hidden_up"), sem("y_ps"), sem("y_added")
        params = [(wg[:, :], io["L2_ffn_Wg"]), (w1[:, :, :], io["L2_ffn_W1"].rearrange("e d f -> d e f")),
                  (b2[:, :], io["L2_ffn_b2"]), (tie[:, :], io["const_tie8"])]
        params += [(w2[:, e, :, :], io["L2_ffn_W2"][e, :, :].rearrange("(t f) d -> f t d", t=FT)) for e in range(E)]
        params += [(b1[:, e, t:t + 1], io["L2_ffn_b1"][e:e + 1, 128 * t:128 * t + 128].rearrange("e f -> f e")) for e in range(E) for t in range(FT)]
        H_PER = E * FT
        block = st.enter_context(nc.Block())

        @block.sync
        def _(sp):
            for dst, src in params:
                sp.dma_start(dst, src).then_inc(params_in, 16)

        @block.vector
        def _(dve):
            dve.wait_ge(params_in, 16 * len(params))
            with dve.Fori(0, B) as i:
                token_norm(dve, i, xln, tokens, stats, mv, var, inv, tmp).then_inc(S["ln_up"], 1)
                dve.wait_ge(S["gate_ps"], i + 1)
                dve.tensor_copy(gate["logits"][:, :, :], ps_h[1][:, 0:NT * E].rearrange("p (t e) -> p t e", t=NT))
                dve.drain()
                gate_shift(dve, gate, E).then_inc(S["shift_up"], 1)
                dve.wait_ge(S["exp_up"], i + 1)
                gate_choose(dve, gate, E, K, 1e-6, tie[:, :]).then_inc(S["score_up"], 1)
                dve.wait_ge(S["st_ps"], i + 1)
                dve.tensor_copy(score_t[:, :], ps_y[0][0:E, :]).then_inc(S["st_up"], 1)
                dve.drain()
                dve.wait_ge(S["b2_ps"], i + 1)
                here = tokens[:, bass.ds(i, 1), :, :].rearrange("p a t c -> p (a t) c")
                dve.tensor_tensor(here, here, ps_y[1][:, :].rearrange("p (t c) -> p t c", t=NT), ALU.add).then_inc(S["done"], 1)
                dve.drain()
                for e in range(E):
                    dve.wait_ge(y_ps, i * E + e + 1)
                    for t in range(NT):
                        tile = tokens[:, bass.ds(i, 1), t, :].rearrange("p a c -> p (a c)")
                        last = dve.scalar_tensor_tensor(tile, ps_y[e % 2][:, 128 * t:128 * t + 128], gate["score"][:, t, e:e + 1], tile,
                                                        ALU.mult, ALU.add)
                    last.then_inc(y_added, 1)
                    dve.drain()

        @block.scalar
        def _(act):
            act.wait_ge(params_in, 16 * len(params))
            with act.Fori(0, B) as i:
                act.wait_ge(S["lnt_ps"], i + 1)
                act.activation(xt[:, :], ps_h[0][:, :], ACT.Copy).then_inc(S["xt_up"], 1)
                act.wait_ge(S["shift_up"], i + 1)
                act.activation(gate["probs"][:, :, :], gate["probs"][:, :, :], ACT.Exp).then_inc(S["exp_up"], 1)
                for n in range(H_PER):
                    e, f = divmod(n, FT)
                    act.wait_ge(hidden_ps, i * H_PER + n + 1)
                    act.activation(hidden[:, e % 2, f, :], ps_h[n % 2][:, :], ACT.Gelu, bias=b1[:, e, f:f + 1]).then_inc(hidden_up, 1)

        @block.tensor
        def _(pe):
            pe.wait_ge(params_in, 16 * len(params))
            with pe.Fori(0, B) as i:
                pe.wait_ge(S["ln_up"], i + 1)
                turn_tiles(pe, ps_h[0], xln, const["ident"]).then_inc(S["lnt_ps"], 1)
                pe.wait_ge(S["xt_up"], i + 1)
                for t in range(NT):
                    last = pe.matmul(ps_h[1][:, E * t:E * t + E], xt[:, 128 * t:128 * t + 128], wg[:, :], start=True, stop=True)
                last.then_inc(S["gate_ps"], 1)
                pe.wait_ge(S["score_up"], i + 1)
                for t in range(NT):
                    last = pe.transpose(ps_y[0][0:E, 128 * t:128 * t + 128], gate["score"][:, t, :], const["ident"])
                last.then_inc(S["st_ps"], 1)
                pe.wait_ge(S["st_up"], i + 1)
                for t in range(NT):
                    last = pe.matmul(ps_y[1][:, 128 * t:128 * t + 128], score_t[:, 128 * t:128 * t + 128], b2[:, :], start=True, stop=True)
                last.then_inc(S["b2_ps"], 1)
                pe.wait_ge(S["done"], i + 1)

                def second_layer(e):
                    pe.wait_ge(hidden_up, i * H_PER + FT * e + FT)
                    if e >= 2:
                        pe.wait_ge(y_added, i * E + e - 1)
                    for t in range(NT):
                        for f in range(FT):
                            last = pe.matmul(ps_y[e % 2][:, 128 * t:128 * t + 128], hidden[:, e % 2, f, 128 * t:128 * t + 128],
                                             w2[:, e, f, :], start=(f == 0), stop=(f == FT - 1))
                    last.then_inc(y_ps, 1)

                for e in range(E):
                    for f in range(FT):
                        n = e * FT + f
                        if n >= 2:
                            pe.wait_ge(hidden_up, i * H_PER + n - 1)
                        for k in range(HALVES):
                            last = pe.matmul(ps_h[n % 2][:, 512 * k:512 * k + 512], w1[:, e, 128 * f:128 * f + 128],
                                             xt[:, 512 * k:512 * k + 512], start=True, stop=True)
                        last.then_inc(hidden_ps, 1)
                    if e:
                        second_layer(e - 1)
                second_layer(E - 1)


def self_attention_phase(nc, ctx, B, io, const, tokens):
    with ExitStack() as st:
        def sb(name, shape, dt=F32):
            return st.enter_context(nc.sbuf_tensor("t_" + name, shape, dt))

        def sem(name):
            return ctx.enter_context(nc.semaphore("t_" + name))

        xln, xt, qt = sb("xln", [128, NT, C]), sb("xt", [128, N]), sb("qt", [128, N])
        stats, mv = sb("stats", [128, NT, 6]), sb("mv", [128, NT, 2])
        var, inv, tmp = sb("var", [128, NT]), sb("inv", [128, NT]), sb("tmp", [128, NT])
        w, b = sb("w", [128, C]), sb("b", [128, 1])
        negmax, sums = sb("negmax", [128, NT]), sb("sums", [128, NT])
        probs, probs_t = sb("probs", [128, 2, N]), sb("probs_t", [128, 2, NT, 128])
        ps_s = [st.enter_context(nc.psum_tensor(f"t_ps_s{n}", [128, N], F32)) for n in range(2)]
        ps_t = st.enter_context(nc.psum_tensor("t_ps_t", [128, N], F32))
        ps_o = [st.enter_context(nc.psum_tensor(f"t_ps_o{n}", [128, 512], F32)) for n in range(2)]
        S = {name: sem(name) for name in "params_in ln_up lnt_ps xt_up q_ps q_up s_ps max_up exp_up turned_ps turned_v turned_a out_ps added".split()}
        block = st.enter_context(nc.Block())

        @block.sync
        def _(sp):
            sp.dma_start(w[:, :], io["L3_attn_W"]).then_inc(S["params_in"], 16)
            sp.dma_start(b[:, :], io["L3_attn_b"]).then_inc(S["params_in"], 16)

        def add_out(dve, i, t):
            dve.wait_ge(S["out_ps"], i * NT + t + 1)
            dve.reciprocal(sums[:, t:t + 1], sums[:, t:t + 1])
            dve.drain()
            tile = tokens[:, bass.ds(i, 1), t, :].rearrange("p a c -> p (a c)")
            dve.scalar_tensor_tensor(tile, ps_o[t % 2][:, 0:C], sums[:, t:t + 1], tile, ALU.mult, ALU.add).then_inc(S["added"], 1)
            dve.drain()

        @block.vector
        def _(dve):
            with dve.Fori(0, B) as i:
                token_norm(dve, i, xln, tokens, stats, mv, var, inv, tmp).then_inc(S["ln_up"], 1)

                def row_max(t):
                    dve.wait_ge(S["s_ps"], i * NT + t + 1)
                    dve.tensor_reduce(negmax[:, t:t + 1], ps_s[t % 2][:, :], axis=AX.X, op=ALU.max, negate=True).then_inc(S["max_up"], 1)

                row_max(0)
                for t in range(NT):
                    if t + 1 < NT:
                        row_max(t + 1)
                    dve.wait_ge(S["turned_ps"], i * NT + t + 1)
                    dve.tensor_copy(probs_t[:, t % 2, 0:4, :].rearrange("p m n -> p (m n)"), ps_t[:, 0:512]).then_inc(S["turned_v"], 1)
                    if t == 0:
                        continue
                    add_out(dve, i, t - 1)
                add_out(dve, i, NT - 1)

        @block.scalar
        def _(act):
            act.wait_ge(S["params_in"], 32)
            with act.Fori(0, B) as i:
                act.wait_ge(S["lnt_ps"], i + 1)
                act.activation(xt[:, :], ps_s[0][:, :], ACT.Copy).then_inc(S["xt_up"], 1)
                act.wait_ge(S["q_ps"], i + 1)
                act.activation(qt[:, :], ps_s[1][:, :], ACT.Identity, bias=b[:, :]).then_inc(S["q_up"], 1)

                def exponential(t):
                    act.wait_ge(S["max_up"], i * NT + t + 1)
                    if t >= 2:
                        act.wait_ge(S["turned_ps"], i * NT + t - 1)
                    act.activation(probs[:, t % 2, :], ps_s[t % 2][:, :], ACT.Exp, bias=negmax[:, t:t + 1], accum_out=sums[:, t:t + 1]).then_inc(S["exp_up"], 1)

                exponential(0)
                for t in range(NT):
                    if t + 1 < NT:
                        exponential(t + 1)
                    act.wait_ge(S["turned_ps"], i * NT + t + 1)
                    act.activation(probs_t[:, t % 2, 4:8, :].rearrange("p m n -> p (m n)"), ps_t[:, 512:1024], ACT.Copy).then_inc(S["turned_a"], 1)

        @block.tensor
        def _(pe):
            pe.wait_ge(S["params_in"], 32)
            with pe.Fori(0, B) as i:
                pe.wait_ge(S["ln_up"], i + 1)
                turn_tiles(pe, ps_s[0], xln, const["ident"]).then_inc(S["lnt_ps"], 1)
                pe.wait_ge(S["xt_up"], i + 1)
                for k in range(HALVES):
                    last = pe.matmul(ps_s[1][:, 512 * k:512 * k + 512], w[:, :], xt[:, 512 * k:512 * k + 512], start=True, stop=True)
                last.then_inc(S["q_ps"], 1)
                pe.wait_ge(S["q_up"], i + 1)

                def scores(t):
                    if t >= 2:
                        pe.wait_ge(S["exp_up"], i * NT + t - 1)
                    for k in range(HALVES):
                        last = pe.matmul(ps_s[t % 2][:, 512 * k:512 * k + 512], qt[:, 128 * t:128 * t + 128], qt[:, 512 * k:512 * k + 512], start=True, stop=True)
                    last.then_inc(S["s_ps"], 1)

                def weigh(t):
                    pe.wait_ge(S["turned_v"], i * NT + t + 1)
                    pe.wait_ge(S["turned_a"], i * NT + t + 1)
                    if t >= 2:
                        pe.wait_ge(S["added"], i * NT + t - 1)
                    for m in range(NT):
                        last = pe.matmul(ps_o[t % 2][:, 0:C], probs_t[:, t % 2, m, :], xln[:, m, :], start=(m == 0), stop=(m == NT - 1))
                    last.then_inc(S["out_ps"], 1)

                scores(0)
                scores(1)
                for t in range(NT):
                    if t:
                        pe.wait_ge(S["turned_v"], i * NT + t)
                        pe.wait_ge(S["turned_a"], i * NT + t)
                    pe.wait_ge(S["exp_up"], i * NT + t + 1)
                    for m in range(NT):
                        last = pe.transpose(ps_t[:, 128 * m:128 * m + 128], probs[:, t % 2, 128 * m:128 * m + 128], const["ident"])
                    last.then_inc(S["turned_ps"], 1)
                    if t + 2 < NT:
                        scores(t + 2)
                    if t:
                        weigh(t - 1)
                weigh(NT - 1)


def silu_experts_phase(nc, ctx, B, io, const, tokens, out):
    with ExitStack() as st:
        def sb(name, shape, dt=F32):
            return st.enter_context(nc.sbuf_tensor("e_" + name, shape, dt))

        def sem(name):
            return ctx.enter_context(nc.semaphore("e_" + name))

        E, K, F = 16, 6, 64
        PAIRS = E * F // 128
        UNITS = PAIRS + 1
        CAP = max(1, int(B * N * K * 2.0 / E))
        xln, xt = sb("xln", [128, NT, C]), sb("xt", [128, N])
        stats, mv = sb("stats", [128, NT, 6]), sb("mv", [128, NT, 2])
        var, inv, tmp = sb("var", [128, NT]), sb("inv", [128, NT]), sb("tmp", [128, NT])
        gate = gate_tiles(sb, E)
        tile_in = sb("tile_in", [128, NT, C])
        chosen_before = sb("chosen_before", [128, NT + 1, E])
        score_t = sb("score_t", [E, N])
        wg, wu, wd = sb("wg", [128, UNITS, 128]), sb("wu", [128, UNITS, 128]), sb("wd", [128, UNITS, C])
        wr, rbias, tie = sb("wr", [128, E]), sb("rbias", [128, E]), sb("tie", [128, E * E])
        before, ones, pairsel = sb("before", [128, 128]), sb("ones", [128, 128]), sb("pairsel", [E, PAIRS, 128])
        act_up, mixed = sb("act_up", [128, 2, 512]), sb("mixed", [128, 2, 512])
        result = sb("result", [128, 2, 512])
        ps_g, ps_u, ps_b = ([st.enter_context(nc.psum_tensor(f"e_ps_{x}{n}", [128, 512], F32)) for n in range(2)] for x in "gub")
        ps_o = [st.enter_context(nc.psum_tensor(f"e_ps_o{n}", [128, 512], F32)) for n in range(2)]
        S = {name: sem(name) for name in "params_in ln_up lnt_ps xt_up gate_ps shift_up exp_up chosen_up count_ps score_up st_ps st_up out_ps result_up".split()}
        unit_ps, silu_up, mixed_up = sem("unit_ps"), sem("silu_up"), sem("mixed_up")
        stored = [sem(f"stored{n}") for n in range(2)]
        params = [(wr[:, :], io["L3_routerT"]), (rbias[:, :], io["L3_ffn_bias"].rearrange("c b -> b c").broadcast_to((128, E))),
                  (tie[:, :], io["const_tie16"]), (before[:, :], io["const_before"]), (ones[:, :], io["const_ones"]),
                  (pairsel[:, :, :], io["const_pairsel"].rearrange("e (q p) -> e q p", q=PAIRS)),
                  (wg[:, 0:PAIRS, :], io["L3_gT"].rearrange("d (q f) -> d q f", q=PAIRS)), (wg[:, PAIRS, :], io["L3_sgT"]),
                  (wu[:, 0:PAIRS, :], io["L3_uT"].rearrange("d (q f) -> d q f", q=PAIRS)), (wu[:, PAIRS, :], io["L3_suT"]),
                  (wd[:, 0:PAIRS, :], io["L3_dT"].rearrange("(q f) d -> f q d", q=PAIRS)), (wd[:, PAIRS, :], io["L3_sdT"])]
        STEPS = HALVES * UNITS
        block = st.enter_context(nc.Block())

        @block.sync
        def _(sp):
            for dst, src in params:
                sp.dma_start(dst, src).then_inc(S["params_in"], 16)
            with sp.Fori(0, B) as i:
                for k in range(HALVES):
                    sp.wait_ge(S["result_up"], i * HALVES + k + 2)
                    sp.dma_start(out[bass.ds(i, 1), :, 512 * k:512 * k + 512].rearrange("a c n -> (a c) n"), result[:, k, :]).then_inc(stored[k], 16)
            for k in range(HALVES):
                sp.wait_ge(stored[k], 16 * B + 16)

        @block.vector
        def _(dve):
            dve.memset(chosen_before[:, :, :], 0.0)
            dve.wait_ge(S["params_in"], 16 * len(params))
            dve.drain()
            with dve.Fori(0, B) as i:
                token_norm(dve, i, xln, tokens, stats, mv, var, inv, tmp)
                dve.tensor_copy(tile_in[:, :, :], tokens[:, bass.ds(i, 1), :, :].rearrange("p a t c -> p (a t) c")).then_inc(S["ln_up"], 1)
                dve.wait_ge(S["gate_ps"], i + 1)
                dve.tensor_tensor(gate["logits"][:, :, :], ps_u[0][:, 0:NT * E].rearrange("p (t e) -> p t e", t=NT),
                                  rbias[:, :].unsqueeze(1).broadcast_to((128, NT, E)), ALU.add)
                dve.drain()
                gate_shift(dve, gate, E).then_inc(S["shift_up"], 1)
                dve.wait_ge(S["exp_up"], i + 1)
                gate_choose(dve, gate, E, K, 1e-9, tie[:, :])
                dve.drain()
                for t in range(NT):
                    last = dve.tensor_tensor(chosen_before[:, t + 1, :], chosen_before[:, t, :], gate["chosen"][:, t, :], ALU.add)
                    dve.drain()
                dve.drain().then_inc(S["chosen_up"], 1)
                dve.wait_ge(S["count_ps"], i + 1)
                dve.tensor_copy(chosen_before[:, 0, :], chosen_before[:, NT, :])
                dve.scalar_tensor_tensor(gate["score"][:, :, :], ps_u[1][:, 0:NT * E].rearrange("p (t e) -> p t e", t=NT), float(CAP), gate["score"][:, :, :],
                                         ALU.is_lt, ALU.mult).then_inc(S["score_up"], 1)
                dve.drain()
                for k in range(HALVES):
                    dve.wait_ge(S["st_ps"], i * HALVES + k + 1)
                    dve.tensor_copy(score_t[:, 512 * k:512 * k + 512], ps_g[k][0:E, :]).then_inc(S["st_up"], 1)
                for n in range(STEPS):
                    k, unit = divmod(n, UNITS)
                    dve.wait_ge(silu_up, i * STEPS + n + 1)
                    if unit < PAIRS:
                        dve.tensor_tensor(act_up[:, n % 2, :], act_up[:, n % 2, :], ps_u[n % 2][:, :], ALU.mult)
                        dve.drain()
                        dve.tensor_tensor(mixed[:, n % 2, :], act_up[:, n % 2, :], ps_b[n % 2][:, :], ALU.mult).then_inc(mixed_up, 1)
                    else:
                        dve.scalar_tensor_tensor(mixed[:, n % 2, :], act_up[:, n % 2, :], 0.5, ps_u[n % 2][:, :], ALU.mult, ALU.mult).then_inc(mixed_up, 1)

        def store_half(act, i, k):
            act.wait_ge(S["out_ps"], i * HALVES + k + 1)
            act.wait_ge(stored[k], i * 16 + 16)
            act.activation(result[:, k, :], ps_o[k][:, :], ACT.Copy).then_inc(S["result_up"], 1)

        @block.scalar
        def _(act):
            act.sem_inc(S["result_up"], 1)
            for k in range(HALVES):
                act.sem_inc(stored[k], 16)
            with act.Fori(0, B) as i:
                for k in range(HALVES):
                    act.wait_ge(S["lnt_ps"], i * HALVES + k + 1)
                    act.activation(xt[:, 512 * k:512 * k + 512], ps_g[k][:, :], ACT.Copy).then_inc(S["xt_up"], 1)
                act.wait_ge(S["shift_up"], i + 1)
                act.activation(gate["probs"][:, :, :], gate["probs"][:, :, :], ACT.Exp).then_inc(S["exp_up"], 1)
                for n in range(STEPS):
                    k, unit = divmod(n, UNITS)
                    act.wait_ge(unit_ps, i * STEPS + n + 1)
                    if n >= 2:
                        act.wait_ge(mixed_up, i * STEPS + n - 1)
                    act.activation(act_up[:, n % 2, :], ps_g[n % 2][:, :], ACT.Silu).then_inc(silu_up, 1)
                    if n == UNITS:
                        store_half(act, i, 0)
                store_half(act, i, 1)

        @block.tensor
        def _(pe):
            pe.wait_ge(S["params_in"], 16 * len(params))
            with pe.Fori(0, B) as i:
                pe.wait_ge(S["ln_up"], i + 1)
                for k in range(HALVES):
                    for t in range(4):
                        last = pe.transpose(ps_g[k][:, 128 * t:128 * t + 128], xln[:, 4 * k + t, :], const["ident"])
                    last.then_inc(S["lnt_ps"], 1)
                pe.wait_ge(S["xt_up"], i * HALVES + HALVES)
                for t in range(NT):
                    last = pe.matmul(ps_u[0][:, E * t:E * t + E], xt[:, 128 * t:128 * t + 128], wr[:, :], start=True, stop=True)
                last.then_inc(S["gate_ps"], 1)
                pe.wait_ge(S["chosen_up"], i + 1)
                pe.matmul(ps_u[1][:, 0:NT * E], before[:, :], gate["chosen"][:, :, :].rearrange("p t e -> p (t e)"), start=True, stop=False)
                pe.matmul(ps_u[1][:, 0:NT * E], ones[:, :], chosen_before[:, 0:NT, :].rearrange("p t e -> p (t e)"), start=False, stop=True).then_inc(S["count_ps"], 1)
                pe.wait_ge(S["score_up"], i + 1)
                for k in range(HALVES):
                    for t in range(4):
                        last = pe.transpose(ps_g[k][0:E, 128 * t:128 * t + 128], gate["score"][:, 4 * k + t, :], const["ident"])
                    last.then_inc(S["st_ps"], 1)
                pe.wait_ge(S["st_up"], i * HALVES + HALVES)

                def down(n):
                    k, unit = divmod(n, UNITS)
                    if unit == 0:
                        if k == 0:
                            pe.wait_ge(S["result_up"], i * HALVES + 1)
                        for t in range(4):
                            pe.matmul(ps_o[k][:, 128 * t:128 * t + 128], tile_in[:, 4 * k + t, :], const["ident"],
                                      start=(t == 0), stop=False, skip_group_check=True)
                    pe.wait_ge(mixed_up, i * STEPS + n + 1)
                    last = pe.matmul(ps_o[k][:, :], wd[:, unit, :], mixed[:, n % 2, :], start=False, stop=(unit == UNITS - 1), skip_group_check=True)
                    if unit == UNITS - 1:
                        last.then_inc(S["out_ps"], 1)

                for n in range(STEPS):
                    k, unit = divmod(n, UNITS)
                    cols = slice(512 * k, 512 * k + 512)
                    if n >= 2:
                        pe.wait_ge(mixed_up, i * STEPS + n - 1)
                    if unit < PAIRS:
                        pe.matmul(ps_b[n % 2][:, :], pairsel[:, unit, :], score_t[:, cols], start=True, stop=True)
                    pe.matmul(ps_u[n % 2][:, :], wu[:, unit, :], xt[:, cols], start=True, stop=True)
                    pe.matmul(ps_g[n % 2][:, :], wg[:, unit, :], xt[:, cols], start=True, stop=True).then_inc(unit_ps, 1)
                    if n:
                        down(n - 1)
                down(STEPS - 1)


def program(nc, B, io, out):
    ctx = ExitStack()
    with ctx:
        def keep(name, shape, dt=F32):
            return ctx.enter_context(nc.sbuf_tensor(name, shape, dt))

        cap = {k[6:]: v for k, v in io.items() if k.startswith("const_")}
        const, const_in = {}, []
        for name in ("ident", "block16", "block4", "sumsel"):
            tile = keep("c_" + name, [128, 128])
            const[name] = tile[:, :]
            const_in.append((tile[:, :], cap[name]))
        gn2 = keep("gn2", [128, 2, B])
        x1_dram = nc.dram_tensor("x1_scratch", (B, C, N), F32).ap()
        split_dram = nc.dram_tensor("split_scratch", (2, 3, C, N), BF16).ap()
        band_dram = nc.dram_tensor("band_scratch", (BANDS, C, HW * BAND), F32).ap()
        u_stack = ExitStack()
        setup_phase(nc, ctx, io, const, const_in, band_dram)
        maps_stack = ExitStack()
        u_cols = u_stack.enter_context(nc.sbuf_tensor("u_cols", [128, B, 32, HW], F32))
        attention_phase(nc, ctx, B, io, const, u_cols, gn2, x1_dram, split_dram)
        maps = maps_stack.enter_context(nc.sbuf_tensor("maps", [128, B, 32, HW], F32))
        conv_phase(nc, ctx, B, io, u_cols, maps, band_dram)
        tokens = u_cols[:, :, :, :].rearrange("p b c h -> p b (c h)").rearrange("p b (t c) -> p b t c", t=NT)
        landmark_phase(nc, ctx, B, io, const, maps, gn2, x1_dram, tokens)
        maps_stack.close()
        gelu_experts_phase(nc, ctx, B, io, const, tokens)
        self_attention_phase(nc, ctx, B, io, const, tokens)
        silu_experts_phase(nc, ctx, B, io, const, tokens, out)
        u_stack.close()


_SHAPED = {
    "L0_qkvT": ("L0_conv_qkv_w", lambda a: a.T), "L0_projT": ("L0_conv_proj_w", lambda a: a.T),
    "L1_w3T": ("L1_conv_w3", lambda a: a[:, :, 0, 0].T),
    "L2_qkvT": ("L2_attn_Wqkv", lambda a: a.T), "L2_projT": ("L2_attn_Wproj", lambda a: a.T),
    "L2_ffn_Wg": ("L2_ffn_Wg", lambda a: a), "L2_ffn_W1": ("L2_ffn_W1", lambda a: a),
    "L2_ffn_W2": ("L2_ffn_W2", lambda a: a), "L2_ffn_b1": ("L2_ffn_b1", lambda a: a), "L2_ffn_b2": ("L2_ffn_b2", lambda a: a),
    "L3_attn_W": ("L3_attn_W", lambda a: a), "L3_routerT": ("L3_ffn_router_w", lambda a: a.T),
    "L3_sgT": ("L3_ffn_shared_w_gate", lambda a: a.reshape(-1, C).T), "L3_suT": ("L3_ffn_shared_w_up", lambda a: a.reshape(-1, C).T),
    "L3_sdT": ("L3_ffn_shared_w_down", lambda a: a.transpose(0, 2, 1).reshape(-1, C)),
    "L3_gT": ("L3_ffn_w_gate", lambda a: a.reshape(-1, C).T), "L3_uT": ("L3_ffn_w_up", lambda a: a.reshape(-1, C).T),
    "L3_dT": ("L3_ffn_w_down", lambda a: a.transpose(0, 2, 1).reshape(-1, C)),
}
_TAPS = ["L1_conv_w0"] + ["L1_conv_" + w for v, h, _ in KERNELS for w in (v, h)]
_COLUMNS = ["L0_conv_norm_w", "L0_conv_norm_b", "L0_conv_qkv_b", "L0_conv_proj_b", "L1_conv_b0", "L1_conv_b0_1", "L1_conv_b0_2",
            "L1_conv_b1_1", "L1_conv_b1_2", "L1_conv_b2_1", "L1_conv_b2_2", "L1_conv_b3", "L2_attn_bqkv", "L2_attn_bproj",
            "L3_attn_b", "L3_ffn_bias"]


def kernel(**inputs):
    import concourse.bacc as _bacc
    from concourse.bass_utils import run_bass_kernel_spmd as _run

    a = {k: np.asarray(v) for k, v in inputs.items()}
    B = a["x"].shape[0]
    host = {"x": a["x"].reshape(B, C, N)}
    host.update({k: f(a[n]) for k, (n, f) in _SHAPED.items()})
    host.update({n: a[n].reshape(C, -1)[:, ::-1] if n != "L1_conv_w0" else a[n].reshape(C, 5, 5)[:, :, ::-1].reshape(C, 25) for n in _TAPS})
    host.update({n: a[n].reshape(-1, 1) for n in _COLUMNS})
    host.update({"const_" + k: v for k, v in shape_constants().items()})
    nc = _bacc.Bacc("TRN2", target_bir_lowering=False, num_devices=1)
    arrays, io = {}, {}
    for k, v in host.items():
        v = np.ascontiguousarray(v)
        arrays[f"in_{k}_dram"] = v
        io[k] = nc.dram_tensor(f"in_{k}_dram", v.shape, mybir.dt.from_np(v.dtype), kind="ExternalInput").ap()
    out = nc.dram_tensor("out_0_dram", (B, C, N), F32, kind="ExternalOutput").ap()
    program(nc, B, io, out)
    r = _run(nc, [arrays], core_ids=[0])
    return r.results[0]["out_0_dram"].reshape(B, C, HW, HW)
```

```python
import concourse.bass as bass
from concourse import mybir
from concourse.alu_op_type import AluOpType as ALU
from contextlib import ExitStack
import numpy as np

F32 = mybir.dt.float32
BF16 = mybir.dt.bfloat16
I32 = mybir.dt.int32
ACT = mybir.ActivationFunctionType
AX = mybir.AxisListType

C = 128
HW = 32
N = HW * HW
NT = N // 128
HALVES = N // 512
HEADS = 8
D = C // HEADS
CQ = 4


def shape_constants():
    p = np.arange(128)
    f = np.float32
    m = {}
    m["ident"] = np.eye(128, dtype=f)
    m["block16"] = (p[:, None] // 16 == p[None, :] // 16).astype(f)
    m["block4"] = (p[:, None] // 4 == p[None, :] // 4).astype(f)
    m["sumsel"] = ((p[:, None] % 32 == 16) & (p[:, None] // 32 == p[None, :] // 32)).astype(f)
    m["before"] = (p[:, None] < p[None, :]).astype(f)
    m["ones"] = np.ones((128, 128), f)
    m["pairsel"] = np.stack([(np.arange(16)[:, None] == 2 * q + (p[None, :] // 64)) for q in range(8)], 1).astype(f).reshape(16, 1024)
    for e in (8, 16):
        r = np.arange(e)
        m[f"tie{e}"] = np.broadcast_to((r[None, :] < r[:, None]).astype(f).reshape(1, e * e), (128, e * e)).copy()
    return m


def rsqrt(dve, y, v, t):
    dve.tensor_scalar(y.bitcast(I32), v.bitcast(I32), -0.5, 1597463007.0, ALU.mult, ALU.add)
    for _ in range(4):
        dve.drain()
        dve.tensor_tensor(t, y, y, ALU.mult)
        dve.drain()
        dve.tensor_tensor(t, t, v, ALU.mult)
        dve.drain()
        dve.tensor_scalar(t, t, -0.5, 1.5, ALU.mult, ALU.add)
        dve.drain()
        last = dve.tensor_tensor(y, y, t, ALU.mult)
    dve.drain()
    return last


def channel_moments(dve, moments, stats, mv, x):
    for k in range(HALVES):
        dve.bn_stats(stats[:, k, :], x[:, 512 * k:512 * k + 512])
    dve.drain()
    dve.bn_aggr(mv[:, :], stats[:, :, :])
    dve.drain()
    dve.tensor_copy(moments[:, 0:1], mv[:, 0:1])
    return dve.scalar_tensor_tensor(moments[:, 1:2], mv[:, 0:1], mv[:, 0:1], mv[:, 1:2], ALU.mult, ALU.add)


def group_affine(dve, scale, shift, group, sums, width, small, eps):
    dve.tensor_scalar(group[:, :], sums, 1.0 / width, None, ALU.mult)
    dve.drain()
    dve.tensor_tensor(small[:, 0:1], group[:, 0:1], group[:, 0:1], ALU.mult)
    dve.drain()
    dve.tensor_tensor(small[:, 1:2], group[:, 1:2], small[:, 0:1], ALU.subtract)
    dve.drain()
    dve.tensor_scalar(small[:, 1:2], small[:, 1:2], 0.0, eps, ALU.max, ALU.add)
    dve.drain()
    rsqrt(dve, scale, small[:, 1:2], small[:, 2:3])
    dve.scalar_tensor_tensor(shift, group[:, 0:1], -1.0, scale, ALU.mult, ALU.mult)
    dve.drain()


def attention_phase(nc, ctx, B, io, const, u_cols, gn2, x1_dram, split_dram):
    with ExitStack() as st:
        def sb(name, shape, dt=F32):
            return st.enter_context(nc.sbuf_tensor("a_" + name, shape, dt))

        def sem(name):
            return ctx.enter_context(nc.semaphore("a_" + name))

        SLOTS = ((0, 0), (0, 1), (1, 0), (1, 1), (0, 2), (2, 0))
        KS = len(SLOTS) * D
        PIECES = 3
        x = sb("x", [128, N])
        xn = sb("xn", [128, N])
        full, rest = sb("full", [128, N]), sb("rest", [128, N])
        pieces = sb("pieces", [128, 2, PIECES, N], BF16)
        q_stack = sb("q_stack", [KS + PIECES, HEADS, N], BF16)
        k_stack = sb("k_stack", [KS + PIECES, HEADS, N], BF16)
        v_ones = sb("v_ones", [128, NT, HEADS, 32])
        probs = sb("probs", [128, 3, N])
        o_sums = sb("o_sums", [128, 2, N])
        o_inv = sb("o_inv", [128, 512])
        x1 = sb("x1", [128, N])
        u_tr = sb("u_tr", [128, 32, HW])
        wqkv = sb("wqkv", [128, 3 * C])
        wproj = sb("wproj", [128, 2, C])
        vbias = sb("vbias", [128, C])
        qbias, kbias, pbias = sb("qbias", [128, 1]), sb("kbias", [128, 1]), sb("pbias", [128, 1])
        nw, nb = sb("nw", [128, 1]), sb("nb", [128, 1])
        stats, mv = sb("stats", [128, HALVES, 6]), sb("mv", [128, 2])
        moments, group, small = sb("moments", [128, 2]), sb("group", [128, 2]), sb("small", [128, 4])
        gscale, gshift = sb("gscale", [128, 1]), sb("gshift", [128, 1])
        maxes = sb("maxes", [128, 2, NT, 2])
        negmax = sb("negmax", [128, 2, NT])
        shift32 = sb("shift32", [NT, 2, 128])
        shift3 = sb("shift3", [NT, 2, PIECES, 128], BF16)
        ps_a = st.enter_context(nc.psum_tensor("ps_a", [128, 2, 512], F32))
        ps_b = st.enter_context(nc.psum_tensor("ps_b", [128, 2, N], F32))
        ps_o = st.enter_context(nc.psum_tensor("ps_o", [128, N], F32))

        params_in, x_in, zeroed = sem("params_in"), sem("x_in"), sem("zeroed")
        moments_up, sums_up, xn_up = sem("moments_up"), sem("sums_up"), sem("xn_up")
        qk_ps, v_ps, split_up, v_up = sem("qk_ps"), sem("v_ps"), sem("split_up"), sem("v_up")
        split_stored, qk_stacked = [sem(f"split_stored{n}") for n in range(2)], sem("qk_stacked")
        shift_in = [sem(f"shift_in{n}") for n in range(2)]
        a_up, a_read, max_up, shift_up = sem("a_up"), sem("a_read"), sem("max_up"), sem("shift_up")
        b_up, b_exp, o_up, o_out = sem("b_up"), sem("b_exp"), sem("o_up"), sem("o_out")
        bc_up, on_up, proj_up, x1_up = sem("bc_up"), sem("on_up"), sem("proj_up"), sem("x1_up")
        moments2_up, sums2_up, ut_up = sem("moments2_up"), sem("sums2_up"), sem("ut_up")
        x1_stored, u_stored, x_free = sem("x1_stored"), sem("u_stored"), sem("x_free")

        ring = []
        for h in range(HEADS):
            ring += [("scores", h, g) for g in range(2)]
            if h:
                ring.append(("shift", h - 1, 0))
            ring += [("scores", h, g) for g in range(2, 2 * NT)]
        ring.append(("shift", HEADS - 1, 0))
        place = {item: n for n, item in enumerate(ring)}
        A_PER, B_PER = len(ring), HEADS * NT
        PARAMS = 16 * (7 + HEADS)
        SHIFTS = 16 * PIECES * HEADS // 2
        block = st.enter_context(nc.Block())

        @block.sync
        def _(sp):
            sp.wait_ge(zeroed, 1)
            for dst, src in ((wqkv[:, :], io["L0_qkvT"]), (qbias[:, :], io["L0_conv_qkv_b"][0:C, :]),
                             (kbias[:, :], io["L0_conv_qkv_b"][C:2 * C, :]), (pbias[:, :], io["L0_conv_proj_b"]),
                             (nw[:, :], io["L0_conv_norm_w"]), (nb[:, :], io["L0_conv_norm_b"]),
                             (vbias[:, :], io["L0_conv_qkv_b"][2 * C:3 * C, :].rearrange("c b -> b c").broadcast_to((128, C)))):
                sp.dma_start(dst, src).then_inc(params_in, 16)
            for h in range(HEADS):
                sp.dma_start(wproj[32 * (h % 4):32 * (h % 4) + D, h // 4, :],
                             io["L0_projT"][D * h:D * h + D, :]).then_inc(params_in, 16)
            with sp.Fori(0, B) as i:
                sp.wait_ge(x_free, i + 1)
                sp.dma_start(x[:, :], io["x"][bass.ds(i, 1), :, :].rearrange("a c n -> (a c) n")).then_inc(x_in, 16)
                for qk in range(2):
                    sp.wait_ge(split_up, i * 2 + qk + 1)
                    sp.dma_start(split_dram[qk, :, :, :].rearrange("s c n -> c s n"), pieces[:, qk, :, :]).then_inc(split_stored[qk], 16)
                for qk, stack in enumerate((q_stack, k_stack)):
                    sp.wait_ge(split_stored[qk], i * 16 + 16)
                    for s, slot in enumerate(SLOTS):
                        sp.dma_start(stack[D * s:D * s + D, :, :],
                                     split_dram[qk, slot[qk], :, :].rearrange("(h d) n -> d h n", d=D)).then_inc(qk_stacked, 16)
                for h in range(HEADS):
                    sp.wait_ge(shift_up, i * HEADS + h + 1)
                    for s in range(PIECES):
                        sp.dma_start(q_stack[KS + s:KS + s + 1, h, :].rearrange("s (t n) -> s t n", t=NT),
                                     shift3[:, h % 2, s, :]).then_inc(shift_in[h % 2], 16)
                sp.wait_ge(ut_up, i + 1)
                sp.dma_start(x1_dram[bass.ds(i, 1), :, :].rearrange("a c n -> (a c) n"), x1[:, :]).then_inc(x1_stored, 16)
                sp.dma_start(u_cols[:, bass.ds(i, 1), :, :].rearrange("p a c h -> p (a c h)"),
                             u_tr[:, :, :].rearrange("p c h -> p (c h)")).then_inc(u_stored, 16)
            sp.wait_ge(x1_stored, 16 * B + 16)
            sp.wait_ge(u_stored, 16 * B + 16)

        @block.gpsimd
        def _(pool):
            pool.memset(wproj[:, :, :], 0.0)
            pool.drain()
            pool.memset(k_stack[KS:KS + PIECES, :, :], 1.0)
            pool.drain()
            pool.memset(v_ones[:, :, :, :], 1.0)
            pool.drain().then_inc(zeroed, 1)

        @block.vector
        def _(dve):
            dve.wait_ge(params_in, PARAMS)
            dve.sem_inc(x_free, 1)
            dve.sem_inc(x1_stored, 16)
            dve.sem_inc(u_stored, 16)
            with dve.Fori(0, B) as i:
                dve.wait_ge(x_in, i * 16 + 16)
                channel_moments(dve, moments, stats, mv, x).then_inc(moments_up, 1)
                dve.wait_ge(sums_up, i + 1)
                group_affine(dve, gscale[:, :], gshift[:, :], group, ps_a[:, 0, 0:2], C // 8, small, 1e-5)
                dve.tensor_tensor(gscale[:, :], gscale[:, :], nw[:, :], ALU.mult)
                dve.tensor_tensor(gshift[:, :], gshift[:, :], nw[:, :], ALU.mult)
                dve.drain()
                dve.tensor_tensor(gshift[:, :], gshift[:, :], nb[:, :], ALU.add)
                dve.drain()
                dve.tensor_scalar(xn[:, :], x[:, :], gscale[:, :], gshift[:, :], ALU.mult, ALU.add).then_inc(xn_up, 1)
                for qk, bias in enumerate((qbias, kbias)):
                    dve.drain()
                    dve.wait_ge(qk_ps, i * 2 + qk + 1)
                    dve.tensor_scalar(full[:, :], ps_b[:, qk, :], bias[:, :], 1.0 if qk else 1.0 / D, ALU.add, ALU.mult)
                    dve.drain()
                    for s in range(PIECES):
                        src = full if s == 0 else rest
                        dve.tensor_copy(pieces[:, qk, s, :], src[:, :])
                        dve.drain()
                        if s < PIECES - 1:
                            dve.tensor_tensor(rest[:, :], src[:, :], pieces[:, qk, s, :], ALU.subtract)
                            dve.drain()
                    dve.drain().then_inc(split_up, 1)
                dve.wait_ge(v_ps, i + 1)
                for t in range(NT):
                    last = dve.tensor_tensor(v_ones[:, t, :, 0:D],
                                             ps_o[:, 128 * t:128 * t + 128].rearrange("p (h d) -> p h d", h=HEADS),
                                             vbias[:, :].rearrange("p (h d) -> p h d", h=HEADS), ALU.add)
                last.then_inc(v_up, 1)

                def take_output(h):
                    dve.wait_ge(o_up, i * HEADS + h + 1)
                    r = 32 * (h % 4)
                    dve.tensor_copy(o_sums[r:r + 32, h // 4, :], ps_o[r:r + 32, :]).then_inc(o_out, 1)

                for n, (what, h, g) in enumerate(ring):
                    dve.wait_ge(a_up, i * A_PER + n + 1)
                    if what == "scores":
                        dve.reduce_max(maxes[:, h % 2, g // 2, g % 2:g % 2 + 1], ps_a[:, n % 2, :], axis=AX.X).then_inc(a_read, 1)
                        if g == 2 * NT - 1:
                            dve.drain()
                            dve.tensor_reduce(negmax[:, h % 2, :], maxes[:, h % 2, :, :], axis=AX.X, op=ALU.max,
                                              negate=True).then_inc(max_up, 1)
                        if g == NT and h >= 3:
                            take_output(h - 3)
                    else:
                        if h >= 2:
                            dve.wait_ge(shift_in[h % 2], i * SHIFTS + 16 * PIECES * (h // 2))
                        dve.tensor_copy(shift32[:, h % 2, :], ps_a[0:NT, n % 2, 0:128]).then_inc(a_read, 1)
                        dve.drain()
                        for s in range(PIECES):
                            dve.tensor_copy(shift3[:, h % 2, s, :], shift32[:, h % 2, :])
                            dve.drain()
                            if s < PIECES - 1:
                                dve.tensor_tensor(shift32[:, h % 2, :], shift32[:, h % 2, :], shift3[:, h % 2, s, :], ALU.subtract)
                                dve.drain()
                        dve.drain().then_inc(shift_up, 1)
                for h in range(HEADS - 3, HEADS):
                    take_output(h)
                for n in range(4):
                    g, k = n // 2, n % 2
                    dve.wait_ge(bc_up, i * 4 + n + 1)
                    dve.reciprocal(o_inv[:, :], ps_b[:, g, 512 * k:512 * k + 512])
                    dve.drain()
                    part = o_sums[:, g, 512 * k:512 * k + 512]
                    dve.tensor_tensor(part, part, o_inv[:, :], ALU.mult)
                    dve.drain()
                dve.drain().then_inc(on_up, 1)
                dve.wait_ge(proj_up, i + 1)
                dve.wait_ge(x1_stored, i * 16 + 16)
                dve.wait_ge(u_stored, i * 16 + 16)
                dve.scalar_tensor_tensor(x1[:, :], ps_o[:, :], pbias[:, :], x[:, :], ALU.add, ALU.add).then_inc(x_free, 1)
                dve.drain()
                channel_moments(dve, moments, stats, mv, x1).then_inc(moments2_up, 1)
                dve.wait_ge(sums2_up, i + 1)
                group_affine(dve, gscale[:, :], gshift[:, :], group, ps_a[:, 0, 0:2], C // 32, small, 1e-5)
                dve.tensor_copy(gn2[:, 0, bass.ds(i, 1)], gscale[:, :])
                dve.tensor_copy(gn2[:, 1, bass.ds(i, 1)], gshift[:, :])
                dve.tensor_scalar(xn[:, :], x1[:, :], gscale[:, :], gshift[:, :], ALU.mult, ALU.add)
                dve.drain()
                dve.transpose(u_tr[:, :, :].rearrange("p c h -> p h c"), xn[:, :]).then_inc(ut_up, 1)
                dve.drain()

        @block.scalar
        def _(act):
            with act.Fori(0, B) as i:
                for m in range(B_PER):
                    act.wait_ge(b_up, i * B_PER + m + 1)
                    act.activation(probs[:, m % 3, :], ps_b[:, m % 2, :], ACT.Exp).then_inc(b_exp, 1)

        @block.tensor
        def _(pe):
            pe.wait_ge(params_in, PARAMS)
            with pe.Fori(0, B) as i:
                pe.wait_ge(moments_up, i + 1)
                pe.matmul(ps_a[:, 0, 0:2], const["block16"], moments[:, :], start=True, stop=True).then_inc(sums_up, 1)
                pe.wait_ge(xn_up, i + 1)
                for qk in range(2):
                    for k in range(HALVES):
                        last = pe.matmul(ps_b[:, qk, 512 * k:512 * k + 512], wqkv[:, C * qk:C * qk + C],
                                         xn[:, 512 * k:512 * k + 512], start=True, stop=True)
                    last.then_inc(qk_ps, 1)
                for t in range(NT):
                    last = pe.matmul(ps_o[:, 128 * t:128 * t + 128], xn[:, 128 * t:128 * t + 128], wqkv[:, 2 * C:3 * C],
                                     start=True, stop=True)
                last.then_inc(v_ps, 1)
                pe.wait_ge(qk_stacked, i * 32 * len(SLOTS) + 32 * len(SLOTS))

                def ring_item(n):
                    what, h, g = ring[n]
                    if n >= 2:
                        pe.wait_ge(a_read, i * A_PER + n - 1)
                    if what == "scores":
                        t, k = g // 2, g % 2
                        pe.matmul(ps_a[:, n % 2, :], q_stack[0:KS, h, 128 * t:128 * t + 128],
                                  k_stack[0:KS, h, 512 * k:512 * k + 512], start=True, stop=True).then_inc(a_up, 1)
                    else:
                        pe.wait_ge(max_up, i * HEADS + h + 1)
                        pe.transpose(ps_a[0:NT, n % 2, 0:128], negmax[:, h % 2, :], const["ident"]).then_inc(a_up, 1)

                def shifted_scores(m):
                    h, t = divmod(m, NT)
                    if t == 0:
                        pe.wait_ge(shift_in[h % 2], i * SHIFTS + 16 * PIECES * (h // 2 + 1))
                    if m >= 2:
                        pe.wait_ge(b_exp, i * B_PER + m - 1)
                    for k in range(HALVES):
                        last = pe.matmul(ps_b[:, m % 2, 512 * k:512 * k + 512], k_stack[:, h, 128 * t:128 * t + 128],
                                         q_stack[:, h, 512 * k:512 * k + 512], start=True, stop=True)
                    last.then_inc(b_up, 1)

                def weigh_values(m):
                    h, t = divmod(m, NT)
                    r = 32 * (h % 4)
                    if m == 0:
                        pe.wait_ge(v_up, i + 1)
                    if t == 0 and h >= 4:
                        pe.wait_ge(o_out, i * HEADS + h - 3)
                    pe.wait_ge(b_exp, i * B_PER + m + 1)
                    for k in range(HALVES):
                        last = pe.matmul(ps_o[r:r + 32, 512 * k:512 * k + 512], v_ones[:, t, h, :],
                                         probs[:, m % 3, 512 * k:512 * k + 512], start=(t == 0), stop=(t == NT - 1))
                    if t == NT - 1:
                        last.then_inc(o_up, 1)

                n = 0
                for step in range(HEADS + 2):
                    for t in range(NT):
                        upto = place[("scores", step, 2 * t + 1)] + 1 if step < HEADS else len(ring)
                        while n < upto:
                            ring_item(n)
                            n += 1
                        if step >= 2:
                            m = (step - 2) * NT + t
                            shifted_scores(m)
                            if m >= 1:
                                weigh_values(m - 1)
                weigh_values(B_PER - 1)
                pe.wait_ge(o_out, i * HEADS + HEADS)
                for g in range(2):
                    for k in range(HALVES):
                        pe.matmul(ps_b[:, g, 512 * k:512 * k + 512], const["sumsel"], o_sums[:, g, 512 * k:512 * k + 512],
                                  start=True, stop=True).then_inc(bc_up, 1)
                pe.wait_ge(on_up, i + 1)
                for k in range(HALVES):
                    for g in range(2):
                        last = pe.matmul(ps_o[:, 512 * k:512 * k + 512], wproj[:, g, :], o_sums[:, g, 512 * k:512 * k + 512],
                                         start=(g == 0), stop=(g == 1))
                last.then_inc(proj_up, 1)
                pe.wait_ge(moments2_up, i + 1)
                pe.matmul(ps_a[:, 0, 0:2], const["block4"], moments[:, :], start=True, stop=True).then_inc(sums2_up, 1)


KERNELS = (("w0_1", "w0_2", 7), ("w1_1", "w1_2", 11), ("w2_1", "w2_2", 21))
ROWS5 = 5
BANDS = ROWS5 + 2 * len(KERNELS)
BAND = 2 * HW - 1


def setup_phase(nc, ctx, io, const, const_in, band_dram):
    with ExitStack() as st:
        def sb(name, shape, dt=F32):
            return st.enter_context(nc.sbuf_tensor("s_" + name, shape, dt))

        def sem(name):
            return ctx.enter_context(nc.semaphore("s_" + name))

        taps5 = sb("taps_square", [128, ROWS5, 5])
        taps = [sb(f"taps{n}", [128, k]) for n, k in enumerate(k for _, _, k in KERNELS for _ in range(2))]
        row = sb("row", [128, BANDS, BAND])
        rows = sb("rows", [128, 2, HW, BAND])
        consts_in, taps_in, rows_up = sem("consts_in"), sem("taps_in"), sem("rows_up")
        rows_stored = [sem(f"rows_stored{n}") for n in range(2)]
        block = st.enter_context(nc.Block())

        @block.sync
        def _(sp):
            sp.dma_start(taps5[:, :, :], io["L1_conv_w0"].rearrange("c (a b) -> c a b", a=ROWS5)).then_inc(taps_in, 16)
            names = [w for v, h, _ in KERNELS for w in (v, h)]
            for tap, name in zip(taps, names):
                sp.dma_start(tap[:, :], io["L1_conv_" + name]).then_inc(taps_in, 16)
            for dst, src in const_in:
                sp.dma_start(dst, src).then_inc(consts_in, 16)
            for k in range(BANDS):
                sp.wait_ge(rows_up, k + 1)
                sp.dma_start(band_dram[k, :, :], rows[:, k % 2, :, :].rearrange("c a b -> c (a b)")).then_inc(rows_stored[k % 2], 16)
            for n in range(2):
                sp.wait_ge(rows_stored[n], 16 * ((BANDS + 1 - n) // 2))
            sp.wait_ge(consts_in, 16 * len(const_in))

        @block.vector
        def _(dve):
            dve.memset(row[:, :, :], 0.0)
            dve.wait_ge(taps_in, 16 * (1 + len(taps)))
            dve.drain()
            dve.tensor_copy(row[:, 0:ROWS5, HW - 3:HW + 2], taps5[:, :, :])
            for n, tap in enumerate(taps):
                half = 3 * (KERNELS[n // 2][2] // 2)
                dve.tensor_copy(row[:, ROWS5 + n, HW - 1 - half:HW + half:3], tap[:, :])
            dve.drain()
            for k in range(BANDS):
                if k >= 2:
                    dve.wait_ge(rows_stored[k % 2], 16 * (k // 2))
                dve.tensor_copy(rows[:, k % 2, :, :], row[:, k, :].unsqueeze(1).broadcast_to((128, HW, BAND))).then_inc(rows_up, 1)


def conv_phase(nc, ctx, B, io, u_cols, maps, band_dram):
    with ExitStack() as st:
        def sb(name, shape, dt=F32):
            return st.enter_context(nc.sbuf_tensor("c_" + name, shape, dt))

        def sem(name):
            return ctx.enter_context(nc.semaphore("c_" + name))

        K = len(KERNELS)
        L = B * HW
        bands = [sb(f"bands{n}", [128, BANDS, 128]) for n in range(2)]
        square = [sb(f"square{n}", [128, L]) for n in range(2)]
        square_t = [sb(f"square_t{n}", [128, L]) for n in range(2)]
        along = [sb(f"along{n}", [128, K, L]) for n in range(2)]
        along_t = [sb(f"along_t{n}", [128, K, L]) for n in range(2)]
        bias = sb("bias", [128, 1 + 2 * K, 32])
        last_bias = sb("last_bias", [128, 32])
        ps_s = [st.enter_context(nc.psum_tensor(f"c_ps_s{n}", [128, 512], F32)) for n in range(2)]
        ps_h = [st.enter_context(nc.psum_tensor(f"c_ps_h{n}", [128, K, 512], F32)) for n in range(2)]
        zeroed, bias_in, bands_in = sem("zeroed"), sem("bias_in"), [sem(f"bands_in{n}") for n in range(2)]
        square_ps, square_up, square_turned = sem("square_ps"), sem("square_up"), sem("square_turned")
        along_ps, along_up, turned = sem("along_ps"), sem("along_up"), sem("turned")
        maps_ps, maps_up = sem("maps_ps"), sem("maps_up")
        block = st.enter_context(nc.Block())
        names = ["L1_conv_b0"] + ["L1_conv_b" + v[1:] for v, _, _ in KERNELS] + ["L1_conv_b" + h[1:] for _, h, _ in KERNELS]

        @block.gpsimd
        def _(pool):
            for n in range(2):
                pool.memset(bands[n][:, :, :], 0.0)
                pool.drain()
            pool.drain().then_inc(zeroed, 1)

        @block.sync
        def _(sp):
            for n, name in enumerate(names):
                for q in range(CQ):
                    sp.dma_start(bias[HW * q:HW * q + HW, n, :],
                                 io[name][32 * q:32 * q + 32, :].rearrange("c b -> b c").broadcast_to((HW, 32))).then_inc(bias_in, 16)
            sp.wait_ge(zeroed, 1)
            with sp.Fori(0, 16) as j:
                c = j * 2
                for n in range(2):
                    sp.wait_ge(maps_ps, c + n + 1)
                    for q in range(CQ):
                        rows = band_dram[:, bass.ds(c + (32 * q + n), 1), HW - 1:HW - 1 + HW * (BAND - 1)]
                        sp.dma_start(bands[n][HW * q:HW * q + HW, :, HW * q:HW * q + HW],
                                     rows.rearrange("t a (w e) -> w t (a e)", e=BAND - 1)[:, :, 0:HW]).then_inc(bands_in[n], 16)

        @block.tensor
        def _(pe):
            pe.sem_inc(maps_ps, 2)
            with pe.Fori(0, 16) as j:
                c = j * 2
                for n in range(2):
                    pe.wait_ge(bands_in[n], c * 32 + 64)
                    pe.wait_ge(maps_up, c + n + 1)
                    out4 = ps_s[n][:, 0:L].rearrange("p (b h) -> p b h", b=B)
                    src = u_cols[:, :, bass.ds(c + n, 1), :].rearrange("p b a h -> p b (a h)")
                    for j, ky in enumerate((2, 0, 1, 3, 4)):
                        d = ky - 2
                        lo, hi = max(0, -d), min(HW, HW - d)
                        last = pe.matmul(out4[:, :, lo:hi], bands[n][:, ky, :], src[:, :, lo + d:hi + d],
                                         start=(j == 0), stop=(j == 4))
                    last.then_inc(square_ps, 1)
                for n in range(2):
                    pe.wait_ge(square_up, c + n + 1)
                    pe.wait_ge(along_up, c + n + 1)
                    for k in range(K):
                        last = pe.matmul(ps_h[n][:, k, 0:L], bands[n][:, ROWS5 + 2 * k, :], square[n][:, :], start=True, stop=True)
                    last.then_inc(along_ps, 1)
                for n in range(2):
                    pe.wait_ge(turned, c + n + 3)
                    for k in range(K):
                        last = pe.matmul(ps_s[n][:, 0:L], bands[n][:, ROWS5 + 2 * k + 1, :], along_t[n][:, k, :],
                                         start=(k == 0), stop=(k == K - 1))
                    last.then_inc(maps_ps, 1)

        @block.scalar
        def _(act):
            act.wait_ge(bias_in, 16 * CQ * len(names))
            act.sem_inc(along_up, 2)
            act.sem_inc(square_turned, 2)
            act.sem_inc(turned, 2)
            with act.Fori(0, 16) as j:
                c = j * 2
                for n in range(2):
                    act.wait_ge(square_ps, c + n + 1)
                    act.wait_ge(square_turned, c + n + 1)
                    act.activation(square[n][:, :], ps_s[n][:, 0:L], ACT.Identity, bias=bias[:, 0, bass.ds(c + n, 1)]).then_inc(square_up, 1)
                for n in range(2):
                    act.wait_ge(along_ps, c + n + 1)
                    act.wait_ge(turned, c + n + 1)
                    for k in range(K):
                        last = act.activation(along[n][:, k, :], ps_h[n][:, k, 0:L], ACT.Identity,
                                              bias=bias[:, 1 + k, bass.ds(c + n, 1)])
                    last.then_inc(along_up, 1)

        @block.vector
        def _(dve):
            dve.wait_ge(bias_in, 16 * CQ * len(names))
            dve.tensor_tensor(last_bias[:, :], bias[:, 1 + K, :], bias[:, 2 + K, :], ALU.add)
            dve.drain()
            dve.tensor_tensor(last_bias[:, :], last_bias[:, :], bias[:, 3 + K, :], ALU.add)
            dve.drain()
            dve.sem_inc(maps_up, 2)
            with dve.Fori(0, 16) as j:
                c = j * 2
                for n in range(2):
                    dve.wait_ge(square_up, c + n + 1)
                    dve.transpose(square_t[n][:, :], square[n][:, :]).then_inc(square_turned, 1)
                for n in range(2):
                    dve.wait_ge(along_up, c + n + 3)
                    dve.transpose(along_t[n][:, :, :].rearrange("p k l -> p (k l)"), along[n][:, :, :].rearrange("p k l -> p (k l)")).then_inc(turned, 1)
                for n in range(2):
                    dve.wait_ge(maps_ps, c + n + 3)
                    dve.scalar_tensor_tensor(square_t[n][:, :], ps_s[n][:, 0:L], last_bias[:, bass.ds(c + n, 1)], square_t[n][:, :],
                                             ALU.add, ALU.add)
                    dve.drain()
                    dve.tensor_copy(maps[:, :, bass.ds(c + n, 1), :].rearrange("p b a w -> p b (a w)"),
                                    square_t[n][:, :].rearrange("p (b w) -> p b w", b=B)).then_inc(maps_up, 1)
                    dve.drain()


def token_norm(dve, out, tile, stats, mv, var, inv, tmp):
    for t in range(NT):
        dve.bn_stats(stats[:, t, :], tile[:, t, :])
    dve.drain()
    for t in range(NT):
        dve.bn_aggr(mv[:, t, :], stats[:, t, :])
    dve.drain()
    dve.tensor_scalar(var[:, :], mv[:, :, 1], 1e-5, None, ALU.add)
    dve.drain()
    rsqrt(dve, inv[:, :], var[:, :], tmp[:, :])
    for t in range(NT):
        last = dve.tensor_scalar(out[:, t, :], tile[:, t, :], mv[:, t, 0:1], inv[:, t:t + 1], ALU.subtract, ALU.mult)
    return last


def turn_tiles(pe, out, tiles, ident):
    for t in range(NT):
        last = pe.transpose(out[:, 128 * t:128 * t + 128], tiles[:, t, :], ident)
    return last


def gate_tiles(st_sb, E):
    t = {n: st_sb("gate_" + n, [128, NT, E]) for n in ("logits", "probs", "rank", "chosen", "score")}
    t.update({n: st_sb("gate_" + n, [128, NT]) for n in ("top", "total", "picked")})
    t.update({n: st_sb("gate_" + n, [128, NT * E, E]) for n in ("above", "same")})
    return t


def gate_shift(dve, t, E):
    dve.tensor_reduce(t["top"][:, :], t["logits"][:, :, :], axis=AX.X, op=ALU.max)
    dve.drain()
    return dve.tensor_tensor(t["probs"][:, :, :], t["logits"][:, :, :], t["top"][:, :].unsqueeze(2).broadcast_to((128, NT, E)), ALU.subtract)


def gate_choose(dve, t, E, K, eps, tie):
    p, rank, chosen = t["probs"], t["rank"], t["chosen"]
    other = p[:, :, :].unsqueeze(2).broadcast_to((128, NT, E, E))
    own = p[:, :, :].unsqueeze(3).broadcast_to((128, NT, E, E))
    above = t["above"][:, :, :].rearrange("p (t e) f -> p t e f", t=NT)
    same = t["same"][:, :, :].rearrange("p (t e) f -> p t e f", t=NT)
    dve.tensor_tensor(above, other, own, ALU.is_gt)
    dve.tensor_tensor(same, other, own, ALU.is_equal)
    dve.tensor_reduce(t["total"][:, :], p[:, :, :], axis=AX.X, op=ALU.add)
    dve.drain()
    flat = t["same"][:, :, :].rearrange("p (t e) f -> p t (e f)", t=NT)
    dve.tensor_tensor(flat, flat, tie.unsqueeze(1).broadcast_to((128, NT, E * E)), ALU.mult)
    dve.drain()
    dve.tensor_tensor(t["above"][:, :, :], t["above"][:, :, :], t["same"][:, :, :], ALU.add)
    dve.drain()
    dve.tensor_reduce(rank[:, :, :], above, axis=AX.X, op=ALU.add)
    dve.drain()
    dve.tensor_scalar(chosen[:, :, :], rank[:, :, :], float(K), None, ALU.is_lt)
    dve.drain()
    dve.tensor_tensor(t["score"][:, :, :], p[:, :, :], chosen[:, :, :], ALU.mult)
    dve.drain()
    dve.tensor_reduce(t["picked"][:, :], t["score"][:, :, :], axis=AX.X, op=ALU.add)
    dve.drain()
    dve.scalar_tensor_tensor(t["picked"][:, :], t["total"][:, :], eps, t["picked"][:, :], ALU.mult, ALU.add)
    dve.drain()
    dve.reciprocal(t["picked"][:, :], t["picked"][:, :])
    dve.drain()
    return dve.tensor_tensor(t["score"][:, :, :], t["score"][:, :, :], t["picked"][:, :].unsqueeze(2).broadcast_to((128, NT, E)), ALU.mult)


def landmark_and_gelu_phase(nc, ctx, B, io, const, maps, gn2, x1_dram, tok_dram):
    with ExitStack() as st:
        def sb(name, shape, dt=F32):
            return st.enter_context(nc.sbuf_tensor("n_" + name, shape, dt))

        def sem(name):
            return ctx.enter_context(nc.semaphore("n_" + name))

        LM = 16
        STEP = N // LM
        NEWTON = 6
        SCALE = float(D) ** -0.5
        E, K, F = 8, 2, 512
        FT = F // 128
        SLOTS = 8 * (E + 1)
        LATE = SLOTS
        y_in, yt = sb("y_in", [128, 32, HW]), sb("yt", [128, N])
        x1, u = sb("x1", [128, N]), sb("u", [128, N])
        w3, wqkv, wproj = sb("w3", [128, C]), sb("wqkv", [128, 3 * C]), sb("wproj", [128, C])
        b3, qb, kb = sb("b3", [128, 1]), sb("qb", [128, 1]), sb("kb", [128, 1])
        vb, pb = sb("vb", [128, C]), sb("pb", [128, C])
        tok_next, tok = sb("tok_next", [128, NT, C]), sb("tok", [128, NT, C])
        xln = sb("xln", [128, NT, C])
        xt, qt, kt = sb("xt", [128, N]), sb("qt", [128, N]), sb("kt", [128, N])
        v = sb("v", [128, NT, C])
        q_lm, k_lm = sb("q_lm", [128, C]), sb("k_lm", [128, C])
        k1, e3 = sb("k1", [128, NT, C]), sb("e3", [128, NT, 128])
        k1t, e3t = yt, u
        max1, sum1 = sb("max1", [128, NT * HEADS]), sb("sum1", [128, NT * HEADS])
        max3, sum3 = sb("max3", [128, 1]), sb("sum3", [128, 1])
        max2, sum2, e2, e2q = sb("max2", [128, 1]), sb("sum2", [128, 1]), sb("e2", [128, LM]), sb("e2q", [128, LM])
        fro = sb("fro", [128, 1])
        m2, m2t = sb("m2", [128, 128]), sb("m2t", [128, 128])
        z, zt, mz = sb("z", [128, 128]), sb("zt", [128, 128]), sb("mz", [128, 128])
        kv, mixed, mixed_p = sb("kv", [128, 128]), sb("mixed", [128, 128]), sb("mixed_p", [128, 128])
        stats, mv = sb("stats", [128, NT, 6]), sb("mv", [128, NT, 2])
        var, inv, tmp = sb("var", [128, NT]), sb("inv", [128, NT]), sb("tmp", [128, NT])
        gate = gate_tiles(sb, E)
        score_t = sb("score_t", [E, N])
        xt_now, score_now = sb("xt_now", [128, N]), sb("score_now", [128, NT, E])
        hidden = sb("hidden", [128, 2, FT, N])
        wg, w1, w2 = sb("wg", [128, E]), sb("w1", [128, E, F]), sb("w2", [128, E, FT, C])
        b1, b2, tie = sb("b1", [128, E, FT]), sb("b2", [E, C]), sb("tie", [128, E * E])
        ps_h = [st.enter_context(nc.psum_tensor(f"n_ps_h{n}", [128, 512], F32)) for n in range(2)]
        ps_y = [st.enter_context(nc.psum_tensor(f"n_ps_y{n}", [128, 512], F32)) for n in range(2)]
        pa, pb_ = [st.enter_context(nc.psum_tensor(f"n_ps_f{n}", [128, N], F32)) for n in range(2)]
        events = ("x1_in y_in y_turned gate_ps x2_up tok_ps tok_up ln_up lnt_ps xt_up q_ps k_ps v_ps q_up k_up v_up lm_up "
                  "s2_ps s1_ps s3_ps d2_up e2_up m2_up m2t_ps fro_in fro_ps z0_up d1_up e1_up k1_up k1t_ps k1t_up max3_up e3_up e3t_ps e3t_up "
                  "kv_ps kv_up mixed_ps mixed_up mixp_ps mixp_up attn_ps attn_up ln2_up ln2t_ps xt2_up router_ps shift_up exp_up score_up "
                  "st_ps st_up b2_ps handed tok_done tok_stored")
        S = {name: sem(name) for name in events.split()}
        mz_ps, mz_up, znew_ps, z_up = sem("mz_ps"), sem("mz_up"), sem("znew_ps"), sem("z_up")
        params_in, hidden_ps, hidden_up, y_ps, y_added = sem("params_in"), sem("hidden_ps"), sem("hidden_up"), sem("y_ps"), sem("y_added")
        row = lambda ap, n: ap.rearrange("c b -> b c").broadcast_to((128, n))
        params = [(w3[:, :], io["L1_w3T"]), (wqkv[:, :], io["L2_qkvT"]), (wproj[:, :], io["L2_projT"]), (b3[:, :], io["L1_conv_b3"]),
                  (qb[:, :], io["L2_attn_bqkv"][0:C, :]), (kb[:, :], io["L2_attn_bqkv"][C:2 * C, :]),
                  (vb[:, :], row(io["L2_attn_bqkv"][2 * C:3 * C, :], C)), (pb[:, :], row(io["L2_attn_bproj"], C)),
                  (wg[:, :], io["L2_ffn_Wg"]), (w1[:, :, :], io["L2_ffn_W1"].rearrange("e d f -> d e f")),
                  (b2[:, :], io["L2_ffn_b2"]), (tie[:, :], io["const_tie8"])]
        params += [(w2[:, e, :, :], io["L2_ffn_W2"][e, :, :].rearrange("(t f) d -> f t d", t=FT)) for e in range(E)]
        params += [(b1[:, e, t:t + 1], io["L2_ffn_b1"][e:e + 1, 128 * t:128 * t + 128].rearrange("e f -> f e")) for e in range(E) for t in range(FT)]
        H_PER, Y_PER = 8 * E, 2 * E
        block = st.enter_context(nc.Block())

        def due(front, slot):
            while front and front[1] <= slot:
                front[1] = next(front[0], LATE + 1)

        @block.sync
        def _(sp):
            for dst, src in params:
                sp.dma_start(dst, src).then_inc(params_in, 16)

            def load(i):
                sp.dma_start(y_in[:, :, :].rearrange("p c w -> p (c w)"), maps[:, bass.ds(i, 1), :, :].rearrange("p a c w -> p (a c w)")).then_inc(S["y_in"], 16)
                sp.dma_start(x1[:, :], x1_dram[bass.ds(i, 1), :, :].rearrange("a c n -> (a c) n")).then_inc(S["x1_in"], 16)

            def store(i):
                sp.wait_ge(S["tok_done"], i + 1)
                sp.dma_start(tok_dram[bass.ds(i, 1), :, :].rearrange("a p n -> (a p) n"), tok[:, :, :].rearrange("p t c -> p (t c)")).then_inc(S["tok_stored"], 16)

            load(0)
            with sp.Fori(0, B - 1) as i:
                sp.wait_ge(S["x2_up"], i + 1)
                load(i + 1)
                store(i)
            store(B - 1)
            sp.wait_ge(S["tok_stored"], 16 * B + 16)

        @block.vector
        def _(dve):
            b16 = const["block16"].rearrange("p (h l) -> p h l", h=HEADS)

            def front(i):
                yield 0
                dve.wait_ge(S["y_in"], i * 16 + 16)
                dve.transpose(yt[:, :].rearrange("p (h w) -> p w h", h=HW), y_in[:, :, :].rearrange("p c w -> p w c")).then_inc(S["y_turned"], 1)
                dve.wait_ge(S["x1_in"], i * 16 + 16)
                dve.tensor_scalar(u[:, :], x1[:, :], gn2[:, 0, bass.ds(i, 1)], gn2[:, 1, bass.ds(i, 1)], ALU.mult, ALU.add)
                yield 4
                dve.drain()
                dve.wait_ge(S["gate_ps"], i + 1)
                dve.scalar_tensor_tensor(u[:, :], pa[:, :], b3[:, :], u[:, :], ALU.add, ALU.mult)
                dve.drain()
                dve.tensor_tensor(u[:, :], u[:, :], x1[:, :], ALU.add).then_inc(S["x2_up"], 1)
                yield 9
                dve.wait_ge(S["tok_up"], i + 1)
                token_norm(dve, xln, tok_next, stats, mv, var, inv, tmp).then_inc(S["ln_up"], 1)
                yield 20
                for src, dst, up in ((qt, q_lm, "q_up"), (kt, k_lm, "k_up")):
                    dve.wait_ge(S[up], i + 1)
                    last = dve.tensor_tensor(dst[:, :].rearrange("p (h l) -> p h l", h=HEADS), b16,
                                             src[:, 0:N:STEP].unsqueeze(1).broadcast_to((128, HEADS, LM)), ALU.mult)
                last.then_inc(S["lm_up"], 1)
                yield 21
                dve.wait_ge(S["v_ps"], i + 1)
                dve.tensor_tensor(v[:, :, :], pb_[:, :].rearrange("p (t c) -> p t c", t=NT),
                                  vb[:, :].unsqueeze(1).broadcast_to((128, NT, C)), ALU.add).then_inc(S["v_up"], 1)
                yield 23
                dve.wait_ge(S["s2_ps"], i + 1)
                dve.tensor_reduce(max2[:, :], pa[:, 0:LM], axis=AX.X, op=ALU.max)
                dve.drain()
                dve.tensor_scalar(e2[:, :], pa[:, 0:LM], max2[:, :], None, ALU.subtract).then_inc(S["d2_up"], 1)
                yield 25
                s1 = pb_[:, :].rearrange("p (g l) -> p g l", l=LM)
                k1v = k1[:, :, :].rearrange("p t (h l) -> p (t h) l", l=LM)
                dve.wait_ge(S["s1_ps"], i + 1)
                dve.tensor_reduce(max1[:, :], s1, axis=AX.X, op=ALU.max)
                dve.drain()
                dve.tensor_tensor(k1v, s1, max1[:, :].unsqueeze(2).broadcast_to((128, NT * HEADS, LM)), ALU.subtract).then_inc(S["d1_up"], 1)
                yield 27
                dve.wait_ge(S["e2_up"], i + 1)
                dve.reciprocal(sum2[:, :], sum2[:, :])
                dve.drain()
                dve.tensor_scalar(e2[:, :], e2[:, :], sum2[:, :], None, ALU.mult)
                dve.drain()
                dve.tensor_tensor(m2[:, :].rearrange("p (h l) -> p h l", h=HEADS), b16,
                                  e2[:, :].unsqueeze(1).broadcast_to((128, HEADS, LM)), ALU.mult).then_inc(S["m2_up"], 1)
                dve.tensor_tensor(e2q[:, :], e2[:, :], e2[:, :], ALU.mult)
                dve.drain()
                dve.tensor_reduce(max2[:, :], e2q[:, :], axis=AX.X, op=ALU.add).then_inc(S["fro_in"], 1)
                yield 29
                dve.wait_ge(S["fro_ps"], i + 1)
                dve.wait_ge(S["m2t_ps"], i + 1)
                dve.tensor_scalar(fro[:, :], pa[:, 0:1], 1e-12, None, ALU.max)
                dve.tensor_copy(m2t[:, :], pa[:, 512:640])
                dve.drain()
                dve.reciprocal(fro[:, :], fro[:, :])
                dve.drain()
                dve.tensor_scalar(z[:, :], m2t[:, :], fro[:, :], None, ALU.mult)
                dve.tensor_scalar(zt[:, :], m2[:, :], fro[:, :], None, ALU.mult).then_inc(S["z0_up"], 1)
                for it in range(NEWTON):
                    yield 30 + 2 * it
                    dve.drain()
                    dve.wait_ge(mz_ps, i * NEWTON + it + 1)
                    dve.tensor_copy(mz[:, :], pa[:, 0:128]).then_inc(mz_up, 1)
                    yield 31 + 2 * it
                    dve.wait_ge(znew_ps, i * NEWTON + it + 1)
                    dve.scalar_tensor_tensor(z[:, :], z[:, :], 2.0, pa[:, 512:640], ALU.mult, ALU.subtract)
                    dve.scalar_tensor_tensor(zt[:, :], zt[:, :], 2.0, pa[:, 640:768], ALU.mult, ALU.subtract).then_inc(z_up, 1)
                    dve.drain()
                    if it == 1:
                        dve.wait_ge(S["s3_ps"], i + 1)
                        dve.tensor_reduce(max3[:, :], pb_[:, :], axis=AX.X, op=ALU.max)
                        dve.drain()
                        dve.tensor_scalar(max3[:, :], max3[:, :], -SCALE, None, ALU.mult).then_inc(S["max3_up"], 1)
                    if it == 2:
                        dve.wait_ge(S["e1_up"], i + 1)
                        dve.tensor_reduce(sum1[:, :], k1v, axis=AX.X, op=ALU.add)
                        dve.drain()
                        dve.reciprocal(sum1[:, :], sum1[:, :])
                        dve.drain()
                        dve.tensor_tensor(k1v, k1v, sum1[:, :].unsqueeze(2).broadcast_to((128, NT * HEADS, LM)), ALU.mult).then_inc(S["k1_up"], 1)
                yield 43
                dve.wait_ge(S["e3_up"], i + 1)
                dve.reciprocal(sum3[:, :], sum3[:, :])
                dve.drain()
                dve.wait_ge(S["kv_ps"], i + 1)
                dve.scalar_tensor_tensor(kv[:, :], pb_[:, 0:128], sum3[:, :], const["block16"], ALU.mult, ALU.mult).then_inc(S["kv_up"], 1)
                yield 45
                dve.wait_ge(S["mixed_ps"], i + 1)
                dve.tensor_copy(mixed[:, :], pa[:, 0:128]).then_inc(S["mixed_up"], 1)
                dve.tensor_tensor(tok_next[:, :, :], tok_next[:, :, :], pb[:, :].unsqueeze(1).broadcast_to((128, NT, C)), ALU.add)
                yield 47
                dve.drain()
                dve.wait_ge(S["mixp_ps"], i + 1)
                dve.tensor_copy(mixed_p[:, :], pa[:, 512:640]).then_inc(S["mixp_up"], 1)
                yield 49
                dve.wait_ge(S["attn_ps"], i + 1)
                dve.tensor_tensor(tok_next[:, :, :], tok_next[:, :, :], pb_[:, :].rearrange("p (t c) -> p t c", t=NT), ALU.add).then_inc(S["attn_up"], 1)
                dve.drain()
                token_norm(dve, xln, tok_next, stats, mv, var, inv, tmp).then_inc(S["ln2_up"], 1)
                yield 58
                dve.wait_ge(S["router_ps"], i + 1)
                dve.tensor_copy(gate["logits"][:, :, :], pb_[:, 0:NT * E].rearrange("p (t e) -> p t e", t=NT))
                dve.drain()
                gate_shift(dve, gate, E).then_inc(S["shift_up"], 1)
                yield 60
                dve.wait_ge(S["exp_up"], i + 1)
                gate_choose(dve, gate, E, K, 1e-6, tie[:, :]).then_inc(S["score_up"], 1)
                yield 66
                dve.wait_ge(S["st_ps"], i + 1)
                dve.tensor_copy(score_t[:, :], pa[0:E, :]).then_inc(S["st_up"], 1)
                yield 69
                dve.drain()
                dve.wait_ge(S["b2_ps"], i + 1)
                dve.tensor_tensor(tok_next[:, :, :], tok_next[:, :, :], pb_[:, :].rearrange("p (t c) -> p t c", t=NT), ALU.add)

            def hand_over(i):
                dve.tensor_copy(xt_now[:, :], xt[:, :]).then_inc(S["handed"], 1)
                dve.drain()
                dve.tensor_copy(score_now[:, :, :], gate["score"][:, :, :])
                dve.wait_ge(S["tok_stored"], i * 16 + 16)
                dve.tensor_copy(tok[:, :, :], tok_next[:, :, :])
                dve.drain()

            def experts(i, front):
                for slot in range(SLOTS):
                    if slot >= 8 and slot % 4 == 3:
                        e, k = slot // 8 - 1, slot // 4 % 2
                        dve.wait_ge(y_ps, i * Y_PER + 2 * e + k + 1)
                        for t in range(4):
                            tile = tok[:, 4 * k + t, :]
                            last = dve.scalar_tensor_tensor(tile, ps_y[k][:, 128 * t:128 * t + 128], score_now[:, 4 * k + t, e:e + 1], tile,
                                                            ALU.mult, ALU.add)
                        last.then_inc(y_added, 1)
                        dve.drain()
                    due(front, slot)
                due(front, LATE)
                dve.drain().then_inc(S["tok_done"], 1)

            dve.wait_ge(params_in, 16 * len(params))
            dve.sem_inc(S["tok_stored"], 16)
            due([front(0), -1], LATE)
            dve.drain()
            hand_over(0)
            with dve.Fori(0, B - 1) as i:
                experts(i, [front(i + 1), -1])
                hand_over(i + 1)
            experts(B - 1, None)

        @block.scalar
        def _(act):
            def front(i):
                yield 8
                act.wait_ge(S["tok_ps"], i + 1)
                act.activation(tok_next[:, :, :].rearrange("p t c -> p (t c)"), pb_[:, :], ACT.Copy).then_inc(S["tok_up"], 1)
                yield 15
                act.wait_ge(S["lnt_ps"], i + 1)
                act.activation(xt[:, :], pa[:, :], ACT.Copy).then_inc(S["xt_up"], 1)
                yield 18
                act.wait_ge(S["q_ps"], i + 1)
                act.activation(qt[:, :], pb_[:, :], ACT.Identity, bias=qb[:, :]).then_inc(S["q_up"], 1)
                yield 19
                act.wait_ge(S["k_ps"], i + 1)
                act.activation(kt[:, :], pa[:, :], ACT.Identity, bias=kb[:, :]).then_inc(S["k_up"], 1)
                yield 26
                act.wait_ge(S["d2_up"], i + 1)
                act.activation(e2[:, :], e2[:, :], ACT.Exp, scale=SCALE, accum_out=sum2[:, :]).then_inc(S["e2_up"], 1)
                act.wait_ge(S["d1_up"], i + 1)
                act.activation(k1[:, :, :], k1[:, :, :], ACT.Exp, scale=SCALE).then_inc(S["e1_up"], 1)
                yield 35
                act.wait_ge(S["max3_up"], i + 1)
                act.activation(e3[:, :, :].rearrange("p t n -> p (t n)"), pb_[:, :], ACT.Exp, scale=SCALE, bias=max3[:, :], accum_out=sum3[:, :]).then_inc(S["e3_up"], 1)
                yield 37
                act.wait_ge(S["k1t_ps"], i + 1)
                act.activation(k1t[:, :], pb_[:, :], ACT.Copy).then_inc(S["k1t_up"], 1)
                yield 40
                act.wait_ge(S["e3t_ps"], i + 1)
                act.activation(e3t[:, :], pb_[:, :], ACT.Copy).then_inc(S["e3t_up"], 1)
                yield 55
                act.wait_ge(S["ln2t_ps"], i + 1)
                act.activation(xt[:, :], pa[:, :], ACT.Copy).then_inc(S["xt2_up"], 1)
                yield 59
                act.wait_ge(S["shift_up"], i + 1)
                act.activation(gate["probs"][:, :, :], gate["probs"][:, :, :], ACT.Exp).then_inc(S["exp_up"], 1)

            def experts(i, front):
                for slot in range(SLOTS):
                    if slot < H_PER:
                        e, k, f = slot // 8, slot // 4 % 2, slot % 4
                        act.wait_ge(hidden_ps, i * H_PER + slot + 1)
                        act.activation(hidden[:, e % 2, f, 512 * k:512 * k + 512], ps_h[slot % 2][:, :], ACT.Gelu, bias=b1[:, e, f:f + 1]).then_inc(hidden_up, 1)
                    due(front, slot)
                due(front, LATE)

            act.wait_ge(params_in, 16 * len(params))
            due([front(0), -1], LATE)
            with act.Fori(0, B - 1) as i:
                experts(i, [front(i + 1), -1])
            experts(B - 1, None)

        @block.tensor
        def _(pe):
            ident = const["ident"]

            def wide(out, w, src):
                for k in range(HALVES):
                    last = pe.matmul(out[:, 512 * k:512 * k + 512], w, src[:, 512 * k:512 * k + 512], start=True, stop=True)
                return last

            def front(i):
                yield 2
                pe.wait_ge(S["y_turned"], i + 1)
                wide(pa, w3[:, :], yt).then_inc(S["gate_ps"], 1)
                yield 7
                pe.wait_ge(S["x2_up"], i + 1)
                for t in range(NT):
                    last = pe.transpose(pb_[:, 128 * t:128 * t + 128], u[:, 128 * t:128 * t + 128], ident)
                last.then_inc(S["tok_ps"], 1)
                yield 14
                pe.wait_ge(S["ln_up"], i + 1)
                turn_tiles(pe, pa, xln, ident).then_inc(S["lnt_ps"], 1)
                yield 16
                pe.wait_ge(S["xt_up"], i + 1)
                wide(pb_, wqkv[:, 0:C], xt).then_inc(S["q_ps"], 1)
                yield 17
                wide(pa, wqkv[:, C:2 * C], xt).then_inc(S["k_ps"], 1)
                yield 19
                pe.wait_ge(S["q_up"], i + 1)
                for t in range(NT):
                    last = pe.matmul(pb_[:, 128 * t:128 * t + 128], xt[:, 128 * t:128 * t + 128], wqkv[:, 2 * C:3 * C], start=True, stop=True)
                last.then_inc(S["v_ps"], 1)
                yield 22
                pe.wait_ge(S["lm_up"], i + 1)
                pe.matmul(pa[:, 0:LM], q_lm[:, :], kt[:, 0:N:STEP], start=True, stop=True).then_inc(S["s2_ps"], 1)
                yield 24
                pe.wait_ge(S["v_up"], i + 1)
                for t in range(NT):
                    last = pe.matmul(pb_[:, 128 * t:128 * t + 128], qt[:, 128 * t:128 * t + 128], k_lm[:, :], start=True, stop=True)
                last.then_inc(S["s1_ps"], 1)
                yield 28
                pe.wait_ge(S["m2_up"], i + 1)
                pe.transpose(pa[:, 512:640], m2[:, :], ident).then_inc(S["m2t_ps"], 1)
                pe.wait_ge(S["fro_in"], i + 1)
                pe.matmul(pa[:, 0:1], const["block16"], max2[:, :], start=True, stop=True).then_inc(S["fro_ps"], 1)
                for it in range(NEWTON):
                    yield 30 + 2 * it
                    if it == 0:
                        pe.wait_ge(S["z0_up"], i + 1)
                    else:
                        pe.wait_ge(z_up, i * NEWTON + it)
                    pe.matmul(pa[:, 0:128], m2t[:, :], z[:, :], start=True, stop=True).then_inc(mz_ps, 1)
                    yield 31 + 2 * it
                    pe.wait_ge(mz_up, i * NEWTON + it + 1)
                    pe.matmul(pa[:, 512:640], zt[:, :], mz[:, :], start=True, stop=True)
                    pe.matmul(pa[:, 640:768], mz[:, :], zt[:, :], start=True, stop=True).then_inc(znew_ps, 1)
                    if it == 0:
                        pe.wait_ge(S["d1_up"], i + 1)
                        wide(pb_, q_lm[:, :], kt).then_inc(S["s3_ps"], 1)
                    if it == 3:
                        pe.wait_ge(S["e3_up"], i + 1)
                        pe.wait_ge(S["k1_up"], i + 1)
                        turn_tiles(pe, pb_, k1, ident).then_inc(S["k1t_ps"], 1)
                    if it == 4:
                        pe.wait_ge(S["k1t_up"], i + 1)
                        turn_tiles(pe, pb_, e3, ident).then_inc(S["e3t_ps"], 1)
                yield 42
                pe.wait_ge(S["e3t_up"], i + 1)
                for t in range(NT):
                    last = pe.matmul(pb_[:, 0:128], e3t[:, 128 * t:128 * t + 128], v[:, t, :], start=(t == 0), stop=(t == NT - 1))
                last.then_inc(S["kv_ps"], 1)
                yield 44
                pe.wait_ge(z_up, i * NEWTON + NEWTON)
                pe.wait_ge(S["kv_up"], i + 1)
                pe.matmul(pa[:, 0:128], kv[:, :], zt[:, :], start=True, stop=True).then_inc(S["mixed_ps"], 1)
                yield 46
                pe.wait_ge(S["mixed_up"], i + 1)
                pe.matmul(pa[:, 512:640], mixed[:, :], wproj[:, :], start=True, stop=True).then_inc(S["mixp_ps"], 1)
                yield 48
                pe.wait_ge(S["mixp_up"], i + 1)
                for t in range(NT):
                    last = pe.matmul(pb_[:, 128 * t:128 * t + 128], k1t[:, 128 * t:128 * t + 128], mixed_p[:, :], start=True, stop=True)
                last.then_inc(S["attn_ps"], 1)
                yield 54
                pe.wait_ge(S["ln2_up"], i + 1)
                turn_tiles(pe, pa, xln, ident).then_inc(S["ln2t_ps"], 1)
                yield 57
                pe.wait_ge(S["xt2_up"], i + 1)
                for t in range(NT):
                    last = pe.matmul(pb_[:, E * t:E * t + E], xt[:, 128 * t:128 * t + 128], wg[:, :], start=True, stop=True)
                last.then_inc(S["router_ps"], 1)
                yield 65
                pe.wait_ge(S["score_up"], i + 1)
                for t in range(NT):
                    last = pe.transpose(pa[0:E, 128 * t:128 * t + 128], gate["score"][:, t, :], ident)
                last.then_inc(S["st_ps"], 1)
                yield 68
                pe.wait_ge(S["st_up"], i + 1)
                for t in range(NT):
                    last = pe.matmul(pb_[:, 128 * t:128 * t + 128], score_t[:, 128 * t:128 * t + 128], b2[:, :], start=True, stop=True)
                last.then_inc(S["b2_ps"], 1)

            def experts(i, front):
                pe.wait_ge(S["handed"], i + 1)
                for slot in range(SLOTS):
                    e, k, f = slot // 8, slot // 4 % 2, slot % 4
                    if slot < H_PER:
                        if slot >= 2:
                            pe.wait_ge(hidden_up, i * H_PER + slot - 1)
                        pe.matmul(ps_h[slot % 2][:, :], w1[:, e, 128 * f:128 * f + 128], xt_now[:, 512 * k:512 * k + 512],
                                  start=True, stop=True).then_inc(hidden_ps, 1)
                    if slot >= 8:
                        e, t = e - 1, slot % 8
                        if t == 0 or t == 4:
                            pe.wait_ge(hidden_up, i * H_PER + 8 * e + 4 + t)
                            if e:
                                pe.wait_ge(y_added, i * Y_PER + 2 * (e - 1) + k + 1)
                        for f in range(FT):
                            last = pe.matmul(ps_y[k][:, 128 * f_col(t):128 * f_col(t) + 128], hidden[:, e % 2, f, 128 * t:128 * t + 128],
                                             w2[:, e, f, :], start=(f == 0), stop=(f == FT - 1))
                        if t % 4 == 3:
                            last.then_inc(y_ps, 1)
                    due(front, slot)
                due(front, LATE)

            def f_col(t):
                return t % 4

            pe.wait_ge(params_in, 16 * len(params))
            due([front(0), -1], LATE)
            with pe.Fori(0, B - 1) as i:
                experts(i, [front(i + 1), -1])
            experts(B - 1, None)


def self_attention_phase(nc, ctx, B, io, const, tok_dram, tokens):
    with ExitStack() as st:
        def sb(name, shape, dt=F32):
            return st.enter_context(nc.sbuf_tensor("t_" + name, shape, dt))

        def sem(name):
            return ctx.enter_context(nc.semaphore("t_" + name))

        xln, xt, qt = sb("xln", [128, NT, C]), sb("xt", [128, N]), sb("qt", [128, N])
        stats, mv = sb("stats", [128, NT, 6]), sb("mv", [128, NT, 2])
        var, inv, tmp = sb("var", [128, NT]), sb("inv", [128, NT]), sb("tmp", [128, NT])
        w, b = sb("w", [128, C]), sb("b", [128, 1])
        negmax, sums = sb("negmax", [128, NT]), sb("sums", [128, NT])
        probs, probs_t = sb("probs", [128, 2, N]), sb("probs_t", [128, 2, NT, 128])
        ps_s = [st.enter_context(nc.psum_tensor(f"t_ps_s{n}", [128, N], F32)) for n in range(2)]
        ps_t = st.enter_context(nc.psum_tensor("t_ps_t", [128, N], F32))
        ps_o = [st.enter_context(nc.psum_tensor(f"t_ps_o{n}", [128, 512], F32)) for n in range(2)]
        S = {name: sem(name) for name in "params_in tok_in ln_up lnt_ps xt_up q_ps q_up s_ps max_up exp_up turned_ps turned_v turned_a out_ps added".split()}
        block = st.enter_context(nc.Block())

        @block.sync
        def _(sp):
            sp.dma_start(w[:, :], io["L3_attn_W"]).then_inc(S["params_in"], 16)
            sp.dma_start(b[:, :], io["L3_attn_b"]).then_inc(S["params_in"], 16)
            sp.sem_inc(S["tok_in"], 16)
            with sp.Fori(0, B) as i:
                sp.wait_ge(S["tok_in"], i * 16 + 16)
                sp.dma_start(tokens[:, bass.ds(i, 1), :, :].rearrange("p a t c -> p (a t c)"), tok_dram[bass.ds(i, 1), :, :].rearrange("a p n -> (a p) n")).then_inc(S["tok_in"], 16)

        def add_out(dve, i, t):
            dve.wait_ge(S["out_ps"], i * NT + t + 1)
            dve.reciprocal(sums[:, t:t + 1], sums[:, t:t + 1])
            dve.drain()
            tile = tokens[:, bass.ds(i, 1), t, :].rearrange("p a c -> p (a c)")
            dve.scalar_tensor_tensor(tile, ps_o[t % 2][:, 0:C], sums[:, t:t + 1], tile, ALU.mult, ALU.add).then_inc(S["added"], 1)
            dve.drain()

        @block.vector
        def _(dve):
            with dve.Fori(0, B) as i:
                dve.wait_ge(S["tok_in"], i * 16 + 32)
                token_norm(dve, xln, tokens[:, bass.ds(i, 1), :, :].rearrange("p a t c -> p (a t) c"), stats, mv, var, inv, tmp).then_inc(S["ln_up"], 1)

                def row_max(t):
                    dve.wait_ge(S["s_ps"], i * NT + t + 1)
                    dve.tensor_reduce(negmax[:, t:t + 1], ps_s[t % 2][:, :], axis=AX.X, op=ALU.max, negate=True).then_inc(S["max_up"], 1)

                row_max(0)
                for t in range(NT):
                    if t + 1 < NT:
                        row_max(t + 1)
                    dve.wait_ge(S["turned_ps"], i * NT + t + 1)
                    dve.tensor_copy(probs_t[:, t % 2, 0:4, :].rearrange("p m n -> p (m n)"), ps_t[:, 0:512]).then_inc(S["turned_v"], 1)
                    if t == 0:
                        continue
                    add_out(dve, i, t - 1)
                add_out(dve, i, NT - 1)

        @block.scalar
        def _(act):
            act.wait_ge(S["params_in"], 32)
            with act.Fori(0, B) as i:
                act.wait_ge(S["lnt_ps"], i + 1)
                act.activation(xt[:, :], ps_s[0][:, :], ACT.Copy).then_inc(S["xt_up"], 1)
                act.wait_ge(S["q_ps"], i + 1)
                act.activation(qt[:, :], ps_s[1][:, :], ACT.Identity, bias=b[:, :]).then_inc(S["q_up"], 1)

                def exponential(t):
                    act.wait_ge(S["max_up"], i * NT + t + 1)
                    if t >= 2:
                        act.wait_ge(S["turned_ps"], i * NT + t - 1)
                    act.activation(probs[:, t % 2, :], ps_s[t % 2][:, :], ACT.Exp, bias=negmax[:, t:t + 1], accum_out=sums[:, t:t + 1]).then_inc(S["exp_up"], 1)

                exponential(0)
                for t in range(NT):
                    if t + 1 < NT:
                        exponential(t + 1)
                    act.wait_ge(S["turned_ps"], i * NT + t + 1)
                    act.activation(probs_t[:, t % 2, 4:8, :].rearrange("p m n -> p (m n)"), ps_t[:, 512:1024], ACT.Copy).then_inc(S["turned_a"], 1)

        @block.tensor
        def _(pe):
            pe.wait_ge(S["params_in"], 32)
            with pe.Fori(0, B) as i:
                pe.wait_ge(S["ln_up"], i + 1)
                turn_tiles(pe, ps_s[0], xln, const["ident"]).then_inc(S["lnt_ps"], 1)
                pe.wait_ge(S["xt_up"], i + 1)
                for k in range(HALVES):
                    last = pe.matmul(ps_s[1][:, 512 * k:512 * k + 512], w[:, :], xt[:, 512 * k:512 * k + 512], start=True, stop=True)
                last.then_inc(S["q_ps"], 1)
                pe.wait_ge(S["q_up"], i + 1)

                def scores(t):
                    if t >= 2:
                        pe.wait_ge(S["exp_up"], i * NT + t - 1)
                    for k in range(HALVES):
                        last = pe.matmul(ps_s[t % 2][:, 512 * k:512 * k + 512], qt[:, 128 * t:128 * t + 128], qt[:, 512 * k:512 * k + 512], start=True, stop=True)
                    last.then_inc(S["s_ps"], 1)

                def weigh(t):
                    pe.wait_ge(S["turned_v"], i * NT + t + 1)
                    pe.wait_ge(S["turned_a"], i * NT + t + 1)
                    if t >= 2:
                        pe.wait_ge(S["added"], i * NT + t - 1)
                    for m in range(NT):
                        last = pe.matmul(ps_o[t % 2][:, 0:C], probs_t[:, t % 2, m, :], xln[:, m, :], start=(m == 0), stop=(m == NT - 1))
                    last.then_inc(S["out_ps"], 1)

                scores(0)
                scores(1)
                for t in range(NT):
                    if t:
                        pe.wait_ge(S["turned_v"], i * NT + t)
                        pe.wait_ge(S["turned_a"], i * NT + t)
                    pe.wait_ge(S["exp_up"], i * NT + t + 1)
                    for m in range(NT):
                        last = pe.transpose(ps_t[:, 128 * m:128 * m + 128], probs[:, t % 2, 128 * m:128 * m + 128], const["ident"])
                    last.then_inc(S["turned_ps"], 1)
                    if t + 2 < NT:
                        scores(t + 2)
                    if t:
                        weigh(t - 1)
                weigh(NT - 1)


def silu_experts_phase(nc, ctx, B, io, const, tokens, out):
    with ExitStack() as st:
        def sb(name, shape, dt=F32):
            return st.enter_context(nc.sbuf_tensor("e_" + name, shape, dt))

        def sem(name):
            return ctx.enter_context(nc.semaphore("e_" + name))

        E, K, F = 16, 6, 64
        PAIRS = E * F // 128
        UNITS = PAIRS + 1
        CAP = max(1, int(B * N * K * 2.0 / E))
        xln, xt = sb("xln", [128, NT, C]), sb("xt", [128, N])
        stats, mv = sb("stats", [128, NT, 6]), sb("mv", [128, NT, 2])
        var, inv, tmp = sb("var", [128, NT]), sb("inv", [128, NT]), sb("tmp", [128, NT])
        gate = gate_tiles(sb, E)
        tile_in = sb("tile_in", [128, NT, C])
        chosen_before = sb("chosen_before", [128, NT + 1, E])
        score_t = sb("score_t", [E, N])
        wg, wu, wd = sb("wg", [128, UNITS, 128]), sb("wu", [128, UNITS, 128]), sb("wd", [128, UNITS, C])
        wr, rbias, tie = sb("wr", [128, E]), sb("rbias", [128, E]), sb("tie", [128, E * E])
        before, ones, pairsel = sb("before", [128, 128]), sb("ones", [128, 128]), sb("pairsel", [E, PAIRS, 128])
        act_up, mixed = sb("act_up", [128, 2, 512]), sb("mixed", [128, 2, 512])
        result = sb("result", [128, 2, 512])
        ps_g, ps_u, ps_b = ([st.enter_context(nc.psum_tensor(f"e_ps_{x}{n}", [128, 512], F32)) for n in range(2)] for x in "gub")
        ps_o = [st.enter_context(nc.psum_tensor(f"e_ps_o{n}", [128, 512], F32)) for n in range(2)]
        S = {name: sem(name) for name in "params_in ln_up lnt_ps xt_up gate_ps shift_up exp_up chosen_up count_ps score_up st_ps st_up out_ps result_up".split()}
        unit_ps, silu_up, mixed_up = sem("unit_ps"), sem("silu_up"), sem("mixed_up")
        stored = [sem(f"stored{n}") for n in range(2)]
        params = [(wr[:, :], io["L3_routerT"]), (rbias[:, :], io["L3_ffn_bias"].rearrange("c b -> b c").broadcast_to((128, E))),
                  (tie[:, :], io["const_tie16"]), (before[:, :], io["const_before"]), (ones[:, :], io["const_ones"]),
                  (pairsel[:, :, :], io["const_pairsel"].rearrange("e (q p) -> e q p", q=PAIRS)),
                  (wg[:, 0:PAIRS, :], io["L3_gT"].rearrange("d (q f) -> d q f", q=PAIRS)), (wg[:, PAIRS, :], io["L3_sgT"]),
                  (wu[:, 0:PAIRS, :], io["L3_uT"].rearrange("d (q f) -> d q f", q=PAIRS)), (wu[:, PAIRS, :], io["L3_suT"]),
                  (wd[:, 0:PAIRS, :], io["L3_dT"].rearrange("(q f) d -> f q d", q=PAIRS)), (wd[:, PAIRS, :], io["L3_sdT"])]
        STEPS = HALVES * UNITS
        block = st.enter_context(nc.Block())

        @block.sync
        def _(sp):
            for dst, src in params:
                sp.dma_start(dst, src).then_inc(S["params_in"], 16)
            with sp.Fori(0, B) as i:
                for k in range(HALVES):
                    sp.wait_ge(S["result_up"], i * HALVES + k + 2)
                    sp.dma_start(out[bass.ds(i, 1), :, 512 * k:512 * k + 512].rearrange("a c n -> (a c) n"), result[:, k, :]).then_inc(stored[k], 16)
            for k in range(HALVES):
                sp.wait_ge(stored[k], 16 * B + 16)

        @block.vector
        def _(dve):
            dve.memset(chosen_before[:, :, :], 0.0)
            dve.wait_ge(S["params_in"], 16 * len(params))
            dve.drain()
            with dve.Fori(0, B) as i:
                token_norm(dve, xln, tokens[:, bass.ds(i, 1), :, :].rearrange("p a t c -> p (a t) c"), stats, mv, var, inv, tmp)
                dve.tensor_copy(tile_in[:, :, :], tokens[:, bass.ds(i, 1), :, :].rearrange("p a t c -> p (a t) c")).then_inc(S["ln_up"], 1)
                dve.wait_ge(S["gate_ps"], i + 1)
                dve.tensor_tensor(gate["logits"][:, :, :], ps_u[0][:, 0:NT * E].rearrange("p (t e) -> p t e", t=NT),
                                  rbias[:, :].unsqueeze(1).broadcast_to((128, NT, E)), ALU.add)
                dve.drain()
                gate_shift(dve, gate, E).then_inc(S["shift_up"], 1)
                dve.wait_ge(S["exp_up"], i + 1)
                gate_choose(dve, gate, E, K, 1e-9, tie[:, :])
                dve.drain()
                for t in range(NT):
                    last = dve.tensor_tensor(chosen_before[:, t + 1, :], chosen_before[:, t, :], gate["chosen"][:, t, :], ALU.add)
                    dve.drain()
                dve.drain().then_inc(S["chosen_up"], 1)
                dve.wait_ge(S["count_ps"], i + 1)
                dve.tensor_copy(chosen_before[:, 0, :], chosen_before[:, NT, :])
                dve.scalar_tensor_tensor(gate["score"][:, :, :], ps_u[1][:, 0:NT * E].rearrange("p (t e) -> p t e", t=NT), float(CAP), gate["score"][:, :, :],
                                         ALU.is_lt, ALU.mult).then_inc(S["score_up"], 1)
                dve.drain()
                for k in range(HALVES):
                    dve.wait_ge(S["st_ps"], i * HALVES + k + 1)
                    dve.tensor_copy(score_t[:, 512 * k:512 * k + 512], ps_g[k][0:E, :]).then_inc(S["st_up"], 1)
                for n in range(STEPS):
                    k, unit = divmod(n, UNITS)
                    dve.wait_ge(silu_up, i * STEPS + n + 1)
                    if unit < PAIRS:
                        dve.tensor_tensor(act_up[:, n % 2, :], act_up[:, n % 2, :], ps_u[n % 2][:, :], ALU.mult)
                        dve.drain()
                        dve.tensor_tensor(mixed[:, n % 2, :], act_up[:, n % 2, :], ps_b[n % 2][:, :], ALU.mult).then_inc(mixed_up, 1)
                    else:
                        dve.scalar_tensor_tensor(mixed[:, n % 2, :], act_up[:, n % 2, :], 0.5, ps_u[n % 2][:, :], ALU.mult, ALU.mult).then_inc(mixed_up, 1)

        def store_half(act, i, k):
            act.wait_ge(S["out_ps"], i * HALVES + k + 1)
            act.wait_ge(stored[k], i * 16 + 16)
            act.activation(result[:, k, :], ps_o[k][:, :], ACT.Copy).then_inc(S["result_up"], 1)

        @block.scalar
        def _(act):
            act.sem_inc(S["result_up"], 1)
            for k in range(HALVES):
                act.sem_inc(stored[k], 16)
            with act.Fori(0, B) as i:
                for k in range(HALVES):
                    act.wait_ge(S["lnt_ps"], i * HALVES + k + 1)
                    act.activation(xt[:, 512 * k:512 * k + 512], ps_g[k][:, :], ACT.Copy).then_inc(S["xt_up"], 1)
                act.wait_ge(S["shift_up"], i + 1)
                act.activation(gate["probs"][:, :, :], gate["probs"][:, :, :], ACT.Exp).then_inc(S["exp_up"], 1)
                for n in range(STEPS):
                    k, unit = divmod(n, UNITS)
                    act.wait_ge(unit_ps, i * STEPS + n + 1)
                    if n >= 2:
                        act.wait_ge(mixed_up, i * STEPS + n - 1)
                    act.activation(act_up[:, n % 2, :], ps_g[n % 2][:, :], ACT.Silu).then_inc(silu_up, 1)
                    if n == UNITS:
                        store_half(act, i, 0)
                store_half(act, i, 1)

        @block.tensor
        def _(pe):
            pe.wait_ge(S["params_in"], 16 * len(params))
            with pe.Fori(0, B) as i:
                pe.wait_ge(S["ln_up"], i + 1)
                for k in range(HALVES):
                    for t in range(4):
                        last = pe.transpose(ps_g[k][:, 128 * t:128 * t + 128], xln[:, 4 * k + t, :], const["ident"])
                    last.then_inc(S["lnt_ps"], 1)
                pe.wait_ge(S["xt_up"], i * HALVES + HALVES)
                for t in range(NT):
                    last = pe.matmul(ps_u[0][:, E * t:E * t + E], xt[:, 128 * t:128 * t + 128], wr[:, :], start=True, stop=True)
                last.then_inc(S["gate_ps"], 1)
                pe.wait_ge(S["chosen_up"], i + 1)
                pe.matmul(ps_u[1][:, 0:NT * E], before[:, :], gate["chosen"][:, :, :].rearrange("p t e -> p (t e)"), start=True, stop=False)
                pe.matmul(ps_u[1][:, 0:NT * E], ones[:, :], chosen_before[:, 0:NT, :].rearrange("p t e -> p (t e)"), start=False, stop=True).then_inc(S["count_ps"], 1)
                pe.wait_ge(S["score_up"], i + 1)
                for k in range(HALVES):
                    for t in range(4):
                        last = pe.transpose(ps_g[k][0:E, 128 * t:128 * t + 128], gate["score"][:, 4 * k + t, :], const["ident"])
                    last.then_inc(S["st_ps"], 1)
                pe.wait_ge(S["st_up"], i * HALVES + HALVES)

                def down(n):
                    k, unit = divmod(n, UNITS)
                    if unit == 0:
                        if k == 0:
                            pe.wait_ge(S["result_up"], i * HALVES + 1)
                        for t in range(4):
                            pe.matmul(ps_o[k][:, 128 * t:128 * t + 128], tile_in[:, 4 * k + t, :], const["ident"],
                                      start=(t == 0), stop=False, skip_group_check=True)
                    pe.wait_ge(mixed_up, i * STEPS + n + 1)
                    last = pe.matmul(ps_o[k][:, :], wd[:, unit, :], mixed[:, n % 2, :], start=False, stop=(unit == UNITS - 1), skip_group_check=True)
                    if unit == UNITS - 1:
                        last.then_inc(S["out_ps"], 1)

                for n in range(STEPS):
                    k, unit = divmod(n, UNITS)
                    cols = slice(512 * k, 512 * k + 512)
                    if n >= 2:
                        pe.wait_ge(mixed_up, i * STEPS + n - 1)
                    if unit < PAIRS:
                        pe.matmul(ps_b[n % 2][:, :], pairsel[:, unit, :], score_t[:, cols], start=True, stop=True)
                    pe.matmul(ps_u[n % 2][:, :], wu[:, unit, :], xt[:, cols], start=True, stop=True)
                    pe.matmul(ps_g[n % 2][:, :], wg[:, unit, :], xt[:, cols], start=True, stop=True).then_inc(unit_ps, 1)
                    if n:
                        down(n - 1)
                down(STEPS - 1)


def program(nc, B, io, out):
    ctx = ExitStack()
    with ctx:
        def keep(name, shape, dt=F32):
            return ctx.enter_context(nc.sbuf_tensor(name, shape, dt))

        cap = {k[6:]: v for k, v in io.items() if k.startswith("const_")}
        const, const_in = {}, []
        for name in ("ident", "block16", "block4", "sumsel"):
            tile = keep("c_" + name, [128, 128])
            const[name] = tile[:, :]
            const_in.append((tile[:, :], cap[name]))
        gn2 = keep("gn2", [128, 2, B])
        x1_dram = nc.dram_tensor("x1_scratch", (B, C, N), F32).ap()
        split_dram = nc.dram_tensor("split_scratch", (2, 3, C, N), BF16).ap()
        band_dram = nc.dram_tensor("band_scratch", (BANDS, C, HW * BAND), F32).ap()
        tok_dram = nc.dram_tensor("tok_scratch", (B, 128, N), F32).ap()
        maps_stack, u_stack = ExitStack(), ExitStack()
        setup_phase(nc, ctx, io, const, const_in, band_dram)
        u_cols = u_stack.enter_context(nc.sbuf_tensor("u_cols", [128, B, 32, HW], F32))
        attention_phase(nc, ctx, B, io, const, u_cols, gn2, x1_dram, split_dram)
        maps = maps_stack.enter_context(nc.sbuf_tensor("maps", [128, B, 32, HW], F32, side="right"))
        conv_phase(nc, ctx, B, io, u_cols, maps, band_dram)
        u_stack.close()
        landmark_and_gelu_phase(nc, ctx, B, io, const, maps, gn2, x1_dram, tok_dram)
        maps_stack.close()
        tokens = ctx.enter_context(nc.sbuf_tensor("tokens", [128, B, NT, C], F32))
        self_attention_phase(nc, ctx, B, io, const, tok_dram, tokens)
        silu_experts_phase(nc, ctx, B, io, const, tokens, out)


_SHAPED = {
    "L0_qkvT": ("L0_conv_qkv_w", lambda a: a.T), "L0_projT": ("L0_conv_proj_w", lambda a: a.T),
    "L1_w3T": ("L1_conv_w3", lambda a: a[:, :, 0, 0].T),
    "L2_qkvT": ("L2_attn_Wqkv", lambda a: a.T), "L2_projT": ("L2_attn_Wproj", lambda a: a.T),
    "L2_ffn_Wg": ("L2_ffn_Wg", lambda a: a), "L2_ffn_W1": ("L2_ffn_W1", lambda a: a),
    "L2_ffn_W2": ("L2_ffn_W2", lambda a: a), "L2_ffn_b1": ("L2_ffn_b1", lambda a: a), "L2_ffn_b2": ("L2_ffn_b2", lambda a: a),
    "L3_attn_W": ("L3_attn_W", lambda a: a), "L3_routerT": ("L3_ffn_router_w", lambda a: a.T),
    "L3_sgT": ("L3_ffn_shared_w_gate", lambda a: a.reshape(-1, C).T), "L3_suT": ("L3_ffn_shared_w_up", lambda a: a.reshape(-1, C).T),
    "L3_sdT": ("L3_ffn_shared_w_down", lambda a: a.transpose(0, 2, 1).reshape(-1, C)),
    "L3_gT": ("L3_ffn_w_gate", lambda a: a.reshape(-1, C).T), "L3_uT": ("L3_ffn_w_up", lambda a: a.reshape(-1, C).T),
    "L3_dT": ("L3_ffn_w_down", lambda a: a.transpose(0, 2, 1).reshape(-1, C)),
}
_TAPS = ["L1_conv_w0"] + ["L1_conv_" + w for v, h, _ in KERNELS for w in (v, h)]
_COLUMNS = ["L0_conv_norm_w", "L0_conv_norm_b", "L0_conv_qkv_b", "L0_conv_proj_b", "L1_conv_b0", "L1_conv_b0_1", "L1_conv_b0_2",
            "L1_conv_b1_1", "L1_conv_b1_2", "L1_conv_b2_1", "L1_conv_b2_2", "L1_conv_b3", "L2_attn_bqkv", "L2_attn_bproj",
            "L3_attn_b", "L3_ffn_bias"]


def kernel(**inputs):
    import concourse.bacc as _bacc
    from concourse.bass_utils import run_bass_kernel_spmd as _run

    a = {k: np.asarray(v) for k, v in inputs.items()}
    B = a["x"].shape[0]
    host = {"x": a["x"].reshape(B, C, N)}
    host.update({k: f(a[n]) for k, (n, f) in _SHAPED.items()})
    host.update({n: a[n].reshape(C, -1)[:, ::-1] if n != "L1_conv_w0" else a[n].reshape(C, 5, 5)[:, :, ::-1].reshape(C, 25) for n in _TAPS})
    host.update({n: a[n].reshape(-1, 1) for n in _COLUMNS})
    host.update({"const_" + k: v for k, v in shape_constants().items()})
    nc = _bacc.Bacc("TRN2", target_bir_lowering=False, num_devices=1)
    arrays, io = {}, {}
    for k, v in host.items():
        v = np.ascontiguousarray(v)
        arrays[f"in_{k}_dram"] = v
        io[k] = nc.dram_tensor(f"in_{k}_dram", v.shape, mybir.dt.from_np(v.dtype), kind="ExternalInput").ap()
    out = nc.dram_tensor("out_0_dram", (B, C, N), F32, kind="ExternalOutput").ap()
    program(nc, B, io, out)
    r = _run(nc, [arrays], core_ids=[0])
    return r.results[0]["out_0_dram"].reshape(B, C, HW, HW)
```

```python
import concourse.bass as bass
from concourse import mybir
from concourse.alu_op_type import AluOpType as ALU
from contextlib import ExitStack
import numpy as np

F32 = mybir.dt.float32
BF16 = mybir.dt.bfloat16
I32 = mybir.dt.int32
ACT = mybir.ActivationFunctionType
AX = mybir.AxisListType

C = 128
HW = 32
N = HW * HW
NT = N // 128
HALVES = N // 512
HEADS = 8
D = C // HEADS
CQ = 4


def shape_constants():
    p = np.arange(128)
    f = np.float32
    m = {}
    m["ident"] = np.eye(128, dtype=f)
    m["block16"] = (p[:, None] // 16 == p[None, :] // 16).astype(f)
    m["block4"] = (p[:, None] // 4 == p[None, :] // 4).astype(f)
    m["sumsel"] = ((p[:, None] % 32 == 16) & (p[:, None] // 32 == p[None, :] // 32)).astype(f)
    m["before"] = (p[:, None] < p[None, :]).astype(f)
    m["ones"] = np.ones((128, 128), f)
    m["pairsel"] = np.stack([(np.arange(48)[:, None] % 16 == 2 * q + (p[None, :] // 64)) for q in range(8)], 1).astype(f).reshape(48, 1024)
    for e in (8, 16):
        r = np.arange(e)
        m[f"tie{e}"] = np.broadcast_to((r[None, :] < r[:, None]).astype(f).reshape(1, e * e), (128, e * e)).copy()
    return m


def rsqrt(dve, y, v, t):
    dve.tensor_scalar(y.bitcast(I32), v.bitcast(I32), -0.5, 1597463007.0, ALU.mult, ALU.add)
    for _ in range(4):
        dve.drain()
        dve.tensor_tensor(t, y, y, ALU.mult)
        dve.drain()
        dve.tensor_tensor(t, t, v, ALU.mult)
        dve.drain()
        dve.tensor_scalar(t, t, -0.5, 1.5, ALU.mult, ALU.add)
        dve.drain()
        last = dve.tensor_tensor(y, y, t, ALU.mult)
    dve.drain()
    return last


def channel_moments(dve, moments, stats, mv, x):
    for k in range(HALVES):
        dve.bn_stats(stats[:, k, :], x[:, 512 * k:512 * k + 512])
    dve.drain()
    dve.bn_aggr(mv[:, :], stats[:, :, :])
    dve.drain()
    dve.tensor_copy(moments[:, 0:1], mv[:, 0:1])
    return dve.scalar_tensor_tensor(moments[:, 1:2], mv[:, 0:1], mv[:, 0:1], mv[:, 1:2], ALU.mult, ALU.add)


def group_affine(dve, scale, shift, group, sums, width, small, eps):
    dve.tensor_scalar(group[:, :], sums, 1.0 / width, None, ALU.mult)
    dve.drain()
    dve.tensor_tensor(small[:, 0:1], group[:, 0:1], group[:, 0:1], ALU.mult)
    dve.drain()
    dve.tensor_tensor(small[:, 1:2], group[:, 1:2], small[:, 0:1], ALU.subtract)
    dve.drain()
    dve.tensor_scalar(small[:, 1:2], small[:, 1:2], 0.0, eps, ALU.max, ALU.add)
    dve.drain()
    rsqrt(dve, scale, small[:, 1:2], small[:, 2:3])
    dve.scalar_tensor_tensor(shift, group[:, 0:1], -1.0, scale, ALU.mult, ALU.mult)
    dve.drain()


def attention_phase(nc, ctx, B, io, const, u_cols, gn2, x1_dram, split_dram):
    with ExitStack() as st:
        def sb(name, shape, dt=F32):
            return st.enter_context(nc.sbuf_tensor("a_" + name, shape, dt))

        def sem(name):
            return ctx.enter_context(nc.semaphore("a_" + name))

        PRODUCTS = ((0, 0), (0, 1), (1, 0), (1, 1), (0, 2), (2, 0))
        KS = len(PRODUCTS) * D
        PIECES = 3
        xf, xr = sb("xf", [128, N]), sb("xr", [128, N])
        xn = sb("xn", [128, N])
        full, rest = sb("full", [128, 2, N]), sb("rest", [128, 512])
        pieces = sb("pieces", [128, 2, PIECES, N], BF16)
        q_stack = sb("q_stack", [KS + PIECES, HEADS, N], BF16)
        k_stack = sb("k_stack", [KS + PIECES, HEADS, N], BF16)
        v_next = sb("v_next", [128, NT, C])
        v_ones = sb("v_ones", [128, NT, HEADS, 32])
        probs = sb("probs", [128, 2, N])
        o_sums, sums = sb("o_sums", [128, 2, N]), sb("sums", [128, 2, N])
        x1 = sb("x1", [128, N])
        u_tr = sb("u_tr", [128, 32, HW])
        wqkv = sb("wqkv", [128, 3 * C])
        wproj = sb("wproj", [128, 2, C])
        vbias = sb("vbias", [128, C])
        qbias, kbias, pbias = sb("qbias", [128, 1]), sb("kbias", [128, 1]), sb("pbias", [128, 1])
        nw, nb = sb("nw", [128, 1]), sb("nb", [128, 1])
        stats, mv = sb("stats", [128, HALVES, 6]), sb("mv", [128, 2])
        moments, group, small = sb("moments", [128, 2]), sb("group", [128, 2]), sb("small", [128, 4])
        gscale, gshift = sb("gscale", [128, 1]), sb("gshift", [128, 1])
        maxes = sb("maxes", [128, 2, NT, 2])
        negmax = sb("negmax", [128, 2, NT])
        shift32 = sb("shift32", [NT, 2, 128])
        shift3 = sb("shift3", [NT, 2, PIECES, 128], BF16)
        ps_a = st.enter_context(nc.psum_tensor("ps_a", [128, 2, 512], F32))
        ps_b = st.enter_context(nc.psum_tensor("ps_b", [128, 2, N], F32))
        ps_o = st.enter_context(nc.psum_tensor("ps_o", [128, N], F32))

        params_in, zeroed, xf_in, xf_free, xr_in, xr_free = (sem(x) for x in "params_in zeroed xf_in xf_free xr_in xr_free".split())
        moments_up, moments2_up, xn_up, on_up = (sem(x) for x in "moments_up moments2_up xn_up on_up".split())
        sums_up, full_up = sem("sums_up"), sem("full_up")
        v_up, v_copied, v7_copied = sem("v_up"), sem("v_copied"), sem("v7_copied")
        split_up = [sem(f"split_up{n}") for n in range(2)]
        split_stored = [sem(f"split_stored{n}") for n in range(2)]
        stack_in = [sem(f"stack_in{n}") for n in range(HEADS)]
        shift_in = [sem(f"shift_in{n}") for n in range(2)]
        ring_up, ring_read, max_up, shift_up = sem("ring_up"), sem("ring_read"), sem("max_up"), sem("shift_up")
        b_up, b_exp, o_up, o_out = sem("b_up"), sem("b_exp"), sem("o_up"), sem("o_out")
        ut_up, x1_stored, u_stored = sem("ut_up"), sem("x1_stored"), sem("u_stored")

        SLOTS = HEADS * NT
        AHEAD = 2
        PARAMS = 16 * (7 + HEADS)

        def before(k):
            work = [(19, ("moments",)), (21, ("sums", 0)), (22, ("norm",))]
            for qk in range(2):
                for half in range(HALVES):
                    s = 25 + 6 * qk + 3 * half
                    work.append((s, ("qk", qk, half)))
            return work + [(37, ("v", 0)), (38, ("v", 1))]

        def after():
            inverts = [(4 + n, ("invert", n)) for n in range(8)]
            return [(1, ("take", HEADS - 1)), (3, ("spread", 0)), (4, ("spread", 1)), (5, ("spread", 2)), (6, ("spread", 3))] + inverts + [
                    (12, ("project", 0)), (13, ("project", 1)), (14, ("moments2",)), (16, ("sums", 1)), (17, ("norm2",)), (18, ("turn2",))]

        def plan(heads, front, back):
            by_slot = [[] for _ in range(SLOTS)]
            for s in range(SLOTS):
                step, t = divmod(s, NT)
                if step + AHEAD < heads:
                    by_slot[s] += [("scores", step + AHEAD, 2 * t), ("scores", step + AHEAD, 2 * t + 1)]
                if t == 0 and step + AHEAD - 1 < heads:
                    by_slot[s].append(("shift", step + AHEAD - 1))
                if step >= 1 and t == 6:
                    by_slot[s].append(("take", step - 1))
            for s, work in (after() if back else []) + (before(1) if front else []):
                by_slot[s].append(work)
            return by_slot

        RING = ("scores", "shift", "spread", "project", "sums", "qk", "v")
        first = [work for _, work in before(0)]
        first += [("scores", 0, g) for g in range(2 * NT)] + [("scores", 1, 0), ("scores", 1, 1), ("shift", 0)]
        first += [("scores", 1, g) for g in range(2, 2 * NT)]
        bodies = {"first": plan(HEADS + AHEAD, True, False), "middle": plan(HEADS + AHEAD, True, True), "last": plan(HEADS, False, True)}
        count = {name: sum(w[0] in RING for slot in body for w in slot) for name, body in bodies.items()}
        first_count = sum(w[0] in RING for w in first)
        closing = [work for _, work in after()]
        assert count["middle"] % 2 == 0

        def ring_base(kind, i):
            if kind == "prologue":
                return 0, 0
            if kind == "first":
                return first_count, first_count % 2
            base = first_count + count["first"] - count["middle"]
            if kind == "closing":
                n = base + (B - 1) * count["middle"] + count["last"]
                return n, n % 2
            return i * count["middle"] + base, base % 2

        block = st.enter_context(nc.Block())

        @block.sync
        def _(sp):
            def load_image(dst, i, skip, up):
                source = io["x"][skip:B, :, :]
                sp.dma_start(dst[:, :], source[bass.ds(i, 1), :, :].rearrange("a c n -> (a c) n")).then_inc(up, 16)

            def store_image(i):
                sp.dma_start(u_cols[:, bass.ds(i, 1), :, :].rearrange("p a c h -> p (a c h)"),
                             u_tr[:, :, :].rearrange("p c h -> p (c h)")).then_inc(u_stored, 16)
                sp.dma_start(x1_dram[bass.ds(i, 1), :, :].rearrange("a c n -> (a c) n"), x1[:, :]).then_inc(x1_stored, 16)

            def store_split(qk, i):
                if not isinstance(i, int) or i > 0:
                    for h in range(HEADS):
                        sp.wait_ge(stack_in[h], i * 32)
                sp.wait_ge(split_up[qk], i + 1)
                for s, slot in enumerate(PRODUCTS):
                    sp.dma_start(split_dram[qk, :, s, :, :], pieces[:, qk, slot[qk], :]).then_inc(split_stored[qk], 16)

            def load_stack(i, h):
                for qk, stack in enumerate((q_stack, k_stack)):
                    sp.wait_ge(split_stored[qk], i * 96 + 96)
                    sp.dma_start(stack[0:KS, h, :], split_dram[qk, h, :, :, :].rearrange("s d n -> (s d) n")).then_inc(stack_in[h], 16)

            def send_shift(i, s):
                h = s % HEADS
                sp.wait_ge(shift_up, i * HEADS + s + 1)
                for p in range(PIECES):
                    sp.dma_start(q_stack[KS + p:KS + p + 1, h, :].rearrange("s (t n) -> s t n", t=NT),
                                 shift3[:, h % 2, p, :]).then_inc(shift_in[h % 2], 16)

            def body(prev, i, front, back):
                if back:
                    sp.wait_ge(b_up, i * SLOTS)
                    load_stack(i, HEADS - 1)
                if front:
                    sp.wait_ge(xf_free, i + 2)
                    load_image(xf, *((prev, 2) if back else (0, 1)), xf_in)
                for step in range(HEADS if front else HEADS - 1):
                    send_shift(i, step + 1)
                    if step == 1:
                        sp.wait_ge(xr_free, i + 1)
                        load_image(xr, *((prev, 1) if back else (0, 0)), xr_in)
                    if step == 2 and back:
                        sp.wait_ge(ut_up, i)
                        store_image(prev)
                    if front:
                        if step in (4, 5):
                            store_split(step - 4, i + 1)
                        if step >= 5:
                            for h in range(0, 5) if step == 5 else (step - 1,):
                                if h < HEADS - 1:
                                    sp.wait_ge(b_up, i * SLOTS + NT * (h + 1))
                                    load_stack(i + 1, h)

            load_image(xf, 0, 0, xf_in)
            sp.wait_ge(zeroed, 1)
            for dst, src in ((wqkv[:, :], io["L0_qkvT"]), (qbias[:, :], io["L0_conv_qkv_b"][0:C, :]),
                             (kbias[:, :], io["L0_conv_qkv_b"][C:2 * C, :]), (pbias[:, :], io["L0_conv_proj_b"]),
                             (nw[:, :], io["L0_conv_norm_w"]), (nb[:, :], io["L0_conv_norm_b"]),
                             (vbias[:, :], io["L0_conv_qkv_b"][2 * C:3 * C, :].rearrange("c b -> b c").broadcast_to((128, C)))):
                sp.dma_start(dst, src).then_inc(params_in, 16)
            for h in range(HEADS):
                sp.dma_start(wproj[32 * (h % 4):32 * (h % 4) + D, h // 4, :],
                             io["L0_projT"][D * h:D * h + D, :]).then_inc(params_in, 16)
            sp.sem_inc(xf_free, 1)
            sp.sem_inc(xr_free, 1)
            store_split(0, 0)
            store_split(1, 0)
            for h in range(HEADS):
                load_stack(0, h)
            send_shift(0, 0)
            body(0, 0, True, False)
            with sp.Fori(0, B - 2) as prev:
                body(prev, prev + 1, True, True)
            body(B - 2, B - 1, False, True)
            sp.wait_ge(ut_up, B)
            store_image(B - 1)
            sp.wait_ge(x1_stored, 16 * B + 16)
            sp.wait_ge(u_stored, 16 * B + 16)

        @block.gpsimd
        def _(pool):
            pool.memset(wproj[:, :, :], 0.0)
            pool.drain()
            pool.memset(k_stack[KS:KS + PIECES, :, :], 1.0)
            pool.drain()
            pool.memset(v_ones[:, :, :, :], 1.0)
            pool.drain().then_inc(zeroed, 1)

            def divide(i):
                for n in range(8):
                    g, k = divmod(n, 4)
                    part = o_sums[:, g, 256 * k:256 * k + 256]
                    pool.wait_ge(sums_up, i * 8 + n + 1)
                    pool.tensor_tensor(part, part, sums[:, g, 256 * k:256 * k + 256], ALU.mult)
                    pool.drain()
                pool.drain().then_inc(on_up, 1)

            def split(i):
                for n in range(4):
                    qk, half = divmod(n, 2)
                    cols = slice(512 * half, 512 * half + 512)
                    pool.wait_ge(full_up, i * 4 + n + 1)
                    for p in (1, 2):
                        pool.tensor_tensor(rest[:, :], full[:, qk, cols] if p == 1 else rest[:, :], pieces[:, qk, p - 1, cols], ALU.subtract)
                        pool.drain()
                        pool.tensor_copy(pieces[:, qk, p, cols], rest[:, :])
                        pool.drain()
                    if half == 1:
                        pool.drain().then_inc(split_up[qk], 1)

            split(0)
            split(1)
            with pool.Fori(1, B - 1) as i:
                divide(i - 1)
                split(i + 1)
            divide(B - 2)
            divide(B - 1)

        @block.vector
        def _(dve):
            def step(work, i, nxt, prev, n, parity):
                what, bank = work[0], ps_a[:, parity, :]
                if what in RING:
                    dve.wait_ge(ring_up, n + 1)
                if what == "scores":
                    s, g = work[1:]
                    dve.reduce_max(maxes[:, s % 2, g // 2, g % 2:g % 2 + 1], bank, axis=AX.X).then_inc(ring_read, 1)
                    if g == 2 * NT - 1:
                        dve.drain()
                        dve.tensor_reduce(negmax[:, s % 2, :], maxes[:, s % 2, :, :], axis=AX.X, op=ALU.max, negate=True).then_inc(max_up, 1)
                elif what == "shift":
                    s = work[1]
                    if not isinstance(i, int) or i * HEADS + s >= 2:
                        dve.wait_ge(shift_in[s % 2], i * (16 * PIECES * HEADS // 2) + 16 * PIECES * (s // 2))
                    dve.tensor_copy(shift32[:, s % 2, :], ps_a[0:NT, parity, 0:128]).then_inc(ring_read, 1)
                    dve.drain()
                    for p in range(PIECES):
                        dve.tensor_copy(shift3[:, s % 2, p, :], shift32[:, s % 2, :])
                        dve.drain()
                        if p < PIECES - 1:
                            dve.tensor_tensor(shift32[:, s % 2, :], shift32[:, s % 2, :], shift3[:, s % 2, p, :], ALU.subtract)
                            dve.drain()
                    dve.drain().then_inc(shift_up, 1)
                elif what == "take":
                    h = work[1]
                    r = 32 * (h % 4)
                    dve.wait_ge(o_up, (prev if h == HEADS - 1 else i) * HEADS + h + 1)
                    dve.tensor_copy(o_sums[r:r + 32, h // 4, :], ps_o[r:r + 32, :]).then_inc(o_out, 1)
                    dve.drain()
                elif what == "spread":
                    g, k = divmod(work[1], 2)
                    dve.tensor_copy(sums[:, g, 512 * k:512 * k + 512], bank).then_inc(ring_read, 1)
                    dve.drain()
                elif what == "invert":
                    g, k = divmod(work[1], 4)
                    part = sums[:, g, 256 * k:256 * k + 256]
                    dve.reciprocal(part, part)
                    dve.drain().then_inc(sums_up, 1)
                elif what == "project":
                    k = work[1]
                    if k == 0:
                        dve.wait_ge(xr_in, prev * 16 + 16)
                        dve.wait_ge(x1_stored, prev * 16 + 16)
                        dve.wait_ge(u_stored, prev * 16 + 16)
                    cols = slice(512 * k, 512 * k + 512)
                    dve.scalar_tensor_tensor(x1[:, cols], bank, pbias[:, :], xr[:, cols], ALU.add, ALU.add).then_inc(ring_read, 1)
                    if k == 1:
                        dve.drain().then_inc(xr_free, 1)
                elif what == "moments2":
                    channel_moments(dve, moments, stats, mv, x1).then_inc(moments2_up, 1)
                elif what == "sums":
                    width, eps = ((C // 8, 1e-5), (C // 32, 1e-5))[work[1]]
                    group_affine(dve, gscale[:, :], gshift[:, :], group, bank[:, 0:2], width, small, eps)
                    dve.drain().then_inc(ring_read, 1)
                elif what == "norm2":
                    dve.tensor_copy(gn2[:, 0, bass.ds(prev, 1)], gscale[:, :])
                    dve.tensor_copy(gn2[:, 1, bass.ds(prev, 1)], gshift[:, :])
                    dve.tensor_scalar(xn[:, :], x1[:, :], gscale[:, :], gshift[:, :], ALU.mult, ALU.add)
                    dve.drain()
                elif what == "turn2":
                    dve.transpose(u_tr[:, :, :].rearrange("p c h -> p h c"), xn[:, :]).then_inc(ut_up, 1)
                    dve.drain()
                elif what == "moments":
                    dve.wait_ge(xf_in, nxt * 16 + 16)
                    channel_moments(dve, moments, stats, mv, xf).then_inc(moments_up, 1)
                elif what == "norm":
                    dve.tensor_tensor(gscale[:, :], gscale[:, :], nw[:, :], ALU.mult)
                    dve.tensor_tensor(gshift[:, :], gshift[:, :], nw[:, :], ALU.mult)
                    dve.drain()
                    dve.tensor_tensor(gshift[:, :], gshift[:, :], nb[:, :], ALU.add)
                    dve.drain()
                    dve.tensor_scalar(xn[:, :], xf[:, :], gscale[:, :], gshift[:, :], ALU.mult, ALU.add).then_inc(xn_up, 1)
                    dve.drain().then_inc(xf_free, 1)
                elif what == "qk":
                    qk, half = work[1:]
                    if half == 0 and (not isinstance(nxt, int) or nxt > 0):
                        dve.wait_ge(split_stored[qk], nxt * 96)
                    part = full[:, qk, 512 * half:512 * half + 512]
                    dve.tensor_scalar(part, bank, (qbias, kbias)[qk][:, :], 1.0 if qk else 1.0 / D, ALU.add, ALU.mult).then_inc(ring_read, 1)
                    dve.drain()
                    dve.tensor_copy(pieces[:, qk, 0, 512 * half:512 * half + 512], part)
                    dve.drain().then_inc(full_up, 1)
                elif what == "v":
                    half = work[1]
                    if half == 0 and (not isinstance(nxt, int) or nxt > 0):
                        dve.wait_ge(v7_copied, nxt)
                    last = dve.tensor_tensor(v_next[:, 4 * half:4 * half + 4, :], bank.rearrange("p (t c) -> p t c", t=4),
                                             vbias[:, :].unsqueeze(1).broadcast_to((128, 4, C)), ALU.add)
                    last.then_inc(ring_read, 1)
                    if half == 1:
                        dve.drain().then_inc(v_up, 1)

            def run(works, kind, i, n0):
                base, odd = ring_base(kind, i)
                n = n0
                for work in works:
                    step(work, i, i if kind == "prologue" else i + 1, i - 1 if kind != "closing" else B - 1, base + n, (odd + n) % 2)
                    n += work[0] in RING

            dve.wait_ge(params_in, PARAMS)
            dve.sem_inc(x1_stored, 16)
            dve.sem_inc(u_stored, 16)
            run(first, "prologue", 0, 0)
            run([w for slot in bodies["first"] for w in slot], "first", 0, 0)
            with dve.Fori(1, B - 1) as i:
                run([w for slot in bodies["middle"] for w in slot], "middle", i, 0)
            run([w for slot in bodies["last"] for w in slot], "last", B - 1, 0)
            run(closing, "closing", B - 1, 0)

        @block.scalar
        def _(act):
            def copy_v(h0, h1):
                return act.activation(v_ones[:, :, h0:h1, 0:D], v_next[:, :, D * h0:D * h1].rearrange("p t (h d) -> p t h d", d=D), ACT.Copy)

            def body(i, front):
                for m in range(SLOTS):
                    act.wait_ge(b_up, i * SLOTS + m + 1)
                    act.activation(probs[:, m % 2, :], ps_b[:, m % 2, :], ACT.Exp).then_inc(b_exp, 1)
                    if m == 2:
                        copy_v(HEADS - 1, HEADS).then_inc(v7_copied, 1)
                    if m == 59 and front:
                        act.wait_ge(v_up, i + 2)
                        copy_v(0, HEADS - 1).then_inc(v_copied, 1)

            act.wait_ge(v_up, 1)
            copy_v(0, HEADS - 1).then_inc(v_copied, 1)
            body(0, True)
            with act.Fori(1, B - 1) as i:
                body(i, True)
            body(B - 1, False)

        @block.tensor
        def _(pe):
            def step(work, i, nxt, prev, n, parity, early):
                what, bank = work[0], ps_a[:, parity, :]
                if not early:
                    pe.wait_ge(ring_read, n - 1)
                if what == "scores":
                    s, g = work[1:]
                    t, k = g // 2, g % 2
                    h = s % HEADS
                    if g == 0:
                        pe.wait_ge(stack_in[h], (i + s // HEADS) * 32 + 32)
                    last = pe.matmul(bank, q_stack[0:KS, h, 128 * t:128 * t + 128], k_stack[0:KS, h, 512 * k:512 * k + 512], start=True, stop=True)
                elif what == "shift":
                    pe.wait_ge(max_up, i * HEADS + work[1] + 1)
                    last = pe.transpose(ps_a[0:NT, parity, 0:128], negmax[:, work[1] % 2, :], const["ident"])
                elif what == "spread":
                    g, k = divmod(work[1], 2)
                    if work[1] == 0:
                        pe.wait_ge(o_out, prev * HEADS + HEADS)
                    last = pe.matmul(bank, const["sumsel"], o_sums[:, g, 512 * k:512 * k + 512], start=True, stop=True)
                elif what == "project":
                    k = work[1]
                    pe.wait_ge(on_up, prev + 1)
                    for g in range(2):
                        last = pe.matmul(bank, wproj[:, g, :], o_sums[:, g, 512 * k:512 * k + 512], start=(g == 0), stop=(g == 1))
                elif what == "sums":
                    if work[1] == 0:
                        pe.wait_ge(moments_up, nxt + 1)
                    else:
                        pe.wait_ge(moments2_up, prev + 1)
                    last = pe.matmul(bank[:, 0:2], const[("block16", "block4")[work[1]]], moments[:, :], start=True, stop=True)
                elif what == "qk":
                    qk, half = work[1:]
                    pe.wait_ge(xn_up, nxt + 1)
                    last = pe.matmul(bank, wqkv[:, C * qk:C * qk + C], xn[:, 512 * half:512 * half + 512], start=True, stop=True)
                elif what == "v":
                    for t in range(4):
                        cols = slice(512 * work[1] + 128 * t, 512 * work[1] + 128 * t + 128)
                        last = pe.matmul(bank[:, 128 * t:128 * t + 128], xn[:, cols], wqkv[:, 2 * C:3 * C], start=True, stop=True)
                last.then_inc(ring_up, 1)

            def run(works, kind, i, n):
                base, odd = ring_base(kind, i)
                for work in works:
                    if work[0] in RING:
                        step(work, i, i if kind == "prologue" else i + 1, i - 1 if kind != "closing" else B - 1,
                             base + n, (odd + n) % 2, kind == "prologue" and n < 2)
                        n += 1
                return n

            def shifted_scores(i, m):
                h, t = divmod(m, NT)
                if t == 0:
                    pe.wait_ge(shift_in[h % 2], i * (16 * PIECES * HEADS // 2) + 16 * PIECES * (h // 2 + 1))
                if not isinstance(i, int) or i * SLOTS + m >= 2:
                    pe.wait_ge(b_exp, i * SLOTS + m - 1)
                for k in range(HALVES):
                    last = pe.matmul(ps_b[:, m % 2, 512 * k:512 * k + 512], k_stack[:, h, 128 * t:128 * t + 128],
                                     q_stack[:, h, 512 * k:512 * k + 512], start=True, stop=True)
                last.then_inc(b_up, 1)

            def weigh_values(i, m):
                h, t = divmod(m, NT)
                r = 32 * (h % 4)
                if m == 0:
                    pe.wait_ge(v_copied, i + 1)
                if m == NT * (HEADS - 1):
                    pe.wait_ge(v7_copied, i + 1)
                if t == 0 and (not isinstance(i, int) or i * HEADS + h >= 4):
                    pe.wait_ge(o_out, i * HEADS + h - 3)
                pe.wait_ge(b_exp, i * SLOTS + m + 1)
                for k in range(HALVES):
                    last = pe.matmul(ps_o[r:r + 32, 512 * k:512 * k + 512], v_ones[:, t, h, :],
                                     probs[:, m % 2, 512 * k:512 * k + 512], start=(t == 0), stop=(t == NT - 1))
                if t == NT - 1:
                    last.then_inc(o_up, 1)

            def body(kind, i):
                n = 0
                for m, works in enumerate(bodies[kind]):
                    n = run(works, kind, i, n)
                    shifted_scores(i, m)
                    if m:
                        weigh_values(i, m - 1)
                    elif kind != "first":
                        weigh_values(i - 1, SLOTS - 1)

            pe.wait_ge(params_in, PARAMS)
            run(first, "prologue", 0, 0)
            body("first", 0)
            with pe.Fori(1, B - 1) as i:
                body("middle", i)
            body("last", B - 1)
            weigh_values(B - 1, SLOTS - 1)
            run(closing, "closing", B - 1, 0)


KERNELS = (("w0_1", "w0_2", 7), ("w1_1", "w1_2", 11), ("w2_1", "w2_2", 21))
ROWS5 = 5
BANDS = ROWS5 + 2 * len(KERNELS)
BAND = 2 * HW - 1


def setup_phase(nc, ctx, io, const, const_in, band_dram):
    with ExitStack() as st:
        def sb(name, shape, dt=F32):
            return st.enter_context(nc.sbuf_tensor("s_" + name, shape, dt))

        def sem(name):
            return ctx.enter_context(nc.semaphore("s_" + name))

        taps5 = sb("taps_square", [128, ROWS5, 5])
        taps = [sb(f"taps{n}", [128, k]) for n, k in enumerate(k for _, _, k in KERNELS for _ in range(2))]
        row = sb("row", [128, BANDS, BAND])
        rows = sb("rows", [128, 2, HW, BAND])
        consts_in, taps_in, rows_up = sem("consts_in"), sem("taps_in"), sem("rows_up")
        rows_stored = [sem(f"rows_stored{n}") for n in range(2)]
        block = st.enter_context(nc.Block())

        @block.sync
        def _(sp):
            sp.dma_start(taps5[:, :, :], io["L1_conv_w0"].rearrange("c (a b) -> c a b", a=ROWS5)).then_inc(taps_in, 16)
            names = [w for v, h, _ in KERNELS for w in (v, h)]
            for tap, name in zip(taps, names):
                sp.dma_start(tap[:, :], io["L1_conv_" + name]).then_inc(taps_in, 16)
            for dst, src in const_in:
                sp.dma_start(dst, src).then_inc(consts_in, 16)
            for k in range(BANDS):
                sp.wait_ge(rows_up, k + 1)
                sp.dma_start(band_dram[k, :, :], rows[:, k % 2, :, :].rearrange("c a b -> c (a b)")).then_inc(rows_stored[k % 2], 16)
            for n in range(2):
                sp.wait_ge(rows_stored[n], 16 * ((BANDS + 1 - n) // 2))
            sp.wait_ge(consts_in, 16 * len(const_in))

        @block.vector
        def _(dve):
            dve.memset(row[:, :, :], 0.0)
            dve.wait_ge(taps_in, 16 * (1 + len(taps)))
            dve.drain()
            dve.tensor_copy(row[:, 0:ROWS5, HW - 3:HW + 2], taps5[:, :, :])
            for n, tap in enumerate(taps):
                half = 3 * (KERNELS[n // 2][2] // 2)
                dve.tensor_copy(row[:, ROWS5 + n, HW - 1 - half:HW + half:3], tap[:, :])
            dve.drain()
            for k in range(BANDS):
                if k >= 2:
                    dve.wait_ge(rows_stored[k % 2], 16 * (k // 2))
                dve.tensor_copy(rows[:, k % 2, :, :], row[:, k, :].unsqueeze(1).broadcast_to((128, HW, BAND))).then_inc(rows_up, 1)


def conv_phase(nc, ctx, B, io, u_cols, maps, band_dram):
    with ExitStack() as st:
        def sb(name, shape, dt=F32):
            return st.enter_context(nc.sbuf_tensor("c_" + name, shape, dt))

        def sem(name):
            return ctx.enter_context(nc.semaphore("c_" + name))

        K = len(KERNELS)
        FILLS = 4
        L = B * HW
        bands = [sb(f"bands{n}", [128, BANDS, 128]) for n in range(FILLS)]
        square = [sb(f"square{n}", [128, L]) for n in range(2)]
        square_t = [sb(f"square_t{n}", [128, L]) for n in range(2)]
        along = [sb(f"along{n}", [128, K, L]) for n in range(2)]
        along_t = [sb(f"along_t{n}", [128, K, L]) for n in range(2)]
        bias = sb("bias", [128, 1 + 2 * K, 32])
        last_bias = sb("last_bias", [128, 32])
        ps_s = [st.enter_context(nc.psum_tensor(f"c_ps_s{n}", [128, 512], F32)) for n in range(2)]
        ps_h = [st.enter_context(nc.psum_tensor(f"c_ps_h{n}", [128, K, 512], F32)) for n in range(2)]
        zeroed, bias_in, bands_in = sem("zeroed"), sem("bias_in"), [sem(f"bands_in{n}") for n in range(FILLS)]
        square_ps, square_up, square_turned = sem("square_ps"), sem("square_up"), sem("square_turned")
        along_ps, along_up, turned = sem("along_ps"), sem("along_up"), sem("turned")
        maps_ps, maps_up = sem("maps_ps"), sem("maps_up")
        block = st.enter_context(nc.Block())
        names = ["L1_conv_b0"] + ["L1_conv_b" + v[1:] for v, _, _ in KERNELS] + ["L1_conv_b" + h[1:] for _, h, _ in KERNELS]

        @block.gpsimd
        def _(pool):
            for n in range(FILLS):
                pool.memset(bands[n][:, :, :], 0.0)
                pool.drain()
            pool.drain().then_inc(zeroed, 1)

        @block.sync
        def _(sp):
            for n, name in enumerate(names):
                for q in range(CQ):
                    sp.dma_start(bias[HW * q:HW * q + HW, n, :],
                                 io[name][32 * q:32 * q + 32, :].rearrange("c b -> b c").broadcast_to((HW, 32))).then_inc(bias_in, 16)
            sp.wait_ge(zeroed, 1)
            with sp.Fori(0, 32 // FILLS) as i:
                c = i * FILLS
                for n in range(FILLS):
                    sp.wait_ge(maps_ps, c + n + 1)
                    for q in range(CQ):
                        rows = band_dram[:, bass.ds(c + (32 * q + n), 1), HW - 1:HW - 1 + HW * (BAND - 1)]
                        sp.dma_start(bands[n][HW * q:HW * q + HW, :, HW * q:HW * q + HW],
                                     rows.rearrange("t a (w e) -> w t (a e)", e=BAND - 1)[:, :, 0:HW]).then_inc(bands_in[n], 16)

        @block.tensor
        def _(pe):
            pe.sem_inc(maps_ps, FILLS)
            with pe.Fori(0, 32 // FILLS) as i:
                for first in range(0, FILLS, 2):
                    c = i * FILLS + first
                    for n in range(2):
                        pe.wait_ge(bands_in[first + n], i * 64 + 64)
                        pe.wait_ge(maps_up, c + n + 1)
                        out4 = ps_s[n][:, 0:L].rearrange("p (b h) -> p b h", b=B)
                        src = u_cols[:, :, bass.ds(c + n, 1), :].rearrange("p b a h -> p b (a h)")
                        for j, ky in enumerate((2, 0, 1, 3, 4)):
                            d = ky - 2
                            lo, hi = max(0, -d), min(HW, HW - d)
                            last = pe.matmul(out4[:, :, lo:hi], bands[first + n][:, ky, :], src[:, :, lo + d:hi + d],
                                             start=(j == 0), stop=(j == 4))
                        last.then_inc(square_ps, 1)
                    for n in range(2):
                        pe.wait_ge(square_up, c + n + 1)
                        pe.wait_ge(along_up, c + n + 1)
                        for k in range(K):
                            last = pe.matmul(ps_h[n][:, k, 0:L], bands[first + n][:, ROWS5 + 2 * k, :], square[n][:, :], start=True, stop=True)
                        last.then_inc(along_ps, 1)
                    for n in range(2):
                        pe.wait_ge(turned, c + n + 3)
                        for k in range(K):
                            last = pe.matmul(ps_s[n][:, 0:L], bands[first + n][:, ROWS5 + 2 * k + 1, :], along_t[n][:, k, :],
                                             start=(k == 0), stop=(k == K - 1))
                        last.then_inc(maps_ps, 1)

        @block.scalar
        def _(act):
            act.wait_ge(bias_in, 16 * CQ * len(names))
            act.sem_inc(along_up, 2)
            act.sem_inc(square_turned, 2)
            act.sem_inc(turned, 2)
            with act.Fori(0, 32 // FILLS) as i:
                for first in range(0, FILLS, 2):
                    c = i * FILLS + first
                    for n in range(2):
                        act.wait_ge(square_ps, c + n + 1)
                        act.wait_ge(square_turned, c + n + 1)
                        act.activation(square[n][:, :], ps_s[n][:, 0:L], ACT.Identity, bias=bias[:, 0, bass.ds(c + n, 1)]).then_inc(square_up, 1)
                    for n in range(2):
                        act.wait_ge(along_ps, c + n + 1)
                        act.wait_ge(turned, c + n + 1)
                        for k in range(K):
                            last = act.activation(along[n][:, k, :], ps_h[n][:, k, 0:L], ACT.Identity,
                                                  bias=bias[:, 1 + k, bass.ds(c + n, 1)])
                        last.then_inc(along_up, 1)

        @block.vector
        def _(dve):
            dve.wait_ge(bias_in, 16 * CQ * len(names))
            dve.tensor_tensor(last_bias[:, :], bias[:, 1 + K, :], bias[:, 2 + K, :], ALU.add)
            dve.drain()
            dve.tensor_tensor(last_bias[:, :], last_bias[:, :], bias[:, 3 + K, :], ALU.add)
            dve.drain()
            dve.sem_inc(maps_up, 2)
            with dve.Fori(0, 32 // FILLS) as i:
                for first in range(0, FILLS, 2):
                    c = i * FILLS + first
                    for n in range(2):
                        dve.wait_ge(square_up, c + n + 1)
                        dve.transpose(square_t[n][:, :], square[n][:, :]).then_inc(square_turned, 1)
                    for n in range(2):
                        dve.wait_ge(along_up, c + n + 3)
                        dve.transpose(along_t[n][:, :, :].rearrange("p k l -> p (k l)"), along[n][:, :, :].rearrange("p k l -> p (k l)")).then_inc(turned, 1)
                    for n in range(2):
                        dve.wait_ge(maps_ps, c + n + 1 + FILLS)
                        dve.scalar_tensor_tensor(square_t[n][:, :], ps_s[n][:, 0:L], last_bias[:, bass.ds(c + n, 1)], square_t[n][:, :],
                                                 ALU.add, ALU.add)
                        dve.drain()
                        dve.tensor_copy(maps[:, :, bass.ds(c + n, 1), :].rearrange("p b a w -> p b (a w)"),
                                        square_t[n][:, :].rearrange("p (b w) -> p b w", b=B)).then_inc(maps_up, 1)
                        dve.drain()


def spread(slot, steps, apart=1):
    for _ in steps:
        yield slot
        slot += apart


def last_of(steps):
    for last in steps:
        pass
    return last


def token_norm_steps(dve, out, tile, stats, mv, var, inv, tmp):
    for t in range(NT):
        last = dve.bn_stats(stats[:, t, :], tile[:, t, :])
        if t % 4 == 3:
            yield last
    dve.drain()
    for t in range(NT):
        dve.bn_aggr(mv[:, t, :], stats[:, t, :])
    dve.drain()
    last = dve.tensor_scalar(var[:, :], mv[:, :, 1], 1e-5, None, ALU.add)
    yield last
    dve.drain()
    yield rsqrt(dve, inv[:, :], var[:, :], tmp[:, :])
    for t in range(NT):
        last = dve.tensor_scalar(out[:, t, :], tile[:, t, :], mv[:, t, 0:1], inv[:, t:t + 1], ALU.subtract, ALU.mult)
        if t % 4 == 3:
            yield last


def token_norm(*args):
    return last_of(token_norm_steps(*args))


def turn_tiles(pe, out, tiles, ident):
    for t in range(NT):
        last = pe.transpose(out[:, 128 * t:128 * t + 128], tiles[:, t, :], ident)
    return last


def gate_tiles(st_sb, E):
    t = {n: st_sb("gate_" + n, [128, NT, E]) for n in ("logits", "probs", "rank", "chosen", "score")}
    t.update({n: st_sb("gate_" + n, [128, NT]) for n in ("top", "total", "picked")})
    t.update({n: st_sb("gate_" + n, [128, NT * E, E]) for n in ("above", "same")})
    return t


def gate_shift(dve, t, E):
    dve.tensor_reduce(t["top"][:, :], t["logits"][:, :, :], axis=AX.X, op=ALU.max)
    dve.drain()
    return dve.tensor_tensor(t["probs"][:, :, :], t["logits"][:, :, :], t["top"][:, :].unsqueeze(2).broadcast_to((128, NT, E)), ALU.subtract)


def gate_choose_steps(dve, t, E, K, eps, tie):
    p, rank, chosen = t["probs"], t["rank"], t["chosen"]
    other = p[:, :, :].unsqueeze(2).broadcast_to((128, NT, E, E))
    own = p[:, :, :].unsqueeze(3).broadcast_to((128, NT, E, E))
    above = t["above"][:, :, :].rearrange("p (t e) f -> p t e f", t=NT)
    same = t["same"][:, :, :].rearrange("p (t e) f -> p t e f", t=NT)
    yield dve.tensor_tensor(above, other, own, ALU.is_gt)
    yield dve.tensor_tensor(same, other, own, ALU.is_equal)
    dve.tensor_reduce(t["total"][:, :], p[:, :, :], axis=AX.X, op=ALU.add)
    dve.drain()
    flat = t["same"][:, :, :].rearrange("p (t e) f -> p t (e f)", t=NT)
    yield dve.tensor_tensor(flat, flat, tie.unsqueeze(1).broadcast_to((128, NT, E * E)), ALU.mult)
    dve.drain()
    yield dve.tensor_tensor(t["above"][:, :, :], t["above"][:, :, :], t["same"][:, :, :], ALU.add)
    dve.drain()
    yield dve.tensor_reduce(rank[:, :, :], above, axis=AX.X, op=ALU.add)
    dve.drain()
    dve.tensor_scalar(chosen[:, :, :], rank[:, :, :], float(K), None, ALU.is_lt)
    dve.drain()
    dve.tensor_tensor(t["score"][:, :, :], p[:, :, :], chosen[:, :, :], ALU.mult)
    dve.drain()
    yield dve.tensor_reduce(t["picked"][:, :], t["score"][:, :, :], axis=AX.X, op=ALU.add)
    dve.drain()
    dve.scalar_tensor_tensor(t["picked"][:, :], t["total"][:, :], eps, t["picked"][:, :], ALU.mult, ALU.add)
    dve.drain()
    dve.reciprocal(t["picked"][:, :], t["picked"][:, :])
    dve.drain()
    yield dve.tensor_tensor(t["score"][:, :, :], t["score"][:, :, :], t["picked"][:, :].unsqueeze(2).broadcast_to((128, NT, E)), ALU.mult)


def gate_choose(*args):
    return last_of(gate_choose_steps(*args))


def landmark_and_gelu_phase(nc, ctx, B, io, const, maps, gn2, x1_dram, tok_dram):
    with ExitStack() as st:
        def sb(name, shape, dt=F32):
            return st.enter_context(nc.sbuf_tensor("n_" + name, shape, dt))

        def sem(name):
            return ctx.enter_context(nc.semaphore("n_" + name))

        LM = 16
        STEP = N // LM
        NEWTON = 6
        SCALE = float(D) ** -0.5
        E, K, F = 8, 2, 512
        FT = F // 128
        SLOTS = 8 * (E + 1)
        LATE = SLOTS
        y_in, yt = sb("y_in", [128, 32, HW]), sb("yt", [128, N])
        x1, u = sb("x1", [128, N]), sb("u", [128, N])
        w3, wqkv, wproj = sb("w3", [128, C]), sb("wqkv", [128, 3 * C]), sb("wproj", [128, C])
        b3, qb, kb = sb("b3", [128, 1]), sb("qb", [128, 1]), sb("kb", [128, 1])
        vb, pb = sb("vb", [128, C]), sb("pb", [128, C])
        tok_next, tok = sb("tok_next", [128, NT, C]), sb("tok", [128, NT, C])
        xln = sb("xln", [128, NT, C])
        xt, qt, kt = sb("xt", [128, N]), sb("qt", [128, N]), sb("kt", [128, N])
        v = sb("v", [128, NT, C])
        q_lm, k_lm = sb("q_lm", [128, C]), sb("k_lm", [128, C])
        k1, e3 = sb("k1", [128, NT, C]), sb("e3", [128, NT, 128])
        k1t, e3t = yt, u
        max1, sum1 = sb("max1", [128, NT * HEADS]), sb("sum1", [128, NT * HEADS])
        max3, sum3 = sb("max3", [128, 1]), sb("sum3", [128, 1])
        max2, sum2, e2, e2q = sb("max2", [128, 1]), sb("sum2", [128, 1]), sb("e2", [128, LM]), sb("e2q", [128, LM])
        fro = sb("fro", [128, 1])
        m2, m2t = sb("m2", [128, 128]), sb("m2t", [128, 128])
        z, zt, mz = sb("z", [128, 128]), sb("zt", [128, 128]), sb("mz", [128, 128])
        kv, mixed, mixed_p = sb("kv", [128, 128]), sb("mixed", [128, 128]), sb("mixed_p", [128, 128])
        stats, mv = sb("stats", [128, NT, 6]), sb("mv", [128, NT, 2])
        var, inv, tmp = sb("var", [128, NT]), sb("inv", [128, NT]), sb("tmp", [128, NT])
        gate = gate_tiles(sb, E)
        score_t = sb("score_t", [E, N])
        xt_now, score_now = sb("xt_now", [128, N]), sb("score_now", [128, NT, E])
        hidden = sb("hidden", [128, 2, FT, N])
        wg, w1, w2 = sb("wg", [128, E]), sb("w1", [128, E, F]), sb("w2", [128, E, FT, C])
        b1, b2, tie = sb("b1", [128, E, FT]), sb("b2", [E, C]), sb("tie", [128, E * E])
        ps_h = [st.enter_context(nc.psum_tensor(f"n_ps_h{n}", [128, 512], F32)) for n in range(2)]
        ps_y = [st.enter_context(nc.psum_tensor(f"n_ps_y{n}", [128, 512], F32)) for n in range(2)]
        pa, pb_ = [st.enter_context(nc.psum_tensor(f"n_ps_f{n}", [128, N], F32)) for n in range(2)]
        events = ("x1_in y_in y_turned gate_ps x2_up tok_ps tok_up ln_up lnt_ps xt_up qk_ps v_ps qk_up v_up lm_up s_ps xt_handed s3_ps "
                  "d_up e_up m2_up norm_ps fro_in z0_up k1_up turned_ps turned_up max3_up e3_up kv_ps kv_up mixed_ps mixed_up attn_ps attn_up "
                  "router_ps shift_up exp_up score_up scores_ps st_up handed tok_done tok_stored")
        S = {name: sem(name) for name in events.split()}
        mz_ps, mz_up, znew_ps, z_up = sem("mz_ps"), sem("mz_up"), sem("znew_ps"), sem("z_up")
        params_in, hidden_ps, hidden_up, y_ps, y_added = sem("params_in"), sem("hidden_ps"), sem("hidden_up"), sem("y_ps"), sem("y_added")
        row = lambda ap, n: ap.rearrange("c b -> b c").broadcast_to((128, n))
        params = [(w3[:, :], io["L1_w3T"]), (wqkv[:, :], io["L2_qkvT"]), (wproj[:, :], io["L2_projT"]), (b3[:, :], io["L1_conv_b3"]),
                  (qb[:, :], io["L2_attn_bqkv"][0:C, :]), (kb[:, :], io["L2_attn_bqkv"][C:2 * C, :]),
                  (vb[:, :], row(io["L2_attn_bqkv"][2 * C:3 * C, :], C)), (pb[:, :], row(io["L2_attn_bproj"], C)),
                  (wg[:, :], io["L2_ffn_Wg"]), (w1[:, :, :], io["L2_ffn_W1"].rearrange("e d f -> d e f")),
                  (b2[:, :], io["L2_ffn_b2"]), (tie[:, :], io["const_tie8"])]
        params += [(w2[:, e, :, :], io["L2_ffn_W2"][e, :, :].rearrange("(t f) d -> f t d", t=FT)) for e in range(E)]
        params += [(b1[:, e, t:t + 1], io["L2_ffn_b1"][e:e + 1, 128 * t:128 * t + 128].rearrange("e f -> f e")) for e in range(E) for t in range(FT)]
        H_PER, Y_PER = 8 * E, 2 * E
        block = st.enter_context(nc.Block())

        def due(front, slot):
            while front and front[1] <= slot:
                front[1] = next(front[0], LATE + 1)

        @block.sync
        def _(sp):
            for dst, src in params:
                sp.dma_start(dst, src).then_inc(params_in, 16)

            def load(i):
                sp.dma_start(y_in[:, :, :].rearrange("p c w -> p (c w)"), maps[:, bass.ds(i, 1), :, :].rearrange("p a c w -> p (a c w)")).then_inc(S["y_in"], 16)
                sp.dma_start(x1[:, :], x1_dram[bass.ds(i, 1), :, :].rearrange("a c n -> (a c) n")).then_inc(S["x1_in"], 16)

            def store(i):
                sp.wait_ge(S["tok_done"], i + 1)
                sp.dma_start(tok_dram[bass.ds(i, 1), :, :].rearrange("a p n -> (a p) n"), tok[:, :, :].rearrange("p t c -> p (t c)")).then_inc(S["tok_stored"], 16)

            load(0)
            with sp.Fori(0, B - 1) as i:
                sp.wait_ge(S["x2_up"], i + 1)
                load(i + 1)
                store(i)
            store(B - 1)
            sp.wait_ge(S["tok_stored"], 16 * B + 16)

        @block.vector
        def _(dve):
            b16 = const["block16"].rearrange("p (h l) -> p h l", h=HEADS)

            def front(i):
                yield 0
                dve.wait_ge(S["y_in"], i * 16 + 16)
                dve.transpose(yt[:, :].rearrange("p (h w) -> p w h", h=HW), y_in[:, :, :].rearrange("p c w -> p w c")).then_inc(S["y_turned"], 1)
                dve.wait_ge(S["x1_in"], i * 16 + 16)
                dve.tensor_scalar(u[:, :], x1[:, :], gn2[:, 0, bass.ds(i, 1)], gn2[:, 1, bass.ds(i, 1)], ALU.mult, ALU.add)
                yield 4
                dve.drain()
                dve.wait_ge(S["gate_ps"], i + 1)
                dve.scalar_tensor_tensor(u[:, :], pa[:, :], b3[:, :], u[:, :], ALU.add, ALU.mult)
                dve.drain()
                dve.tensor_tensor(u[:, :], u[:, :], x1[:, :], ALU.add).then_inc(S["x2_up"], 1)
                yield 9
                dve.wait_ge(S["tok_up"], i + 1)
                token_norm(dve, xln, tok_next, stats, mv, var, inv, tmp).then_inc(S["ln_up"], 1)
                yield 20
                for src, dst, up in ((qt, q_lm, 1), (kt, k_lm, 2)):
                    dve.wait_ge(S["qk_up"], i * 2 + up)
                    last = dve.tensor_tensor(dst[:, :].rearrange("p (h l) -> p h l", h=HEADS), b16,
                                             src[:, 0:N:STEP].unsqueeze(1).broadcast_to((128, HEADS, LM)), ALU.mult)
                last.then_inc(S["lm_up"], 1)
                yield 21
                dve.wait_ge(S["v_ps"], i + 1)
                dve.tensor_tensor(v[:, :, :], pb_[:, :].rearrange("p (t c) -> p t c", t=NT),
                                  vb[:, :].unsqueeze(1).broadcast_to((128, NT, C)), ALU.add).then_inc(S["v_up"], 1)
                yield 23
                dve.wait_ge(S["s_ps"], i * 2 + 1)
                dve.tensor_reduce(max2[:, :], pa[:, 0:LM], axis=AX.X, op=ALU.max)
                dve.drain()
                dve.tensor_scalar(e2[:, :], pa[:, 0:LM], max2[:, :], None, ALU.subtract).then_inc(S["d_up"], 1)
                yield 25
                s1 = pb_[:, :].rearrange("p (g l) -> p g l", l=LM)
                k1v = k1[:, :, :].rearrange("p t (h l) -> p (t h) l", l=LM)
                dve.wait_ge(S["s_ps"], i * 2 + 2)
                dve.tensor_reduce(max1[:, :], s1, axis=AX.X, op=ALU.max)
                dve.drain()
                dve.tensor_tensor(k1v, s1, max1[:, :].unsqueeze(2).broadcast_to((128, NT * HEADS, LM)), ALU.subtract).then_inc(S["d_up"], 1)
                yield 27
                dve.wait_ge(S["e_up"], i * 2 + 1)
                dve.reciprocal(sum2[:, :], sum2[:, :])
                dve.drain()
                dve.tensor_scalar(e2[:, :], e2[:, :], sum2[:, :], None, ALU.mult)
                dve.drain()
                dve.tensor_tensor(m2[:, :].rearrange("p (h l) -> p h l", h=HEADS), b16,
                                  e2[:, :].unsqueeze(1).broadcast_to((128, HEADS, LM)), ALU.mult).then_inc(S["m2_up"], 1)
                dve.tensor_tensor(e2q[:, :], e2[:, :], e2[:, :], ALU.mult)
                dve.drain()
                dve.tensor_reduce(max2[:, :], e2q[:, :], axis=AX.X, op=ALU.add).then_inc(S["fro_in"], 1)
                yield 29
                dve.wait_ge(S["norm_ps"], i * 2 + 2)
                dve.wait_ge(S["norm_ps"], i * 2 + 1)
                dve.tensor_scalar(fro[:, :], pa[:, 0:1], 1e-12, None, ALU.max)
                dve.tensor_copy(m2t[:, :], pa[:, 512:640])
                dve.drain()
                dve.reciprocal(fro[:, :], fro[:, :])
                dve.drain()
                dve.tensor_scalar(z[:, :], m2t[:, :], fro[:, :], None, ALU.mult)
                dve.tensor_scalar(zt[:, :], m2[:, :], fro[:, :], None, ALU.mult).then_inc(S["z0_up"], 1)
                for it in range(NEWTON):
                    yield 30 + 2 * it
                    dve.drain()
                    dve.wait_ge(mz_ps, i * NEWTON + it + 1)
                    dve.tensor_copy(mz[:, :], pa[:, 0:128]).then_inc(mz_up, 1)
                    yield 31 + 2 * it
                    dve.wait_ge(znew_ps, i * NEWTON + it + 1)
                    dve.scalar_tensor_tensor(z[:, :], z[:, :], 2.0, pa[:, 512:640], ALU.mult, ALU.subtract)
                    dve.scalar_tensor_tensor(zt[:, :], zt[:, :], 2.0, pa[:, 640:768], ALU.mult, ALU.subtract).then_inc(z_up, 1)
                    dve.drain()
                    if it == 1:
                        dve.wait_ge(S["s3_ps"], i + 1)
                        dve.tensor_reduce(max3[:, :], pb_[:, :], axis=AX.X, op=ALU.max)
                        dve.drain()
                        dve.tensor_scalar(max3[:, :], max3[:, :], -SCALE, None, ALU.mult).then_inc(S["max3_up"], 1)
                    if it == 2:
                        dve.wait_ge(S["e_up"], i * 2 + 2)
                        dve.tensor_reduce(sum1[:, :], k1v, axis=AX.X, op=ALU.add)
                        dve.drain()
                        dve.reciprocal(sum1[:, :], sum1[:, :])
                        dve.drain()
                        dve.tensor_tensor(k1v, k1v, sum1[:, :].unsqueeze(2).broadcast_to((128, NT * HEADS, LM)), ALU.mult).then_inc(S["k1_up"], 1)
                yield 43
                dve.wait_ge(S["e3_up"], i + 1)
                dve.reciprocal(sum3[:, :], sum3[:, :])
                dve.drain()
                dve.wait_ge(S["kv_ps"], i + 1)
                dve.scalar_tensor_tensor(kv[:, :], pb_[:, 0:128], sum3[:, :], const["block16"], ALU.mult, ALU.mult).then_inc(S["kv_up"], 1)
                yield 45
                dve.wait_ge(S["mixed_ps"], i * 2 + 1)
                dve.tensor_copy(mixed[:, :], pa[:, 0:128]).then_inc(S["mixed_up"], 1)
                dve.tensor_tensor(tok_next[:, :, :], tok_next[:, :, :], pb[:, :].unsqueeze(1).broadcast_to((128, NT, C)), ALU.add)
                yield 47
                dve.drain()
                dve.wait_ge(S["mixed_ps"], i * 2 + 2)
                dve.tensor_copy(mixed_p[:, :], pa[:, 512:640]).then_inc(S["mixed_up"], 1)
                yield 49
                dve.wait_ge(S["attn_ps"], i + 1)
                dve.tensor_tensor(tok_next[:, :, :], tok_next[:, :, :], pb_[:, :].rearrange("p (t c) -> p t c", t=NT), ALU.add).then_inc(S["attn_up"], 1)
                dve.drain()
                token_norm(dve, xln, tok_next, stats, mv, var, inv, tmp).then_inc(S["ln_up"], 1)
                yield 58
                dve.wait_ge(S["router_ps"], i + 1)
                dve.tensor_copy(gate["logits"][:, :, :], pb_[:, 0:NT * E].rearrange("p (t e) -> p t e", t=NT))
                dve.drain()
                gate_shift(dve, gate, E).then_inc(S["shift_up"], 1)
                yield 60
                dve.wait_ge(S["exp_up"], i + 1)
                gate_choose(dve, gate, E, K, 1e-6, tie[:, :]).then_inc(S["score_up"], 1)
                yield 66
                dve.wait_ge(S["scores_ps"], i * 2 + 1)
                dve.tensor_copy(score_t[:, :], pa[0:E, :]).then_inc(S["st_up"], 1)
                yield 69
                dve.drain()
                dve.wait_ge(S["scores_ps"], i * 2 + 2)
                dve.tensor_tensor(tok_next[:, :, :], tok_next[:, :, :], pb_[:, :].rearrange("p (t c) -> p t c", t=NT), ALU.add)

            def hand_over(i):
                dve.tensor_copy(score_now[:, :, :], gate["score"][:, :, :]).then_inc(S["handed"], 1)
                dve.wait_ge(S["tok_stored"], i * 16 + 16)
                dve.tensor_copy(tok[:, :, :], tok_next[:, :, :])
                dve.drain()

            def experts(i, front):
                for slot in range(SLOTS):
                    if slot >= 8 and slot % 4 == 3:
                        e, k = slot // 8 - 1, slot // 4 % 2
                        dve.wait_ge(y_ps, i * Y_PER + 2 * e + k + 1)
                        for t in range(4):
                            tile = tok[:, 4 * k + t, :]
                            last = dve.scalar_tensor_tensor(tile, ps_y[k][:, 128 * t:128 * t + 128], score_now[:, 4 * k + t, e:e + 1], tile,
                                                            ALU.mult, ALU.add)
                        last.then_inc(y_added, 1)
                        dve.drain()
                    due(front, slot)
                due(front, LATE)
                dve.drain().then_inc(S["tok_done"], 1)

            dve.wait_ge(params_in, 16 * len(params))
            dve.sem_inc(S["tok_stored"], 16)
            due([front(0), -1], LATE)
            dve.drain()
            hand_over(0)
            with dve.Fori(0, B - 1) as i:
                experts(i, [front(i + 1), -1])
                hand_over(i + 1)
            experts(B - 1, None)

        @block.scalar
        def _(act):
            def front(i):
                yield 8
                act.wait_ge(S["tok_ps"], i + 1)
                act.activation(tok_next[:, :, :].rearrange("p t c -> p (t c)"), pb_[:, :], ACT.Copy).then_inc(S["tok_up"], 1)
                yield 15
                act.wait_ge(S["lnt_ps"], i * 2 + 1)
                act.activation(xt[:, :], pa[:, :], ACT.Copy).then_inc(S["xt_up"], 1)
                yield 18
                act.wait_ge(S["qk_ps"], i * 2 + 1)
                act.activation(qt[:, :], pb_[:, :], ACT.Identity, bias=qb[:, :]).then_inc(S["qk_up"], 1)
                yield 19
                act.wait_ge(S["qk_ps"], i * 2 + 2)
                act.activation(kt[:, :], pa[:, :], ACT.Identity, bias=kb[:, :]).then_inc(S["qk_up"], 1)
                yield 26
                act.wait_ge(S["d_up"], i * 2 + 1)
                act.activation(e2[:, :], e2[:, :], ACT.Exp, scale=SCALE, accum_out=sum2[:, :]).then_inc(S["e_up"], 1)
                act.wait_ge(S["d_up"], i * 2 + 2)
                act.activation(k1[:, :, :], k1[:, :, :], ACT.Exp, scale=SCALE).then_inc(S["e_up"], 1)
                yield 35
                act.wait_ge(S["max3_up"], i + 1)
                act.activation(e3[:, :, :].rearrange("p t n -> p (t n)"), pb_[:, :], ACT.Exp, scale=SCALE, bias=max3[:, :], accum_out=sum3[:, :]).then_inc(S["e3_up"], 1)
                yield 37
                act.wait_ge(S["turned_ps"], i * 2 + 1)
                act.activation(k1t[:, :], pb_[:, :], ACT.Copy).then_inc(S["turned_up"], 1)
                yield 40
                act.wait_ge(S["turned_ps"], i * 2 + 2)
                act.activation(e3t[:, :], pb_[:, :], ACT.Copy).then_inc(S["turned_up"], 1)
                yield 55
                act.wait_ge(S["lnt_ps"], i * 2 + 2)
                act.activation(xt[:, :], pa[:, :], ACT.Copy).then_inc(S["xt_up"], 1)
                yield 59
                act.wait_ge(S["shift_up"], i + 1)
                act.activation(gate["probs"][:, :, :], gate["probs"][:, :, :], ACT.Exp).then_inc(S["exp_up"], 1)

            def experts(i, front):
                for slot in range(SLOTS):
                    if slot < H_PER:
                        e, k, f = slot // 8, slot // 4 % 2, slot % 4
                        act.wait_ge(hidden_ps, i * H_PER + slot + 1)
                        act.activation(hidden[:, e % 2, f, 512 * k:512 * k + 512], ps_h[slot % 2][:, :], ACT.Gelu, bias=b1[:, e, f:f + 1]).then_inc(hidden_up, 1)
                    due(front, slot)
                    if slot == H_PER and front:
                        act.activation(xt_now[:, :], xt[:, :], ACT.Copy).then_inc(S["xt_handed"], 1)
                due(front, LATE)

            act.wait_ge(params_in, 16 * len(params))
            due([front(0), -1], LATE)
            act.activation(xt_now[:, :], xt[:, :], ACT.Copy).then_inc(S["xt_handed"], 1)
            with act.Fori(0, B - 1) as i:
                experts(i, [front(i + 1), -1])
            experts(B - 1, None)

        @block.tensor
        def _(pe):
            ident = const["ident"]

            def wide(out, w, src):
                for k in range(HALVES):
                    last = pe.matmul(out[:, 512 * k:512 * k + 512], w, src[:, 512 * k:512 * k + 512], start=True, stop=True)
                return last

            def front(i):
                yield 2
                pe.wait_ge(S["y_turned"], i + 1)
                wide(pa, w3[:, :], yt).then_inc(S["gate_ps"], 1)
                yield 7
                pe.wait_ge(S["x2_up"], i + 1)
                for t in range(NT):
                    last = pe.transpose(pb_[:, 128 * t:128 * t + 128], u[:, 128 * t:128 * t + 128], ident)
                last.then_inc(S["tok_ps"], 1)
                yield 14
                pe.wait_ge(S["ln_up"], i * 2 + 1)
                turn_tiles(pe, pa, xln, ident).then_inc(S["lnt_ps"], 1)
                yield 16
                pe.wait_ge(S["xt_up"], i * 2 + 1)
                wide(pb_, wqkv[:, 0:C], xt).then_inc(S["qk_ps"], 1)
                yield 17
                wide(pa, wqkv[:, C:2 * C], xt).then_inc(S["qk_ps"], 1)
                yield 19
                pe.wait_ge(S["qk_up"], i * 2 + 1)
                for t in range(NT):
                    last = pe.matmul(pb_[:, 128 * t:128 * t + 128], xt[:, 128 * t:128 * t + 128], wqkv[:, 2 * C:3 * C], start=True, stop=True)
                last.then_inc(S["v_ps"], 1)
                yield 22
                pe.wait_ge(S["lm_up"], i + 1)
                pe.matmul(pa[:, 0:LM], q_lm[:, :], kt[:, 0:N:STEP], start=True, stop=True).then_inc(S["s_ps"], 1)
                yield 24
                pe.wait_ge(S["v_up"], i + 1)
                for t in range(NT):
                    last = pe.matmul(pb_[:, 128 * t:128 * t + 128], qt[:, 128 * t:128 * t + 128], k_lm[:, :], start=True, stop=True)
                last.then_inc(S["s_ps"], 1)
                yield 28
                pe.wait_ge(S["m2_up"], i + 1)
                pe.transpose(pa[:, 512:640], m2[:, :], ident).then_inc(S["norm_ps"], 1)
                pe.wait_ge(S["fro_in"], i + 1)
                pe.matmul(pa[:, 0:1], const["block16"], max2[:, :], start=True, stop=True).then_inc(S["norm_ps"], 1)
                for it in range(NEWTON):
                    yield 30 + 2 * it
                    if it == 0:
                        pe.wait_ge(S["z0_up"], i + 1)
                    else:
                        pe.wait_ge(z_up, i * NEWTON + it)
                    pe.matmul(pa[:, 0:128], m2t[:, :], z[:, :], start=True, stop=True).then_inc(mz_ps, 1)
                    yield 31 + 2 * it
                    pe.wait_ge(mz_up, i * NEWTON + it + 1)
                    pe.matmul(pa[:, 512:640], zt[:, :], mz[:, :], start=True, stop=True)
                    pe.matmul(pa[:, 640:768], mz[:, :], zt[:, :], start=True, stop=True).then_inc(znew_ps, 1)
                    if it == 0:
                        pe.wait_ge(S["d_up"], i * 2 + 2)
                        wide(pb_, q_lm[:, :], kt).then_inc(S["s3_ps"], 1)
                    if it == 3:
                        pe.wait_ge(S["e3_up"], i + 1)
                        pe.wait_ge(S["k1_up"], i + 1)
                        turn_tiles(pe, pb_, k1, ident).then_inc(S["turned_ps"], 1)
                    if it == 4:
                        pe.wait_ge(S["turned_up"], i * 2 + 1)
                        turn_tiles(pe, pb_, e3, ident).then_inc(S["turned_ps"], 1)
                yield 42
                pe.wait_ge(S["turned_up"], i * 2 + 2)
                for t in range(NT):
                    last = pe.matmul(pb_[:, 0:128], e3t[:, 128 * t:128 * t + 128], v[:, t, :], start=(t == 0), stop=(t == NT - 1))
                last.then_inc(S["kv_ps"], 1)
                yield 44
                pe.wait_ge(z_up, i * NEWTON + NEWTON)
                pe.wait_ge(S["kv_up"], i + 1)
                pe.matmul(pa[:, 0:128], kv[:, :], zt[:, :], start=True, stop=True).then_inc(S["mixed_ps"], 1)
                yield 46
                pe.wait_ge(S["mixed_up"], i * 2 + 1)
                pe.matmul(pa[:, 512:640], mixed[:, :], wproj[:, :], start=True, stop=True).then_inc(S["mixed_ps"], 1)
                yield 48
                pe.wait_ge(S["mixed_up"], i * 2 + 2)
                for t in range(NT):
                    last = pe.matmul(pb_[:, 128 * t:128 * t + 128], k1t[:, 128 * t:128 * t + 128], mixed_p[:, :], start=True, stop=True)
                last.then_inc(S["attn_ps"], 1)
                yield 54
                pe.wait_ge(S["ln_up"], i * 2 + 2)
                turn_tiles(pe, pa, xln, ident).then_inc(S["lnt_ps"], 1)
                yield 57
                pe.wait_ge(S["xt_up"], i * 2 + 2)
                for t in range(NT):
                    last = pe.matmul(pb_[:, E * t:E * t + E], xt[:, 128 * t:128 * t + 128], wg[:, :], start=True, stop=True)
                last.then_inc(S["router_ps"], 1)
                yield 65
                pe.wait_ge(S["score_up"], i + 1)
                for t in range(NT):
                    last = pe.transpose(pa[0:E, 128 * t:128 * t + 128], gate["score"][:, t, :], ident)
                last.then_inc(S["scores_ps"], 1)
                yield 68
                pe.wait_ge(S["st_up"], i + 1)
                for t in range(NT):
                    last = pe.matmul(pb_[:, 128 * t:128 * t + 128], score_t[:, 128 * t:128 * t + 128], b2[:, :], start=True, stop=True)
                last.then_inc(S["scores_ps"], 1)

            def experts(i, front):
                pe.wait_ge(S["xt_handed"], i + 1)
                for slot in range(SLOTS):
                    e, k, f = slot // 8, slot // 4 % 2, slot % 4
                    if slot < H_PER:
                        if slot >= 2:
                            pe.wait_ge(hidden_up, i * H_PER + slot - 1)
                        pe.matmul(ps_h[slot % 2][:, :], w1[:, e, 128 * f:128 * f + 128], xt_now[:, 512 * k:512 * k + 512],
                                  start=True, stop=True).then_inc(hidden_ps, 1)
                    if slot >= 8:
                        e, t = e - 1, slot % 8
                        if e == 0 and t == 0:
                            pe.wait_ge(S["handed"], i + 1)
                        if t == 0 or t == 4:
                            pe.wait_ge(hidden_up, i * H_PER + 8 * e + 4 + t)
                            if e:
                                pe.wait_ge(y_added, i * Y_PER + 2 * (e - 1) + k + 1)
                        for f in range(FT):
                            last = pe.matmul(ps_y[k][:, 128 * f_col(t):128 * f_col(t) + 128], hidden[:, e % 2, f, 128 * t:128 * t + 128],
                                             w2[:, e, f, :], start=(f == 0), stop=(f == FT - 1))
                        if t % 4 == 3:
                            last.then_inc(y_ps, 1)
                    due(front, slot)
                due(front, LATE)

            def f_col(t):
                return t % 4

            pe.wait_ge(params_in, 16 * len(params))
            due([front(0), -1], LATE)
            with pe.Fori(0, B - 1) as i:
                experts(i, [front(i + 1), -1])
            experts(B - 1, None)


def dense_attention_and_silu_phase(nc, ctx, B, io, const, tok_dram, out):
    with ExitStack() as st:
        def sb(name, shape, dt=F32):
            return st.enter_context(nc.sbuf_tensor("e_" + name, shape, dt))

        def sem(name):
            return ctx.enter_context(nc.semaphore("e_" + name))

        E, K, F = 16, 6, 64
        PAIRS = E * F // 128
        UNITS = PAIRS + 1
        STEPS = HALVES * UNITS
        SLOTS = 3 * STEPS
        LATE = SLOTS
        FIRST, PER_TILE = 15, 3
        TURN = 9
        COUNT = 4
        AFTER_TILES = lambda tiles: FIRST + PER_TILE * tiles + 2
        PIECES = 3
        CAP = max(1, int(B * N * K * 2.0 / E))
        tokens = sb("tokens", [128, B, NT, C])
        xln, xt, qt = sb("xln", [128, NT, C]), sb("xt", [128, N]), sb("qt", [128, N])
        wq, bq = sb("wq", [128, C]), sb("bq", [128, 1])
        negmax, sums = sb("negmax", [128, NT]), sb("sums", [128, NT])
        probs, probs_t = sb("probs", [128, 2, N]), sb("probs_t", [128, 2, NT, 128])
        norm = (sb("stats", [128, NT, 6]), sb("mv", [128, NT, 2]), sb("var", [128, NT]), sb("inv", [128, NT]), sb("tmp", [128, NT]))
        xln2, xt2 = sb("xln2", [128, NT, C]), sb("xt2", [128, N])
        gate = gate_tiles(sb, E)
        chosen_before = sb("chosen_before", [128, NT + 1, E])
        score_bf = sb("score_bf", [128, NT, E], BF16)
        score_pieces = sb("score_pieces", [128, NT, 128])
        score_t = sb("score_t", [PIECES * E, N], BF16)
        wr, rbias, tie = sb("wr", [128, E]), sb("rbias", [128, E]), sb("tie", [128, E * E])
        before, ones = sb("before", [128, 128]), sb("ones", [128, 128])
        xt_now, score_now, tile_in = sb("xt_now", [128, N]), sb("score_now", [PIECES * E, N], BF16), sb("tile_in", [128, NT, C])
        wg, wu, wd = sb("wg", [128, UNITS, 128]), sb("wu", [128, UNITS, 128]), sb("wd", [128, UNITS, C])
        pairsel_in, pairsel = sb("pairsel_in", [PIECES * E, PAIRS * 128]), sb("pairsel", [PIECES * E, PAIRS * 128], BF16)
        act_up, mixed = sb("act_up", [128, 2, 512]), sb("mixed", [128, 2, 512])
        result = sb("result", [128, 2, 512])
        ps_g, ps_u, ps_b, ps_o = (st.enter_context(nc.psum_tensor("e_ps_" + x, [128, 512], F32)) for x in "gubo")
        pa, pb = (st.enter_context(nc.psum_tensor("e_ps_f" + x, [128, N], F32)) for x in "ab")
        events = ("ln_up lnt_ps xt_up q_ps q_up s_ps max_up exp_up turned_ps turned_v turned_a out_ps added ln2_up "
                  "lnt2_ps xt2_up router_ps shift_up gexp_up chosen_up count_ps count_read score_up st_ps st_up "
                  "xt_handed score_handed tile_handed")
        S = {name: sem(name) for name in events.split()}
        params_in, tok_in, result_ps, result_up = sem("params_in"), sem("tok_in"), sem("result_ps"), sem("result_up")
        g_ps, u_ps, b_ps, silu_up, u_read, mixed_up = (sem(x) for x in "g_ps u_ps b_ps silu_up u_read mixed_up".split())
        stored = [sem(f"stored{n}") for n in range(2)]
        row = lambda ap, n: ap.rearrange("c b -> b c").broadcast_to((128, n))
        params = [(wq[:, :], io["L3_attn_W"]), (bq[:, :], io["L3_attn_b"]),
                  (wr[:, :], io["L3_routerT"]), (rbias[:, :], row(io["L3_ffn_bias"], E)),
                  (tie[:, :], io["const_tie16"]), (before[:, :], io["const_before"]), (ones[:, :], io["const_ones"]),
                  (pairsel_in[:, :], io["const_pairsel"]),
                  (wg[:, 0:PAIRS, :], io["L3_gT"].rearrange("d (q f) -> d q f", q=PAIRS)), (wg[:, PAIRS, :], io["L3_sgT"]),
                  (wu[:, 0:PAIRS, :], io["L3_uT"].rearrange("d (q f) -> d q f", q=PAIRS)), (wu[:, PAIRS, :], io["L3_suT"]),
                  (wd[:, 0:PAIRS, :], io["L3_dT"].rearrange("(q f) d -> f q d", q=PAIRS)), (wd[:, PAIRS, :], io["L3_sdT"])]
        block = st.enter_context(nc.Block())

        def due(stage, slot):
            while stage and stage[1] <= slot:
                stage[1] = next(stage[0], LATE + 1)

        def alone(stage):
            due([stage, -1], LATE)

        def pipeline(engine, attention, choice, experts, hand_over=None):
            alone(attention(0))
            stages = [[choice(0, True), -1], [attention(1), -1]]
            for slot in range(LATE + 1):
                for stage in stages:
                    due(stage, slot)
            if hand_over:
                hand_over(0)
            experts_and_stages = lambda i, stages: experts(i, [[stage, -1] for stage in stages])
            with engine.Fori(0, B - 2) as i:
                experts_and_stages(i, [choice(i + 1, True), attention(i + 2)])
            experts_and_stages(B - 2, [choice(B - 1, False)])
            experts_and_stages(B - 1, [])

        def started(i):
            return not isinstance(i, int) or i > 0

        @block.sync
        def _(sp):
            for dst, src in params:
                sp.dma_start(dst, src).then_inc(params_in, 16)
            sp.sem_inc(tok_in, 16)
            with sp.Fori(0, B) as i:
                sp.wait_ge(tok_in, i * 16 + 16)
                sp.dma_start(tokens[:, bass.ds(i, 1), :, :].rearrange("p a t c -> p (a t c)"), tok_dram[bass.ds(i, 1), :, :].rearrange("a p n -> (a p) n")).then_inc(tok_in, 16)
            with sp.Fori(0, B) as i:
                for k in range(HALVES):
                    sp.wait_ge(result_up, i * HALVES + k + 2)
                    sp.dma_start(out[bass.ds(i, 1), :, 512 * k:512 * k + 512].rearrange("a c n -> (a c) n"), result[:, k, :]).then_inc(stored[k], 16)
            for k in range(HALVES):
                sp.wait_ge(stored[k], 16 * B + 16)

        @block.vector
        def _(dve):
            def tiles_of(i):
                return tokens[:, bass.ds(i, 1), :, :].rearrange("p a t c -> p (a t) c")

            def attention(i):
                yield 0
                dve.wait_ge(tok_in, i * 16 + 32)
                yield from spread(0, token_norm_steps(dve, xln, tiles_of(i), *norm))
                dve.drain().then_inc(S["ln_up"], 1)
                for t in range(NT + 1):
                    yield FIRST + PER_TILE * t
                    if t:
                        dve.wait_ge(S["turned_ps"], i * NT + t)
                        dve.tensor_copy(probs_t[:, (t - 1) % 2, 0:4, :].rearrange("p m n -> p (m n)"), pb[:, 0:512]).then_inc(S["turned_v"], 1)
                    if t < NT:
                        dve.wait_ge(S["s_ps"], i * NT + t + 1)
                        dve.tensor_reduce(negmax[:, t:t + 1], pa[:, :], axis=AX.X, op=ALU.max, negate=True).then_inc(S["max_up"], 1)
                    yield FIRST + PER_TILE * t + 1
                    if t:
                        dve.wait_ge(S["out_ps"], i * NT + t)
                        dve.reciprocal(sums[:, t - 1:t], sums[:, t - 1:t])
                        dve.drain()
                        tile = tokens[:, bass.ds(i, 1), t - 1, :].rearrange("p a c -> p (a c)")
                        dve.scalar_tensor_tensor(tile, pb[:, 0:C], sums[:, t - 1:t], tile, ALU.mult, ALU.add).then_inc(S["added"], 1)
                        dve.drain()
                yield from spread(FIRST + PER_TILE * NT + 1, token_norm_steps(dve, xln2, tiles_of(i), *norm))
                dve.drain().then_inc(S["ln2_up"], 1)

            def choice(i, beside_attention):
                yield 4
                dve.wait_ge(S["router_ps"], i + 1)
                dve.tensor_tensor(gate["logits"][:, :, :], pb[:, 0:NT * E].rearrange("p (t e) -> p t e", t=NT),
                                  rbias[:, :].unsqueeze(1).broadcast_to((128, NT, E)), ALU.add)
                dve.drain()
                gate_shift(dve, gate, E).then_inc(S["shift_up"], 1)
                yield 7
                dve.wait_ge(S["gexp_up"], i + 1)
                yield from spread(7, gate_choose_steps(dve, gate, E, K, 1e-9, tie[:, :]), 3)
                dve.drain()
                for t in range(NT):
                    dve.tensor_tensor(chosen_before[:, t + 1, :], chosen_before[:, t, :], gate["chosen"][:, t, :], ALU.add)
                    dve.drain()
                dve.drain().then_inc(S["chosen_up"], 1)
                yield AFTER_TILES(COUNT)
                dve.wait_ge(S["count_ps"], i + 1)
                dve.tensor_copy(chosen_before[:, 0, :], chosen_before[:, NT, :])
                dve.scalar_tensor_tensor(gate["score"][:, :, :], pb[:, 0:NT * E].rearrange("p (t e) -> p t e", t=NT), float(CAP), gate["score"][:, :, :],
                                         ALU.is_lt, ALU.mult).then_inc(S["count_read"], 1)
                for p in range(PIECES):
                    dve.drain()
                    dve.tensor_copy(score_bf[:, :, :], gate["score"][:, :, :])
                    dve.drain()
                    dve.tensor_copy(score_pieces[:, :, E * p:E * p + E], score_bf[:, :, :])
                    dve.tensor_tensor(gate["score"][:, :, :], gate["score"][:, :, :], score_bf[:, :, :], ALU.subtract)
                dve.drain().then_inc(S["score_up"], 1)

            def hand_over(i):
                if started(i):
                    dve.wait_ge(result_ps, i * HALVES)
                dve.wait_ge(S["st_up"], i + 1)
                dve.tensor_copy(score_now[:, :], score_t[:, :]).then_inc(S["score_handed"], 1)
                dve.tensor_copy(tile_in[:, :, :], tiles_of(i)).then_inc(S["tile_handed"], 1)

            def experts(i, stages):
                for slot in range(SLOTS):
                    n = slot // 3
                    k, unit = divmod(n, UNITS)
                    if slot % 3 == 1:
                        dve.wait_ge(silu_up, i * STEPS + n + 1)
                        dve.wait_ge(u_ps, i * STEPS + n + 1)
                        if unit < PAIRS:
                            dve.tensor_tensor(act_up[:, n % 2, :], act_up[:, n % 2, :], ps_u[:, :], ALU.mult).then_inc(u_read, 1)
                            dve.drain()
                        else:
                            dve.scalar_tensor_tensor(mixed[:, n % 2, :], act_up[:, n % 2, :], 0.5, ps_u[:, :], ALU.mult, ALU.mult).then_inc(u_read, 1)
                            dve.drain().then_inc(mixed_up, 1)
                    if slot % 3 == 2 and unit < PAIRS:
                        dve.wait_ge(b_ps, i * (HALVES * PAIRS) + k * PAIRS + unit + 1)
                        dve.tensor_tensor(mixed[:, n % 2, :], act_up[:, n % 2, :], ps_b[:, :], ALU.mult).then_inc(mixed_up, 1)
                    for stage in stages:
                        due(stage, slot)
                for stage in stages:
                    due(stage, LATE)
                if stages:
                    hand_over(i + 1)

            dve.memset(chosen_before[:, :, :], 0.0)
            dve.memset(score_pieces[:, :, :], 0.0)
            dve.wait_ge(params_in, 16 * len(params))
            dve.tensor_copy(pairsel[:, :], pairsel_in[:, :])
            dve.sem_inc(u_read, 1)
            dve.drain()
            pipeline(dve, attention, choice, experts, hand_over)

        @block.scalar
        def _(act):
            def attention(i):
                yield TURN + 1
                act.wait_ge(S["lnt_ps"], i + 1)
                act.activation(xt[:, :], pa[:, :], ACT.Copy).then_inc(S["xt_up"], 1)
                yield TURN + 3
                act.wait_ge(S["q_ps"], i + 1)
                act.activation(qt[:, :], pb[:, :], ACT.Identity, bias=bq[:, :]).then_inc(S["q_up"], 1)
                for t in range(NT + 1):
                    yield FIRST + PER_TILE * t
                    if t:
                        act.wait_ge(S["turned_ps"], i * NT + t)
                        act.activation(probs_t[:, (t - 1) % 2, 4:8, :].rearrange("p m n -> p (m n)"), pb[:, 512:1024], ACT.Copy).then_inc(S["turned_a"], 1)
                    if t < NT:
                        act.wait_ge(S["max_up"], i * NT + t + 1)
                        act.activation(probs[:, t % 2, :], pa[:, :], ACT.Exp, bias=negmax[:, t:t + 1], accum_out=sums[:, t:t + 1]).then_inc(S["exp_up"], 1)

            def choice(i, beside_attention):
                yield 1
                act.wait_ge(S["lnt2_ps"], i + 1)
                act.activation(xt2[:, :], pa[:, :], ACT.Copy).then_inc(S["xt2_up"], 1)
                yield 5
                act.wait_ge(S["shift_up"], i + 1)
                act.activation(gate["probs"][:, :, :], gate["probs"][:, :, :], ACT.Exp).then_inc(S["gexp_up"], 1)
                yield AFTER_TILES(COUNT + 1)
                act.wait_ge(S["st_ps"], i + 1)
                act.activation(score_t[:, :], pb[0:PIECES * E, :], ACT.Copy).then_inc(S["st_up"], 1)

            def hand_over(i):
                if started(i):
                    act.wait_ge(u_ps, i * STEPS)
                act.activation(xt_now[:, :], xt2[:, :], ACT.Copy).then_inc(S["xt_handed"], 1)

            def store_half(i, k):
                act.wait_ge(result_ps, i * HALVES + k + 1)
                act.wait_ge(stored[k], i * 16 + 16)
                act.activation(result[:, k, :], ps_o[:, :], ACT.Copy).then_inc(result_up, 1)

            def experts(i, stages):
                for slot in range(SLOTS):
                    n = slot // 3
                    if slot % 3 == 0:
                        act.wait_ge(g_ps, i * STEPS + n + 1)
                        if n >= 2:
                            act.wait_ge(mixed_up, i * STEPS + n - 1)
                        act.activation(act_up[:, n % 2, :], ps_g[:, :], ACT.Silu).then_inc(silu_up, 1)
                        if n == UNITS + 1:
                            store_half(i, 0)
                    for stage in stages:
                        due(stage, slot)
                for stage in stages:
                    due(stage, LATE)
                if stages:
                    hand_over(i + 1)
                store_half(i, 1)

            act.sem_inc(result_up, 1)
            for k in range(HALVES):
                act.sem_inc(stored[k], 16)
            act.wait_ge(params_in, 16 * len(params))
            pipeline(act, attention, choice, experts, hand_over)

        @block.tensor
        def _(pe):
            ident = const["ident"]

            def attention(i):
                yield TURN
                if started(i):
                    pe.wait_ge(S["xt2_up"], i)
                pe.wait_ge(S["ln_up"], i + 1)
                turn_tiles(pe, pa, xln, ident).then_inc(S["lnt_ps"], 1)
                yield TURN + 2
                if started(i):
                    pe.wait_ge(S["shift_up"], i)
                pe.wait_ge(S["xt_up"], i + 1)
                for k in range(HALVES):
                    last = pe.matmul(pb[:, 512 * k:512 * k + 512], wq[:, :], xt[:, 512 * k:512 * k + 512], start=True, stop=True)
                last.then_inc(S["q_ps"], 1)
                for t in range(NT + 1):
                    yield FIRST + PER_TILE * t
                    if t:
                        if t > 1:
                            pe.wait_ge(S["added"], i * NT + t - 1)
                        if started(i):
                            if t == COUNT + 1:
                                pe.wait_ge(S["count_read"], i)
                            if t == COUNT + 2:
                                pe.wait_ge(S["st_up"], i)
                        pe.wait_ge(S["exp_up"], i * NT + t)
                        for m in range(NT):
                            last = pe.transpose(pb[:, 128 * m:128 * m + 128], probs[:, (t - 1) % 2, 128 * m:128 * m + 128], ident)
                        last.then_inc(S["turned_ps"], 1)
                    else:
                        pe.wait_ge(S["q_up"], i + 1)
                    if t < NT:
                        for k in range(HALVES):
                            last = pe.matmul(pa[:, 512 * k:512 * k + 512], qt[:, 128 * t:128 * t + 128], qt[:, 512 * k:512 * k + 512], start=True, stop=True)
                        last.then_inc(S["s_ps"], 1)
                    yield FIRST + PER_TILE * t + 1
                    if t:
                        pe.wait_ge(S["turned_v"], i * NT + t)
                        pe.wait_ge(S["turned_a"], i * NT + t)
                        for m in range(NT):
                            last = pe.matmul(pb[:, 0:C], probs_t[:, (t - 1) % 2, m, :], xln[:, m, :], start=(m == 0), stop=(m == NT - 1))
                        last.then_inc(S["out_ps"], 1)

            def choice(i, beside_attention):
                yield 0
                pe.wait_ge(S["ln2_up"], i + 1)
                turn_tiles(pe, pa, xln2, ident).then_inc(S["lnt2_ps"], 1)
                yield 3
                pe.wait_ge(S["xt2_up"], i + 1)
                for t in range(NT):
                    last = pe.matmul(pb[:, E * t:E * t + E], xt2[:, 128 * t:128 * t + 128], wr[:, :], start=True, stop=True)
                last.then_inc(S["router_ps"], 1)
                yield AFTER_TILES(COUNT)
                pe.wait_ge(S["chosen_up"], i + 1)
                if beside_attention:
                    pe.wait_ge(S["added"], i * NT + NT + COUNT)
                pe.matmul(pb[:, 0:NT * E], before[:, :], gate["chosen"][:, :, :].rearrange("p t e -> p (t e)"), start=True, stop=False)
                pe.matmul(pb[:, 0:NT * E], ones[:, :], chosen_before[:, 0:NT, :].rearrange("p t e -> p (t e)"), start=False, stop=True).then_inc(S["count_ps"], 1)
                yield AFTER_TILES(COUNT + 1)
                pe.wait_ge(S["score_up"], i + 1)
                if beside_attention:
                    pe.wait_ge(S["added"], i * NT + NT + COUNT + 1)
                for t in range(NT):
                    last = pe.transpose(pb[:, 128 * t:128 * t + 128], score_pieces[:, t, :], ident)
                last.then_inc(S["st_ps"], 1)

            def down(i, n):
                k, unit = divmod(n, UNITS)
                if unit == 0:
                    pe.wait_ge(result_up, i * HALVES + k + 1)
                    if k == 0:
                        pe.wait_ge(S["tile_handed"], i + 1)
                    for t in range(4):
                        pe.matmul(ps_o[:, 128 * t:128 * t + 128], tile_in[:, 4 * k + t, :], ident,
                                  start=(t == 0), stop=False, skip_group_check=True)
                pe.wait_ge(mixed_up, i * STEPS + n + 1)
                last = pe.matmul(ps_o[:, :], wd[:, unit, :], mixed[:, n % 2, :], start=False, stop=(unit == UNITS - 1), skip_group_check=True)
                if unit == UNITS - 1:
                    last.then_inc(result_ps, 1)

            def experts(i, stages):
                pe.wait_ge(S["xt_handed"], i + 1)
                for slot in range(SLOTS):
                    n, part = divmod(slot, 3)
                    k, unit = divmod(n, UNITS)
                    cols = slice(512 * k, 512 * k + 512)
                    if part == 0:
                        if n:
                            pe.wait_ge(silu_up, i * STEPS + n)
                        pe.matmul(ps_g[:, :], wg[:, unit, :], xt_now[:, cols], start=True, stop=True).then_inc(g_ps, 1)
                    if part == 1:
                        pe.wait_ge(u_read, i * STEPS + n + 1)
                        pe.matmul(ps_u[:, :], wu[:, unit, :], xt_now[:, cols], start=True, stop=True).then_inc(u_ps, 1)
                    if part == 2:
                        if n:
                            down(i, n - 1)
                        else:
                            pe.wait_ge(S["score_handed"], i + 1)
                        if unit < PAIRS:
                            pe.matmul(ps_b[:, :], pairsel[:, 128 * unit:128 * unit + 128], score_now[:, cols], start=True, stop=True).then_inc(b_ps, 1)
                    for stage in stages:
                        due(stage, slot)
                down(i, STEPS - 1)
                for stage in stages:
                    due(stage, LATE)

            pe.wait_ge(params_in, 16 * len(params))
            pipeline(pe, attention, choice, experts)


def program(nc, B, io, out):
    ctx = ExitStack()
    with ctx:
        def keep(name, shape, dt=F32):
            return ctx.enter_context(nc.sbuf_tensor(name, shape, dt))

        cap = {k[6:]: v for k, v in io.items() if k.startswith("const_")}
        const, const_in = {}, []
        for name in ("ident", "block16", "block4", "sumsel"):
            tile = keep("c_" + name, [128, 128])
            const[name] = tile[:, :]
            const_in.append((tile[:, :], cap[name]))
        gn2 = keep("gn2", [128, 2, B])
        x1_dram = nc.dram_tensor("x1_scratch", (B, C, N), F32).ap()
        split_dram = nc.dram_tensor("split_scratch", (2, HEADS, 6, D, N), BF16).ap()
        band_dram = nc.dram_tensor("band_scratch", (BANDS, C, HW * BAND), F32).ap()
        tok_dram = nc.dram_tensor("tok_scratch", (B, 128, N), F32).ap()
        maps_stack, u_stack = ExitStack(), ExitStack()
        setup_phase(nc, ctx, io, const, const_in, band_dram)
        u_cols = u_stack.enter_context(nc.sbuf_tensor("u_cols", [128, B, 32, HW], F32))
        attention_phase(nc, ctx, B, io, const, u_cols, gn2, x1_dram, split_dram)
        maps = maps_stack.enter_context(nc.sbuf_tensor("maps", [128, B, 32, HW], F32, side="right"))
        conv_phase(nc, ctx, B, io, u_cols, maps, band_dram)
        u_stack.close()
        landmark_and_gelu_phase(nc, ctx, B, io, const, maps, gn2, x1_dram, tok_dram)
        maps_stack.close()
        dense_attention_and_silu_phase(nc, ctx, B, io, const, tok_dram, out)


_SHAPED = {
    "L0_qkvT": ("L0_conv_qkv_w", lambda a: a.T), "L0_projT": ("L0_conv_proj_w", lambda a: a.T),
    "L1_w3T": ("L1_conv_w3", lambda a: a[:, :, 0, 0].T),
    "L2_qkvT": ("L2_attn_Wqkv", lambda a: a.T), "L2_projT": ("L2_attn_Wproj", lambda a: a.T),
    "L2_ffn_Wg": ("L2_ffn_Wg", lambda a: a), "L2_ffn_W1": ("L2_ffn_W1", lambda a: a),
    "L2_ffn_W2": ("L2_ffn_W2", lambda a: a), "L2_ffn_b1": ("L2_ffn_b1", lambda a: a), "L2_ffn_b2": ("L2_ffn_b2", lambda a: a),
    "L3_attn_W": ("L3_attn_W", lambda a: a), "L3_routerT": ("L3_ffn_router_w", lambda a: a.T),
    "L3_sgT": ("L3_ffn_shared_w_gate", lambda a: a.reshape(-1, C).T), "L3_suT": ("L3_ffn_shared_w_up", lambda a: a.reshape(-1, C).T),
    "L3_sdT": ("L3_ffn_shared_w_down", lambda a: a.transpose(0, 2, 1).reshape(-1, C)),
    "L3_gT": ("L3_ffn_w_gate", lambda a: a.reshape(-1, C).T), "L3_uT": ("L3_ffn_w_up", lambda a: a.reshape(-1, C).T),
    "L3_dT": ("L3_ffn_w_down", lambda a: a.transpose(0, 2, 1).reshape(-1, C)),
}
_TAPS = ["L1_conv_w0"] + ["L1_conv_" + w for v, h, _ in KERNELS for w in (v, h)]
_COLUMNS = ["L0_conv_norm_w", "L0_conv_norm_b", "L0_conv_qkv_b", "L0_conv_proj_b", "L1_conv_b0", "L1_conv_b0_1", "L1_conv_b0_2",
            "L1_conv_b1_1", "L1_conv_b1_2", "L1_conv_b2_1", "L1_conv_b2_2", "L1_conv_b3", "L2_attn_bqkv", "L2_attn_bproj",
            "L3_attn_b", "L3_ffn_bias"]


def kernel(**inputs):
    import concourse.bacc as _bacc
    from concourse.bass_utils import run_bass_kernel_spmd as _run

    a = {k: np.asarray(v) for k, v in inputs.items()}
    B = a["x"].shape[0]
    host = {"x": a["x"].reshape(B, C, N)}
    host.update({k: f(a[n]) for k, (n, f) in _SHAPED.items()})
    host.update({n: a[n].reshape(C, -1)[:, ::-1] if n != "L1_conv_w0" else a[n].reshape(C, 5, 5)[:, :, ::-1].reshape(C, 25) for n in _TAPS})
    host.update({n: a[n].reshape(-1, 1) for n in _COLUMNS})
    host.update({"const_" + k: v for k, v in shape_constants().items()})
    nc = _bacc.Bacc("TRN2", target_bir_lowering=False, num_devices=1)
    arrays, io = {}, {}
    for k, v in host.items():
        v = np.ascontiguousarray(v)
        arrays[f"in_{k}_dram"] = v
        io[k] = nc.dram_tensor(f"in_{k}_dram", v.shape, mybir.dt.from_np(v.dtype), kind="ExternalInput").ap()
    out = nc.dram_tensor("out_0_dram", (B, C, N), F32, kind="ExternalOutput").ap()
    program(nc, B, io, out)
    r = _run(nc, [arrays], core_ids=[0])
    return r.results[0]["out_0_dram"].reshape(B, C, HW, HW)
```
